# Optimizing a Trainium2 kernel written in Bass

```python
import numpy as np
import jax
import jax.numpy as jnp

def _softmax(x, axis=-1):
    return jax.nn.softmax(x, axis=axis)

def _gelu(x):
    return jax.nn.gelu(x, approximate=True)

def _silu(x):
    return jax.nn.silu(x)

def _sigmoid(x):
    return jax.nn.sigmoid(x)

def _layernorm(x, axis=-1, eps=1e-05):
    m = jnp.mean(x, axis=axis, keepdims=True)
    v = jnp.var(x, axis=axis, keepdims=True)
    return (x - m) / jnp.sqrt(v + eps)

def _scatter_add(tgt, idx, src, axis=0):
    return tgt.at[idx].add(src)

def _segment_sum(src, seg, n):
    return jax.ops.segment_sum(src, seg, n)
kernel_name = 'mk_recurrent_d4_jaxref_r8_84461a'

def setup_inputs(seed: int=0):
    np.random.seed(seed)
    _w = jnp.asarray

    def _L0_attn_setup():
        import jax, jax.numpy as jnp
        import numpy as np
        B, S, D, H = (2, 256, 128, 16)
        HD = D // H

        def _rope_cos_sin(seq_len, head_dim, base=10000.0):
            i = jnp.arange(head_dim // 2, dtype=jnp.float32)
            theta = base ** (-2.0 * i / head_dim)
            m = jnp.arange(seq_len, dtype=jnp.float32)
            ang = jnp.outer(m, theta)
            return (jnp.cos(ang), jnp.sin(ang))

        def _apply_rope(x, cos, sin):
            xr = x[..., 0::2]
            xi = x[..., 1::2]
            c = cos[None, :, None, :]
            s = sin[None, :, None, :]
            out_r = xr * c - xi * s
            out_i = xr * s + xi * c
            return jnp.stack([out_r, out_i], axis=-1).reshape(x.shape)
        key = jax.random.key(seed)
        ks = jax.random.split(key, 7)
        sc = 1.0 / np.sqrt(D)
        return {'x': jax.random.normal(ks[0], (B, S, D), dtype=jnp.float32), 'wq_w': jax.random.normal(ks[1], (D, D), dtype=jnp.float32) * sc, 'wq_b': jax.random.normal(ks[2], (D,), dtype=jnp.float32) * 0.01, 'wk_w': jax.random.normal(ks[3], (D, D), dtype=jnp.float32) * sc, 'wk_b': jax.random.normal(ks[4], (D,), dtype=jnp.float32) * 0.01, 'wv_w': jax.random.normal(ks[5], (D, D), dtype=jnp.float32) * sc, 'wv_b': jax.random.normal(ks[6], (D,), dtype=jnp.float32) * 0.01}
    _L0_attn_in = _L0_attn_setup()

    def _L0_ffn_setup():
        import jax, jax.numpy as jnp
        import numpy as np
        D_IN, D_HID = (128, 512)

        def _ternary(key, shape):
            return jax.random.randint(key, shape, -1, 2).astype(jnp.float32)

        def _tlin(x, w, s):
            return jnp.einsum('bsi,oi->bso', x, w) * s
        key = jax.random.key(seed)
        ks = jax.random.split(key, 12)
        inv = lambda fan: 1.0 / np.sqrt(fan).astype(np.float32)
        return {'x': jax.random.normal(ks[0], (4, 256, D_IN), dtype=jnp.float32), 'w1_w': _ternary(ks[1], (D_HID, D_IN)), 'w1_s': jax.random.uniform(ks[2], (D_HID,), dtype=jnp.float32) * inv(D_IN), 'w2_w': _ternary(ks[3], (D_HID, D_IN)), 'w2_s': jax.random.uniform(ks[4], (D_HID,), dtype=jnp.float32) * inv(D_IN), 'h1_w': _ternary(ks[5], (D_HID, D_HID)), 'h1_s': jax.random.uniform(ks[6], (D_HID,), dtype=jnp.float32) * inv(D_HID), 'h2_w': _ternary(ks[7], (D_HID, D_HID)), 'h2_s': jax.random.uniform(ks[8], (D_HID,), dtype=jnp.float32) * inv(D_HID), 'w3_w': _ternary(ks[9], (D_IN, D_HID)), 'w3_s': jax.random.uniform(ks[10], (D_IN,), dtype=jnp.float32) * inv(D_HID)}
    _L0_ffn_in = _L0_ffn_setup()

    def _L1_attn_setup():
        import jax, jax.numpy as jnp
        import numpy as np
        B, S, D, H = (2, 256, 128, 16)
        DH = D // H
        key = jax.random.key(seed)
        ks = jax.random.split(key, 5)
        scale = 1.0 / np.sqrt(D)
        return {'in_features': jax.random.normal(ks[0], (B, S, D), jnp.float32), 'Wq': jax.random.normal(ks[1], (D, D), jnp.float32) * scale, 'Wk': jax.random.normal(ks[2], (D, D), jnp.float32) * scale, 'Wv': jax.random.normal(ks[3], (D, D), jnp.float32) * scale, 'Wo': jax.random.normal(ks[4], (D, D), jnp.float32) * scale}
    _L1_attn_in = _L1_attn_setup()

    def _L1_ffn_setup():
        import jax, jax.numpy as jnp
        import numpy as np
        BLOCK = 16
        _GRID = jnp.array([0.0, 0.5, 1.0, 1.5, 2.0, 3.0, 4.0, 6.0], dtype=jnp.float32)
        _MID = jnp.array([0.25, 0.75, 1.25, 1.75, 2.5, 3.5, 5.0], dtype=jnp.float32)

        def fp4_quant_dequant(x):
            shape = x.shape
            xb = x.reshape(shape[:-1] + (shape[-1] // BLOCK, BLOCK))
            scale = jnp.max(jnp.abs(xb), axis=-1, keepdims=True) / 6.0
            scale = jnp.maximum(scale, jnp.float32(1e-12))
            xn = xb / scale
            idx = jnp.searchsorted(_MID, jnp.abs(xn))
            q = _GRID[idx] * jnp.sign(xn) * scale
            return q.reshape(shape)

        def fp4_linear(x, w):
            xq = fp4_quant_dequant(x)
            wq = fp4_quant_dequant(w)
            return jnp.einsum('bsk,nk->bsn', xq, wq)
        key = jax.random.key(seed)
        k1, k2, k3, k4 = jax.random.split(key, 4)
        H, I = (128, 352)
        x = jax.random.normal(k1, (4, 512, H), dtype=jnp.float32)
        w_gate = jax.random.normal(k2, (I, H), dtype=jnp.float32) * 0.02
        w_up = jax.random.normal(k3, (I, H), dtype=jnp.float32) * 0.02
        w_down = jax.random.normal(k4, (H, I), dtype=jnp.float32) * 0.02
        return {'x': x, 'w_gate': w_gate, 'w_up': w_up, 'w_down': w_down}
    _L1_ffn_in = _L1_ffn_setup()

    def _L2_attn_setup():
        import jax, jax.numpy as jnp
        import numpy as np
        N_HEADS = 16
        EPS = 1e-06
        key = jax.random.key(seed)
        ks = jax.random.split(key, 10)
        B, T, D = (2, 256, 128)
        x = jax.random.normal(ks[0], (B, T, D), dtype=jnp.float32)
        norm_w = jnp.ones((D,), dtype=jnp.float32)
        bound = float(np.sqrt(6.0 / (D + D)))

        def lin(k):
            return jax.random.uniform(k, (D, D), dtype=jnp.float32, minval=-bound, maxval=bound)
        Wq, Wk, Wv, Wo = (lin(ks[1]), lin(ks[2]), lin(ks[3]), lin(ks[4]))
        bq = jnp.zeros((D,), dtype=jnp.float32)
        bk = jnp.zeros((D,), dtype=jnp.float32)
        bv = jnp.zeros((D,), dtype=jnp.float32)
        bo = jnp.zeros((D,), dtype=jnp.float32)
        return {'x': x, 'norm_w': norm_w, 'Wq': Wq, 'bq': bq, 'Wk': Wk, 'bk': bk, 'Wv': Wv, 'bv': bv, 'Wo': Wo, 'bo': bo}
    _L2_attn_in = _L2_attn_setup()

    def _L2_ffn_setup():
        import jax, jax.numpy as jnp
        import numpy as np
        DIM = 128
        DEPTH = 2
        HEADS = 8
        DIM_HEAD = 64
        WINDOW = 64
        INNER = HEADS * DIM_HEAD
        HID = int(DIM * 4 * 2 / 3)
        B, N = (2, 1024)
        QK_SCALE = 8.0

        def shift_token(t):
            t1, t2 = jnp.split(t, 2, axis=-1)
            t2 = jnp.pad(t2, ((0, 0), (1, 0), (0, 0)))[:, :-1]
            return jnp.concatenate([t1, t2], axis=-1)

        def l2norm(t):
            return t / jnp.clip(jnp.linalg.norm(t, axis=-1, keepdims=True), 1e-12)

        def rotate_half(x):
            x1, x2 = jnp.split(x, 2, axis=-1)
            return jnp.concatenate([-x2, x1], axis=-1)

        def rotary_xpos(q, k):
            n = q.shape[-2]
            half_idx = jnp.arange(0, DIM_HEAD, 2, dtype=jnp.float32)
            inv_freq = 1.0 / 10000.0 ** (half_idx / DIM_HEAD)
            t = jnp.arange(n, dtype=jnp.float32)
            freqs = t[:, None] * inv_freq[None, :]
            freqs = jnp.concatenate([freqs, freqs], axis=-1)
            base = (half_idx + 0.4 * DIM_HEAD) / (1.4 * DIM_HEAD)
            power = (t - n // 2) / float(WINDOW // 2)
            scale = base[None, :] ** power[:, None]
            scale = jnp.concatenate([scale, scale], axis=-1)
            cos, sin = (jnp.cos(freqs), jnp.sin(freqs))
            q = q * cos * scale + rotate_half(q) * sin * scale
            k = k * cos / scale + rotate_half(k) * sin / scale
            return (q, k)

        def local_attention(q, k, v):
            b, h, n, d = q.shape
            w = n // WINDOW
            bq = q.reshape(b, h, w, WINDOW, d) * QK_SCALE
            bk = k.reshape(b, h, w, WINDOW, d)
            bv = v.reshape(b, h, w, WINDOW, d)

            def look_around(t):
                p = jnp.pad(t, ((0, 0), (0, 0), (1, 0), (0, 0), (0, 0)))
                return jnp.concatenate([p[:, :, :w], p[:, :, 1:]], axis=3)
            bk, bv = (look_around(bk), look_around(bv))
            bt = jnp.arange(n).reshape(w, WINDOW)
            btp = jnp.pad(bt, ((1, 0), (0, 0)), constant_values=-1)
            btk = jnp.concatenate([btp[:w], btp[1:]], axis=1)
            sim = jnp.einsum('bhwid,bhwjd->bhwij', bq, bk)
            i = bt[:, :, None]
            j = btk[:, None, :]
            mask = (i < j) | (i > j + WINDOW) | (j == -1)
            sim = jnp.where(mask, -jnp.finfo(sim.dtype).max, sim)
            attn = jax.nn.softmax(sim, axis=-1)
            out = jnp.einsum('bhwij,bhwjd->bhwid', attn, bv)
            return out.reshape(b, h, n, d)

        def _layer(x, wqkv, qs, ksc, wo, lg, lb, w1, b1, w2, b2):
            b, n, _ = x.shape
            h = shift_token(x)
            qkv = h @ wqkv
            q, k, v = jnp.split(qkv, 3, axis=-1)
            to_heads = lambda t: t.reshape(b, n, HEADS, DIM_HEAD).transpose(0, 2, 1, 3)
            q, k, v = (to_heads(q), to_heads(k), to_heads(v))
            q = l2norm(q) * qs
            k = l2norm(k) * ksc
            q, k = rotary_xpos(q, k)
            o = local_attention(q, k, v)
            o = o.transpose(0, 2, 1, 3).reshape(b, n, INNER)
            x = x + o @ wo
            h = shift_token(x)
            mu = h.mean(-1, keepdims=True)
            var = h.var(-1, keepdims=True)
            h = (h - mu) / jnp.sqrt(var + 1e-05) * lg + lb
            h = h @ w1 + b1
            a, g = jnp.split(h, 2, axis=-1)
            h = a * jax.nn.gelu(g, approximate=False)
            x = x + h @ w2 + b2
            return x
        key = jax.random.key(seed)
        ks = jax.random.split(key, 6)
        return {'x': jax.random.normal(ks[0], (B, N, DIM), jnp.float32), 'wqkv': jax.random.normal(ks[1], (DEPTH, DIM, 3 * INNER), jnp.float32) * 0.02, 'q_scale': jnp.ones((DEPTH, DIM_HEAD), jnp.float32), 'k_scale': jnp.ones((DEPTH, DIM_HEAD), jnp.float32), 'wo': jax.random.normal(ks[2], (DEPTH, INNER, DIM), jnp.float32) * 0.02, 'ln_g': jnp.ones((DEPTH, DIM), jnp.float32), 'ln_b': jnp.zeros((DEPTH, DIM), jnp.float32), 'w1': jax.random.normal(ks[3], (DEPTH, DIM, 2 * HID), jnp.float32) * 0.02, 'b1': jnp.zeros((DEPTH, 2 * HID), jnp.float32), 'w2': jax.random.normal(ks[4], (DEPTH, HID, DIM), jnp.float32) * 0.02, 'b2': jnp.zeros((DEPTH, DIM), jnp.float32)}
    _L2_ffn_in = _L2_ffn_setup()

    def _L3_attn_setup():
        import jax, jax.numpy as jnp
        import numpy as np
        H = 128
        D = 32
        CHUNK = 64
        LR = 0.1
        GRAD_SCALE = 0.1
        MAX_GRAD_NORM = 1.0
        EPS = 1e-06
        P = 2 * D * D

        def _xavier(k, shape, gain=0.1):
            fan_out, fan_in = shape
            a = gain * np.sqrt(6.0 / (fan_in + fan_out))
            return jax.random.uniform(k, shape, jnp.float32, -a, a)

        def _causal_dwconv(x, w, b):
            T = x.shape[1]
            xp = jnp.pad(x, ((0, 0), (3, 0), (0, 0)))
            y = b
            for j in range(4):
                y = y + xp[:, j:j + T, :] * w[:, j]
            return y

        def _mem_loss(p, k_t, v_t):
            W1 = p[:D * D].reshape(D, D)
            W2 = p[D * D:].reshape(D, D)
            pred = jax.nn.silu(k_t @ W1.T) @ W2.T
            return jnp.sum((pred - v_t) ** 2)
        _grad_fn = jax.vmap(jax.vmap(jax.grad(_mem_loss), in_axes=(None, 0, 0)), in_axes=(0, 0, 0))

        def _forward(hidden, Wk, Wv, Wq, Wo, ckw, ckb, cvw, cvb, cqw, cqb, mW1, mW2, aW, ab, eW, eb, tW, tb, norm_g, gW, gb):
            B, S, _ = hidden.shape
            k = _causal_dwconv(hidden @ Wk.T, ckw, ckb)
            v = _causal_dwconv(hidden @ Wv.T, cvw, cvb)
            q = _causal_dwconv(hidden @ Wq.T, cqw, cqb)
            alpha = (jax.nn.sigmoid(hidden @ aW.T + ab) * 0.1).mean(-1)
            eta = (jax.nn.sigmoid(hidden @ eW.T + eb) * 0.9 + 0.05).mean(-1)
            theta = (jax.nn.softplus(hidden @ tW.T + tb) * LR).mean(-1)
            W_state = jnp.tile(jnp.concatenate([mW1.ravel(), mW2.ravel()])[None], (B, 1))
            S_state = jnp.zeros_like(W_state)

            def step(carry, xs):
                Sm, Wm = carry
                gt, et, tt, at = xs
                Sm = et[:, None] * Sm - tt[:, None] * gt
                Wm = (1.0 - at[:, None]) * Wm + Sm
                return ((Sm, Wm), Wm)
            outs = []
            for c0 in range(0, S, CHUNK):
                sl = slice(c0, c0 + CHUNK)
                g = _grad_fn(W_state, k[:, sl], v[:, sl]) * GRAD_SCALE
                gn = jnp.maximum(jnp.linalg.norm(g, axis=-1, keepdims=True), EPS)
                g = g * jnp.minimum(MAX_GRAD_NORM / gn, 1.0)
                g = jax.lax.stop_gradient(g)
                xs = (jnp.swapaxes(g, 0, 1), eta[:, sl].T, theta[:, sl].T, alpha[:, sl].T)
                (S_state, W_state), Wtraj = jax.lax.scan(step, (S_state, W_state), xs)
                Wtraj = jnp.swapaxes(Wtraj, 0, 1)
                T = Wtraj.shape[1]
                W1t = Wtraj[..., :D * D].reshape(B, T, D, D)
                W2t = Wtraj[..., D * D:].reshape(B, T, D, D)
                h = jax.nn.silu(jnp.einsum('btd,btod->bto', q[:, sl], W1t))
                outs.append(jnp.einsum('bto,btpo->btp', h, W2t))
            retrieved = jnp.concatenate(outs, axis=1)
            out = retrieved @ Wo.T
            out = out * jax.lax.rsqrt(jnp.mean(out * out, -1, keepdims=True) + EPS) * norm_g
            gate = hidden @ gW.T + gb
            return out * gate
        key = jax.random.key(seed)
        ks = jax.random.split(key, 24)
        B, S = (1, 128)
        return {'hidden': jax.random.normal(ks[0], (B, S, H), jnp.float32), 'Wk': _xavier(ks[1], (D, H)), 'Wv': _xavier(ks[2], (D, H)), 'Wq': _xavier(ks[3], (D, H)), 'Wo': _xavier(ks[4], (H, D)), 'ckw': jax.random.normal(ks[5], (D, 4), jnp.float32) * 0.05, 'ckb': jnp.zeros((D,), jnp.float32), 'cvw': jax.random.normal(ks[6], (D, 4), jnp.float32) * 0.05, 'cvb': jnp.zeros((D,), jnp.float32), 'cqw': jax.random.normal(ks[7], (D, 4), jnp.float32) * 0.05, 'cqb': jnp.zeros((D,), jnp.float32), 'mW1': _xavier(ks[8], (D, D)), 'mW2': _xavier(ks[9], (D, D)), 'aW': jax.random.normal(ks[10], (D, H), jnp.float32) * 0.02, 'ab': jnp.zeros((D,), jnp.float32), 'eW': jax.random.normal(ks[11], (D, H), jnp.float32) * 0.02, 'eb': jnp.zeros((D,), jnp.float32), 'tW': jax.random.normal(ks[12], (D, H), jnp.float32) * 0.02, 'tb': jnp.zeros((D,), jnp.float32), 'norm_g': jnp.ones((H,), jnp.float32), 'gW': jnp.zeros((H, H), jnp.float32), 'gb': jnp.ones((H,), jnp.float32)}
    _L3_attn_in = _L3_attn_setup()

    def _L3_ffn_setup():
        import jax, jax.numpy as jnp
        import numpy as np
        TOP_K = 2
        key = jax.random.key(seed)
        k1, k2, k3, k4 = jax.random.split(key, 4)
        B, T, D, H, E = (2, 256, 128, 256, 8)
        x = jax.random.normal(k1, (B, T, D), dtype=jnp.float32)
        w12 = jax.random.normal(k2, (E, 2 * H, D), dtype=jnp.float32) * D ** (-0.5)
        w3 = jax.random.normal(k3, (E, D, H), dtype=jnp.float32) * H ** (-0.5)
        gate_w = jax.random.normal(k4, (E, D), dtype=jnp.float32) * D ** (-0.5)
        return {'x': x, 'w12': w12, 'w3': w3, 'gate_w': gate_w}
    _L3_ffn_in = _L3_ffn_setup()
    _d = {'L0_attn_x': _L0_attn_in['x'], 'L0_attn_wq_w': _L0_attn_in['wq_w'], 'L0_attn_wq_b': _L0_attn_in['wq_b'], 'L0_attn_wk_w': _L0_attn_in['wk_w'], 'L0_attn_wk_b': _L0_attn_in['wk_b'], 'L0_attn_wv_w': _L0_attn_in['wv_w'], 'L0_attn_wv_b': _L0_attn_in['wv_b'], 'L0_ffn_w1_w': _L0_ffn_in['w1_w'], 'L0_ffn_w1_s': _L0_ffn_in['w1_s'], 'L0_ffn_w2_w': _L0_ffn_in['w2_w'], 'L0_ffn_w2_s': _L0_ffn_in['w2_s'], 'L0_ffn_h1_w': _L0_ffn_in['h1_w'], 'L0_ffn_h1_s': _L0_ffn_in['h1_s'], 'L0_ffn_h2_w': _L0_ffn_in['h2_w'], 'L0_ffn_h2_s': _L0_ffn_in['h2_s'], 'L0_ffn_w3_w': _L0_ffn_in['w3_w'], 'L0_ffn_w3_s': _L0_ffn_in['w3_s'], 'L1_attn_Wq': _L1_attn_in['Wq'], 'L1_attn_Wk': _L1_attn_in['Wk'], 'L1_attn_Wv': _L1_attn_in['Wv'], 'L1_attn_Wo': _L1_attn_in['Wo'], 'L1_ffn_w_gate': _L1_ffn_in['w_gate'], 'L1_ffn_w_up': _L1_ffn_in['w_up'], 'L1_ffn_w_down': _L1_ffn_in['w_down'], 'L2_attn_norm_w': _L2_attn_in['norm_w'], 'L2_attn_Wq': _L2_attn_in['Wq'], 'L2_attn_bq': _L2_attn_in['bq'], 'L2_attn_Wk': _L2_attn_in['Wk'], 'L2_attn_bk': _L2_attn_in['bk'], 'L2_attn_Wv': _L2_attn_in['Wv'], 'L2_attn_bv': _L2_attn_in['bv'], 'L2_attn_Wo': _L2_attn_in['Wo'], 'L2_attn_bo': _L2_attn_in['bo'], 'L2_ffn_wqkv': _L2_ffn_in['wqkv'], 'L2_ffn_q_scale': _L2_ffn_in['q_scale'], 'L2_ffn_k_scale': _L2_ffn_in['k_scale'], 'L2_ffn_wo': _L2_ffn_in['wo'], 'L2_ffn_ln_g': _L2_ffn_in['ln_g'], 'L2_ffn_ln_b': _L2_ffn_in['ln_b'], 'L2_ffn_w1': _L2_ffn_in['w1'], 'L2_ffn_b1': _L2_ffn_in['b1'], 'L2_ffn_w2': _L2_ffn_in['w2'], 'L2_ffn_b2': _L2_ffn_in['b2'], 'L3_attn_Wk': _L3_attn_in['Wk'], 'L3_attn_Wv': _L3_attn_in['Wv'], 'L3_attn_Wq': _L3_attn_in['Wq'], 'L3_attn_Wo': _L3_attn_in['Wo'], 'L3_attn_ckw': _L3_attn_in['ckw'], 'L3_attn_ckb': _L3_attn_in['ckb'], 'L3_attn_cvw': _L3_attn_in['cvw'], 'L3_attn_cvb': _L3_attn_in['cvb'], 'L3_attn_cqw': _L3_attn_in['cqw'], 'L3_attn_cqb': _L3_attn_in['cqb'], 'L3_attn_mW1': _L3_attn_in['mW1'], 'L3_attn_mW2': _L3_attn_in['mW2'], 'L3_attn_aW': _L3_attn_in['aW'], 'L3_attn_ab': _L3_attn_in['ab'], 'L3_attn_eW': _L3_attn_in['eW'], 'L3_attn_eb': _L3_attn_in['eb'], 'L3_attn_tW': _L3_attn_in['tW'], 'L3_attn_tb': _L3_attn_in['tb'], 'L3_attn_norm_g': _L3_attn_in['norm_g'], 'L3_attn_gW': _L3_attn_in['gW'], 'L3_attn_gb': _L3_attn_in['gb'], 'L3_ffn_w12': _L3_ffn_in['w12'], 'L3_ffn_w3': _L3_ffn_in['w3'], 'L3_ffn_gate_w': _L3_ffn_in['gate_w']}
    _x0 = _d['L0_attn_x']
    _d['L0_attn_x'] = jax.random.normal(jax.random.fold_in(jax.random.key(seed), 1), (8, 512, 128), dtype=_x0.dtype)
    del _x0
    return _d

def reference(L0_attn_x, L0_attn_wq_w, L0_attn_wq_b, L0_attn_wk_w, L0_attn_wk_b, L0_attn_wv_w, L0_attn_wv_b, L0_ffn_w1_w, L0_ffn_w1_s, L0_ffn_w2_w, L0_ffn_w2_s, L0_ffn_h1_w, L0_ffn_h1_s, L0_ffn_h2_w, L0_ffn_h2_s, L0_ffn_w3_w, L0_ffn_w3_s, L1_attn_Wq, L1_attn_Wk, L1_attn_Wv, L1_attn_Wo, L1_ffn_w_gate, L1_ffn_w_up, L1_ffn_w_down, L2_attn_norm_w, L2_attn_Wq, L2_attn_bq, L2_attn_Wk, L2_attn_bk, L2_attn_Wv, L2_attn_bv, L2_attn_Wo, L2_attn_bo, L2_ffn_wqkv, L2_ffn_q_scale, L2_ffn_k_scale, L2_ffn_wo, L2_ffn_ln_g, L2_ffn_ln_b, L2_ffn_w1, L2_ffn_b1, L2_ffn_w2, L2_ffn_b2, L3_attn_Wk, L3_attn_Wv, L3_attn_Wq, L3_attn_Wo, L3_attn_ckw, L3_attn_ckb, L3_attn_cvw, L3_attn_cvb, L3_attn_cqw, L3_attn_cqb, L3_attn_mW1, L3_attn_mW2, L3_attn_aW, L3_attn_ab, L3_attn_eW, L3_attn_eb, L3_attn_tW, L3_attn_tb, L3_attn_norm_g, L3_attn_gW, L3_attn_gb, L3_ffn_w12, L3_ffn_w3, L3_ffn_gate_w):

    def _L0_attn_ref(x, wq_w, wq_b, wk_w, wk_b, wv_w, wv_b):
        import jax, jax.numpy as jnp
        import numpy as np
        B, S, D, H = (2, 256, 128, 16)
        HD = D // H

        def _rope_cos_sin(seq_len, head_dim, base=10000.0):
            i = jnp.arange(head_dim // 2, dtype=jnp.float32)
            theta = base ** (-2.0 * i / head_dim)
            m = jnp.arange(seq_len, dtype=jnp.float32)
            ang = jnp.outer(m, theta)
            return (jnp.cos(ang), jnp.sin(ang))

        def _apply_rope(x, cos, sin):
            xr = x[..., 0::2]
            xi = x[..., 1::2]
            c = cos[None, :, None, :]
            s = sin[None, :, None, :]
            out_r = xr * c - xi * s
            out_i = xr * s + xi * c
            return jnp.stack([out_r, out_i], axis=-1).reshape(x.shape)
        bs, seq_len, dim = x.shape
        xq = (x @ wq_w.T + wq_b).reshape(bs, seq_len, H, HD)
        xk = (x @ wk_w.T + wk_b).reshape(bs, seq_len, H, HD)
        xv = (x @ wv_w.T + wv_b).reshape(bs, seq_len, H, HD)
        cos, sin = _rope_cos_sin(seq_len, HD)
        xq = _apply_rope(xq, cos, sin)
        xk = _apply_rope(xk, cos, sin)
        q = xq.transpose(0, 2, 1, 3)
        k = xk.transpose(0, 2, 1, 3)
        v = xv.transpose(0, 2, 1, 3)
        scores = jnp.einsum('bhqd,bhkd->bhqk', q, k) / np.sqrt(HD)
        attn = jax.nn.softmax(scores.astype(jnp.float32), axis=-1)
        out = jnp.einsum('bhqk,bhkd->bhqd', attn, v)
        return out.transpose(0, 2, 1, 3).reshape(bs, seq_len, dim)

    def _L0_ffn_ref(x, w1_w, w1_s, w2_w, w2_s, h1_w, h1_s, h2_w, h2_s, w3_w, w3_s):
        import jax, jax.numpy as jnp
        import numpy as np
        D_IN, D_HID = (128, 512)

        def _ternary(key, shape):
            return jax.random.randint(key, shape, -1, 2).astype(jnp.float32)

        def _tlin(x, w, s):
            return jnp.einsum('bsi,oi->bso', x, w) * s
        h = jax.nn.silu(_tlin(x, w1_w, w1_s)) * _tlin(x, w2_w, w2_s)
        h = jax.nn.gelu(_tlin(h, h1_w, h1_s), approximate=False)
        h = jax.nn.gelu(_tlin(h, h2_w, h2_s), approximate=False)
        return _tlin(h, w3_w, w3_s)

    def _L1_attn_ref(in_features, Wq, Wk, Wv, Wo):
        import jax, jax.numpy as jnp
        import numpy as np
        B, S, D, H = (2, 256, 128, 16)
        DH = D // H
        seq_len = in_features.shape[-2]
        q = in_features @ Wq.T
        k = in_features @ Wk.T
        v = in_features @ Wv.T

        def split(x):
            return jnp.moveaxis(x.reshape(*x.shape[:-1], H, DH), -3, -2)
        q, k, v = (split(q), split(k), split(v))
        scores = jnp.einsum('...hqd,...hkd->...hqk', q, k) / np.sqrt(DH)
        causal = jnp.triu(jnp.ones((seq_len, seq_len), bool), k=1)
        scores = jnp.where(causal, jnp.float32(-1000000000.0), scores)
        weights = jax.nn.softmax(scores, axis=-1)
        out = jnp.einsum('...hqk,...hkd->...hqd', weights, v)
        out = jnp.moveaxis(out, -3, -2).reshape(*in_features.shape[:-1], D)
        return out @ Wo.T

    def _L1_ffn_ref(x, w_gate, w_up, w_down):
        import jax, jax.numpy as jnp
        import numpy as np
        BLOCK = 16
        _GRID = jnp.array([0.0, 0.5, 1.0, 1.5, 2.0, 3.0, 4.0, 6.0], dtype=jnp.float32)
        _MID = jnp.array([0.25, 0.75, 1.25, 1.75, 2.5, 3.5, 5.0], dtype=jnp.float32)

        def fp4_quant_dequant(x):
            shape = x.shape
            xb = x.reshape(shape[:-1] + (shape[-1] // BLOCK, BLOCK))
            scale = jnp.max(jnp.abs(xb), axis=-1, keepdims=True) / 6.0
            scale = jnp.maximum(scale, jnp.float32(1e-12))
            xn = xb / scale
            idx = jnp.searchsorted(_MID, jnp.abs(xn))
            q = _GRID[idx] * jnp.sign(xn) * scale
            return q.reshape(shape)

        def fp4_linear(x, w):
            xq = fp4_quant_dequant(x)
            wq = fp4_quant_dequant(w)
            return jnp.einsum('bsk,nk->bsn', xq, wq)
        gate = fp4_linear(x, w_gate)
        y = fp4_linear(x, w_up)
        h = jax.nn.silu(gate) * y
        return fp4_linear(h, w_down)

    def _L2_attn_ref(x, norm_w, Wq, bq, Wk, bk, Wv, bv, Wo, bo):
        import jax, jax.numpy as jnp
        import numpy as np
        N_HEADS = 16
        EPS = 1e-06
        B, T, D = x.shape
        H = N_HEADS
        hd = D // H
        xn = x * jax.lax.rsqrt(jnp.mean(x * x, axis=-1, keepdims=True) + EPS) * norm_w
        q = (xn @ Wq.T + bq).reshape(B, T, H, hd).transpose(0, 2, 1, 3)
        k = (xn @ Wk.T + bk).reshape(B, T, H, hd).transpose(0, 2, 1, 3)
        v = (xn @ Wv.T + bv).reshape(B, T, H, hd).transpose(0, 2, 1, 3)
        scale = 1.0 / jnp.sqrt(jnp.asarray(hd, dtype=x.dtype))
        scores = jnp.einsum('bhqd,bhkd->bhqk', q, k) * scale
        causal = jnp.triu(jnp.ones((T, T), dtype=bool), k=1)
        scores = jnp.where(causal, jnp.asarray(-jnp.inf, dtype=scores.dtype), scores)
        attn = jax.nn.softmax(scores, axis=-1)
        out = jnp.einsum('bhqk,bhkd->bhqd', attn, v)
        out = out.transpose(0, 2, 1, 3).reshape(B, T, D)
        out = out @ Wo.T + bo
        return xn + out

    def _L2_ffn_ref(x, wqkv, q_scale, k_scale, wo, ln_g, ln_b, w1, b1, w2, b2):
        import jax, jax.numpy as jnp
        import numpy as np
        DIM = 128
        DEPTH = 2
        HEADS = 8
        DIM_HEAD = 64
        WINDOW = 64
        INNER = HEADS * DIM_HEAD
        HID = int(DIM * 4 * 2 / 3)
        B, N = (2, 1024)
        QK_SCALE = 8.0

        def shift_token(t):
            t1, t2 = jnp.split(t, 2, axis=-1)
            t2 = jnp.pad(t2, ((0, 0), (1, 0), (0, 0)))[:, :-1]
            return jnp.concatenate([t1, t2], axis=-1)

        def l2norm(t):
            return t / jnp.clip(jnp.linalg.norm(t, axis=-1, keepdims=True), 1e-12)

        def rotate_half(x):
            x1, x2 = jnp.split(x, 2, axis=-1)
            return jnp.concatenate([-x2, x1], axis=-1)

        def rotary_xpos(q, k):
            n = q.shape[-2]
            half_idx = jnp.arange(0, DIM_HEAD, 2, dtype=jnp.float32)
            inv_freq = 1.0 / 10000.0 ** (half_idx / DIM_HEAD)
            t = jnp.arange(n, dtype=jnp.float32)
            freqs = t[:, None] * inv_freq[None, :]
            freqs = jnp.concatenate([freqs, freqs], axis=-1)
            base = (half_idx + 0.4 * DIM_HEAD) / (1.4 * DIM_HEAD)
            power = (t - n // 2) / float(WINDOW // 2)
            scale = base[None, :] ** power[:, None]
            scale = jnp.concatenate([scale, scale], axis=-1)
            cos, sin = (jnp.cos(freqs), jnp.sin(freqs))
            q = q * cos * scale + rotate_half(q) * sin * scale
            k = k * cos / scale + rotate_half(k) * sin / scale
            return (q, k)

        def local_attention(q, k, v):
            b, h, n, d = q.shape
            w = n // WINDOW
            bq = q.reshape(b, h, w, WINDOW, d) * QK_SCALE
            bk = k.reshape(b, h, w, WINDOW, d)
            bv = v.reshape(b, h, w, WINDOW, d)

            def look_around(t):
                p = jnp.pad(t, ((0, 0), (0, 0), (1, 0), (0, 0), (0, 0)))
                return jnp.concatenate([p[:, :, :w], p[:, :, 1:]], axis=3)
            bk, bv = (look_around(bk), look_around(bv))
            bt = jnp.arange(n).reshape(w, WINDOW)
            btp = jnp.pad(bt, ((1, 0), (0, 0)), constant_values=-1)
            btk = jnp.concatenate([btp[:w], btp[1:]], axis=1)
            sim = jnp.einsum('bhwid,bhwjd->bhwij', bq, bk)
            i = bt[:, :, None]
            j = btk[:, None, :]
            mask = (i < j) | (i > j + WINDOW) | (j == -1)
            sim = jnp.where(mask, -jnp.finfo(sim.dtype).max, sim)
            attn = jax.nn.softmax(sim, axis=-1)
            out = jnp.einsum('bhwij,bhwjd->bhwid', attn, bv)
            return out.reshape(b, h, n, d)

        def _layer(x, wqkv, qs, ksc, wo, lg, lb, w1, b1, w2, b2):
            b, n, _ = x.shape
            h = shift_token(x)
            qkv = h @ wqkv
            q, k, v = jnp.split(qkv, 3, axis=-1)
            to_heads = lambda t: t.reshape(b, n, HEADS, DIM_HEAD).transpose(0, 2, 1, 3)
            q, k, v = (to_heads(q), to_heads(k), to_heads(v))
            q = l2norm(q) * qs
            k = l2norm(k) * ksc
            q, k = rotary_xpos(q, k)
            o = local_attention(q, k, v)
            o = o.transpose(0, 2, 1, 3).reshape(b, n, INNER)
            x = x + o @ wo
            h = shift_token(x)
            mu = h.mean(-1, keepdims=True)
            var = h.var(-1, keepdims=True)
            h = (h - mu) / jnp.sqrt(var + 1e-05) * lg + lb
            h = h @ w1 + b1
            a, g = jnp.split(h, 2, axis=-1)
            h = a * jax.nn.gelu(g, approximate=False)
            x = x + h @ w2 + b2
            return x
        for l in range(DEPTH):
            x = _layer(x, wqkv[l], q_scale[l], k_scale[l], wo[l], ln_g[l], ln_b[l], w1[l], b1[l], w2[l], b2[l])
        return x

    def _L3_attn_ref(hidden, Wk, Wv, Wq, Wo, ckw, ckb, cvw, cvb, cqw, cqb, mW1, mW2, aW, ab, eW, eb, tW, tb, norm_g, gW, gb):
        import jax, jax.numpy as jnp
        import numpy as np
        H = 128
        D = 32
        CHUNK = 64
        LR = 0.1
        GRAD_SCALE = 0.1
        MAX_GRAD_NORM = 1.0
        EPS = 1e-06
        P = 2 * D * D

        def _xavier(k, shape, gain=0.1):
            fan_out, fan_in = shape
            a = gain * np.sqrt(6.0 / (fan_in + fan_out))
            return jax.random.uniform(k, shape, jnp.float32, -a, a)

        def _causal_dwconv(x, w, b):
            T = x.shape[1]
            xp = jnp.pad(x, ((0, 0), (3, 0), (0, 0)))
            y = b
            for j in range(4):
                y = y + xp[:, j:j + T, :] * w[:, j]
            return y

        def _mem_loss(p, k_t, v_t):
            W1 = p[:D * D].reshape(D, D)
            W2 = p[D * D:].reshape(D, D)
            pred = jax.nn.silu(k_t @ W1.T) @ W2.T
            return jnp.sum((pred - v_t) ** 2)
        _grad_fn = jax.vmap(jax.vmap(jax.grad(_mem_loss), in_axes=(None, 0, 0)), in_axes=(0, 0, 0))

        def _forward(hidden, Wk, Wv, Wq, Wo, ckw, ckb, cvw, cvb, cqw, cqb, mW1, mW2, aW, ab, eW, eb, tW, tb, norm_g, gW, gb):
            B, S, _ = hidden.shape
            k = _causal_dwconv(hidden @ Wk.T, ckw, ckb)
            v = _causal_dwconv(hidden @ Wv.T, cvw, cvb)
            q = _causal_dwconv(hidden @ Wq.T, cqw, cqb)
            alpha = (jax.nn.sigmoid(hidden @ aW.T + ab) * 0.1).mean(-1)
            eta = (jax.nn.sigmoid(hidden @ eW.T + eb) * 0.9 + 0.05).mean(-1)
            theta = (jax.nn.softplus(hidden @ tW.T + tb) * LR).mean(-1)
            W_state = jnp.tile(jnp.concatenate([mW1.ravel(), mW2.ravel()])[None], (B, 1))
            S_state = jnp.zeros_like(W_state)

            def step(carry, xs):
                Sm, Wm = carry
                gt, et, tt, at = xs
                Sm = et[:, None] * Sm - tt[:, None] * gt
                Wm = (1.0 - at[:, None]) * Wm + Sm
                return ((Sm, Wm), Wm)
            outs = []
            for c0 in range(0, S, CHUNK):
                sl = slice(c0, c0 + CHUNK)
                g = _grad_fn(W_state, k[:, sl], v[:, sl]) * GRAD_SCALE
                gn = jnp.maximum(jnp.linalg.norm(g, axis=-1, keepdims=True), EPS)
                g = g * jnp.minimum(MAX_GRAD_NORM / gn, 1.0)
                g = jax.lax.stop_gradient(g)
                xs = (jnp.swapaxes(g, 0, 1), eta[:, sl].T, theta[:, sl].T, alpha[:, sl].T)
                (S_state, W_state), Wtraj = jax.lax.scan(step, (S_state, W_state), xs)
                Wtraj = jnp.swapaxes(Wtraj, 0, 1)
                T = Wtraj.shape[1]
                W1t = Wtraj[..., :D * D].reshape(B, T, D, D)
                W2t = Wtraj[..., D * D:].reshape(B, T, D, D)
                h = jax.nn.silu(jnp.einsum('btd,btod->bto', q[:, sl], W1t))
                outs.append(jnp.einsum('bto,btpo->btp', h, W2t))
            retrieved = jnp.concatenate(outs, axis=1)
            out = retrieved @ Wo.T
            out = out * jax.lax.rsqrt(jnp.mean(out * out, -1, keepdims=True) + EPS) * norm_g
            gate = hidden @ gW.T + gb
            return out * gate
        return _forward(hidden, Wk, Wv, Wq, Wo, ckw, ckb, cvw, cvb, cqw, cqb, mW1, mW2, aW, ab, eW, eb, tW, tb, norm_g, gW, gb)

    def _L3_ffn_ref(x, w12, w3, gate_w):
        import jax, jax.numpy as jnp
        import numpy as np
        TOP_K = 2
        E = gate_w.shape[0]
        H = w3.shape[-1]
        scores = jnp.einsum('btd,ed->bte', x, gate_w)
        topk_scores, topk_idx = jax.lax.top_k(scores, TOP_K)
        topk_probs = jax.nn.softmax(topk_scores, axis=-1)
        total_probs = jnp.sum(jax.nn.one_hot(topk_idx, E, dtype=topk_probs.dtype) * topk_probs[..., None], axis=-2)
        h12 = jnp.einsum('btd,ehd->bteh', x, w12)
        h1, h2 = (h12[..., :H], h12[..., H:])
        hidden = jax.nn.silu(h1) * h2
        expert_out = jnp.einsum('bteh,edh->bted', hidden, w3)
        y = jnp.sum(total_probs[..., None] * expert_out, axis=-2)
        return y
    x = L0_attn_x
    xn = _layernorm(x, axis=-1)
    s = _L0_attn_ref(xn, L0_attn_wq_w, L0_attn_wq_b, L0_attn_wk_w, L0_attn_wk_b, L0_attn_wv_w, L0_attn_wv_b)
    g = _silu(_L0_ffn_ref(xn, L0_ffn_w1_w, L0_ffn_w1_s, L0_ffn_w2_w, L0_ffn_w2_s, L0_ffn_h1_w, L0_ffn_h1_s, L0_ffn_h2_w, L0_ffn_h2_s, L0_ffn_w3_w, L0_ffn_w3_s))
    x = x + s * g
    xn = _layernorm(x, axis=-1)
    s = _L1_attn_ref(xn, L1_attn_Wq, L1_attn_Wk, L1_attn_Wv, L1_attn_Wo)
    g = _silu(_L1_ffn_ref(xn, L1_ffn_w_gate, L1_ffn_w_up, L1_ffn_w_down))
    x = x + s * g
    xn = _layernorm(x, axis=-1)
    s = _L2_attn_ref(xn, L2_attn_norm_w, L2_attn_Wq, L2_attn_bq, L2_attn_Wk, L2_attn_bk, L2_attn_Wv, L2_attn_bv, L2_attn_Wo, L2_attn_bo)
    g = _silu(_L2_ffn_ref(xn, L2_ffn_wqkv, L2_ffn_q_scale, L2_ffn_k_scale, L2_ffn_wo, L2_ffn_ln_g, L2_ffn_ln_b, L2_ffn_w1, L2_ffn_b1, L2_ffn_w2, L2_ffn_b2))
    x = x + s * g
    xn = _layernorm(x, axis=-1)
    s = _L3_attn_ref(xn, L3_attn_Wk, L3_attn_Wv, L3_attn_Wq, L3_attn_Wo, L3_attn_ckw, L3_attn_ckb, L3_attn_cvw, L3_attn_cvb, L3_attn_cqw, L3_attn_cqb, L3_attn_mW1, L3_attn_mW2, L3_attn_aW, L3_attn_ab, L3_attn_eW, L3_attn_eb, L3_attn_tW, L3_attn_tb, L3_attn_norm_g, L3_attn_gW, L3_attn_gb)
    g = _silu(_L3_ffn_ref(xn, L3_ffn_w12, L3_ffn_w3, L3_ffn_gate_w))
    x = x + s * g
    return x

_drawn_inputs = setup_inputs


def setup_inputs(seed=0):
    import zlib

    import numpy as np

    out = dict(_drawn_inputs(seed))
    spreads = {'L2_attn_norm_w': (1.0, 0.2),
     'L2_attn_bq': (0.0, 0.1),
     'L2_attn_bk': (0.0, 0.1),
     'L2_attn_bv': (0.0, 0.1),
     'L2_attn_bo': (0.0, 0.1),
     'L2_ffn_q_scale': (1.0, 0.2),
     'L2_ffn_k_scale': (1.0, 0.2),
     'L2_ffn_ln_g': (1.0, 0.2),
     'L2_ffn_ln_b': (0.0, 0.1),
     'L2_ffn_b1': (0.0, 0.1),
     'L2_ffn_b2': (0.0, 0.1),
     'L3_attn_ckb': (0.0, 0.1),
     'L3_attn_cvb': (0.0, 0.1),
     'L3_attn_cqb': (0.0, 0.1),
     'L3_attn_ab': (0.0, 0.1),
     'L3_attn_eb': (0.0, 0.1),
     'L3_attn_tb': (0.0, 0.1),
     'L3_attn_norm_g': (1.0, 0.2),
     'L3_attn_gW': (0.0, 0.1),
     'L3_attn_gb': (1.0, 0.2)}
    factors = {}
    for name, (base, spread) in spreads.items():
        noise = np.random.default_rng([zlib.crc32(name.encode()), seed]).standard_normal(out[name].shape)
        drawn = base * np.exp(spread * noise) if base else spread * noise
        out[name] = jnp.asarray(drawn.astype(out[name].dtype))
    for name, factor in factors.items():
        out[name] = (out[name] * factor).astype(out[name].dtype)
    return out
```

```python
from contextlib import ExitStack

import numpy as np

import concourse.bass as bass
from concourse import mybir

F32 = mybir.dt.float32
BF16 = mybir.dt.bfloat16
U32 = mybir.dt.uint32
ALU = mybir.AluOpType
ACT = mybir.ActivationFunctionType
AX = mybir.AxisListType

P = 128
BATCH, T, D = 8, 512, 128
NT = T // P
H, HD = 16, 8
NG = H // 4
EPS_LN = 1e-5
NEG = -1.0e30
HID0 = 512
I1, BLK = 352, 16
INNER, LH, LD, WIN, HID2 = 512, 8, 64, 64, 341
DM, CH = 32, 64
E3, H3 = 8, 256
NCH = T // CH


class Chain:

    def __init__(self, eng, sem):
        self.eng, self.sem, self.n = eng, sem, 0

    def tick(self, ins):
        self.n += 1
        ins.then_inc(self.sem, 1)

    def wait(self):
        if self.n:
            self.eng.wait_ge(self.sem, self.n)

    def do(self, ins):
        self.tick(ins)
        self.wait()


class Kit:

    def __init__(self, nc, ctx):
        self.nc = nc
        self.pool = [ctx.enter_context(nc.semaphore(f"sig{i}")) for i in range(24)]
        first = self.pool[0].num
        assert [s.num for s in self.pool] == list(range(first, first + len(self.pool)))

    def clear(self):
        first = self.pool[0].num
        self.nc.vector.sem_clear(range(first, first + len(self.pool)))
        self.nc.all_engine_barrier()


NAMED = {}


def sbuf(nc, ctx, name, shape, dt=F32):
    NAMED[name] = NAMED.get(name, 0) + 1
    if NAMED[name] > 1:
        name = f"{name}_{NAMED[name]}"
    return ctx.enter_context(nc.sbuf_tensor(name, shape, dt))




def load_constants(nc, K, loads):
    landed = K.pool[0]
    with nc.Block() as block:
        @block.sync
        def _(sp):
            for dst, src in loads[0::2]:
                sp.dma_start(dst, src).then_inc(landed, 16)
            sp.wait_ge(landed, 16 * len(loads))

        @block.scalar
        def _(act):
            for dst, src in loads[1::2]:
                act.dma_start(dst, src).then_inc(landed, 16)
    K.clear()


def clear_buffers(nc, K, fills):
    with nc.Block() as block:
        @block.vector
        def _(dve):
            for dst, value in fills:
                nc.vector.memset(dst, value)
    K.clear()


def fp4_blocks(nc, ch, V, Q, a, acc, sc, rs, npart, n):
    nb = n // BLK
    v = V.rearrange("p (b k) -> p b k", k=BLK)
    q = Q.rearrange("p (b k) -> p b k", k=BLK)
    A = a[0:npart, 0:n]
    C = acc[0:npart, 0:n]
    s, r = sc[0:npart, 0:nb], rs[0:npart, 0:nb]
    ch.do(nc.vector.tensor_reduce(s, v, AX.X, ALU.max, apply_absolute_value=True))
    ch.do(nc.vector.tensor_scalar(s, s, 1.0 / 6.0, 1e-12, ALU.mult, ALU.max))
    ch.do(nc.vector.reciprocal(r, s))
    ch.do(nc.vector.tensor_tensor(A.rearrange("p (b k) -> p b k", k=BLK), v,
                                  r.unsqueeze(2).to_broadcast([npart, nb, BLK]), ALU.mult))
    ch.do(nc.vector.scalar_tensor_tensor(A, A, -1.0, A, ALU.mult, ALU.max))
    ch.do(nc.vector.tensor_scalar(C, A, 5.0, 2.0, ALU.is_gt, ALU.mult))
    ch.do(nc.vector.scalar_tensor_tensor(C, A, 3.5, C, ALU.is_gt, ALU.add))
    ch.do(nc.vector.scalar_tensor_tensor(C, A, 2.5, C, ALU.is_gt, ALU.add))
    ch.do(nc.vector.tensor_scalar(C, C, 2.0, None, ALU.mult))
    for mid in (1.75, 1.25, 0.75, 0.25):
        ch.do(nc.vector.scalar_tensor_tensor(C, A, mid, C, ALU.is_gt, ALU.add))
    ch.do(nc.vector.tensor_scalar(A, V, 0.0, 2.0, ALU.is_ge, ALU.mult))
    ch.do(nc.vector.scalar_tensor_tensor(A, A, 1.0, C, ALU.subtract, ALU.mult))
    ch.do(nc.vector.tensor_scalar(s, s, 0.5, None, ALU.mult))
    ch.do(nc.vector.tensor_tensor(q, A.rearrange("p (b k) -> p b k", k=BLK),
                                  s.unsqueeze(2).to_broadcast([npart, nb, BLK]), ALU.mult))


def quantize_weights(nc, K, ctx):
    with ExitStack() as tmp:
        q = sbuf(nc, tmp, "wq4", [P, 7, I1])
        scr = fp4_scratch(nc, tmp, I1)
        vec, quantized, turned, copied = K.pool[0:4]
        jobs = []
        for m, w in enumerate((K.gate_rows, K.up_rows)):
            for c in range(3):
                n = min(P, I1 - c * P)
                jobs.append((n, w[0:n, c, :], q[0:n, 3 * m + c, 0:D], D))
        jobs.append((P, K.down_rows[:, :], q[:, 6, :], I1))
        turns = []
        for m in range(2):
            for c in range(3):
                n = min(P, I1 - c * P)
                turns.append((q[0:n, 3 * m + c, 0:D], n, K.ps[:, m, c * P:c * P + n],
                              K.w_gu[:, m * I1 + c * P:m * I1 + c * P + n]))
        for c in range(3):
            n = min(P, I1 - c * P)
            turns.append((q[:, 6, c * P:c * P + n], P, K.ps[0:n, 2 + c, 0:P], K.w_down[0:n, c, :]))
        with nc.Block() as block:
            @block.vector
            def _(dve):
                ch = Chain(dve, vec)
                for npart, V, Q, n in jobs:
                    fp4_blocks(nc, ch, V, Q, *scr, npart, n)
                nc.vector.engine_nop().then_inc(quantized, 1)
                dve.wait_ge(turned, len(turns))
                for _, _, ps, dst in turns:
                    nc.vector.tensor_copy(dst, ps).then_inc(copied, 1)

            @block.tensor
            def _(pe):
                pe.wait_ge(quantized, 1)
                for src, n, ps, _ in turns:
                    nc.tensor.transpose(ps, src, K.ident[0:n, 0:n]).then_inc(turned, 1)
        K.clear()


def fp4_scratch(nc, ctx, n):
    return (sbuf(nc, ctx, "fp4_abs", [P, n]), sbuf(nc, ctx, "fp4_steps", [P, n], BF16),
            sbuf(nc, ctx, "fp4_scale", [P, n // BLK]), sbuf(nc, ctx, "fp4_rscale", [P, n // BLK]))




def layer_norm(nc, K, load=None):
    loaded, vec, var_ready, rstd_ready, xn_ready, turned, evac = K.pool[0:7]
    with nc.Block() as block:
        if load is not None:
            @block.sync
            def _(sp):
                sp.dma_start(K.x[:, :, :], load).then_inc(loaded, 16)

        @block.vector
        def _(dve):
            ch = Chain(dve, vec)
            if load is not None:
                dve.wait_ge(loaded, 16)
            for t in range(NT):
                ch.tick(nc.vector.bn_stats(K.stats[:, t, :], K.x[:, t, :]))
            ch.wait()
            for t in range(NT):
                ch.tick(nc.vector.bn_aggr(K.mv[:, t, :], K.stats[:, t, :]))
            ch.wait()
            nc.vector.tensor_scalar(K.var[:, 0:NT], K.mv[:, :, 1], EPS_LN, None,
                                    ALU.add).then_inc(var_ready, 1)
            dve.wait_ge(rstd_ready, 1)
            for t in range(NT):
                nc.vector.tensor_scalar(K.xn[:, t, :], K.x[:, t, :], K.mv[:, t, 0:1], K.rstd[:, t:t + 1],
                                        ALU.subtract, ALU.mult).then_inc(xn_ready, 1)

        @block.gpsimd
        def _(pool):
            pool.wait_ge(var_ready, 1)
            nc.gpsimd.tensor_tensor(K.rstd[:, 0:NT], K.var[:, 0:NT], K.neghalf[:, 0:NT],
                                    ALU.pow).then_inc(rstd_ready, 1)

        @block.tensor
        def _(pe):
            for t in range(NT):
                pe.wait_ge(xn_ready, t + 1)
                nc.tensor.transpose(K.ps[:, 0, t * P:(t + 1) * P], K.xn[:, t, :], K.ident[:, :]).then_inc(turned, 1)

        @block.scalar
        def _(act):
            act.wait_ge(turned, NT)
            nc.scalar.activation(K.xnT[:, :], K.ps[:, 0, :], ACT.Identity).then_inc(evac, 1)
    K.clear()


def rms_norm(nc, K):
    vec, var_ready, rstd_ready, xr_ready, turned, evac = K.pool[0:6]
    with nc.Block() as block:
        @block.vector
        def _(dve):
            ch = Chain(dve, vec)
            for t in range(NT):
                ch.tick(nc.vector.bn_stats(K.stats[:, t, :], K.xn[:, t, :]))
            ch.wait()
            for t in range(NT):
                ch.tick(nc.vector.bn_aggr(K.mv[:, t, :], K.stats[:, t, :]))
            ch.wait()
            ch.do(nc.vector.tensor_tensor(K.var[:, 0:NT], K.mv[:, :, 0], K.mv[:, :, 0], ALU.mult))
            nc.vector.scalar_tensor_tensor(K.var[:, 0:NT], K.mv[:, :, 1], 1e-6, K.var[:, 0:NT],
                                           ALU.add, ALU.add).then_inc(var_ready, 1)
            dve.wait_ge(rstd_ready, 1)
            for t in range(NT):
                nc.vector.scalar_tensor_tensor(K.xr[:, t, :], K.xn[:, t, :], K.rstd[:, t:t + 1], K.rmsw[:, :],
                                               ALU.mult, ALU.mult).then_inc(xr_ready, 1)

        @block.gpsimd
        def _(pool):
            pool.wait_ge(var_ready, 1)
            nc.gpsimd.tensor_tensor(K.rstd[:, 0:NT], K.var[:, 0:NT], K.neghalf[:, 0:NT],
                                    ALU.pow).then_inc(rstd_ready, 1)

        @block.tensor
        def _(pe):
            for t in range(NT):
                pe.wait_ge(xr_ready, t + 1)
                nc.tensor.transpose(K.ps[:, 0, t * P:(t + 1) * P], K.xr[:, t, :], K.ident[:, :]).then_inc(turned, 1)

        @block.scalar
        def _(act):
            act.wait_ge(turned, NT)
            nc.scalar.activation(K.xrT[:, :], K.ps[:, 0, :], ACT.Identity).then_inc(evac, 1)
    K.clear()




def project_rope(nc, K):
    projected, vec, rotated, v_free, turned = K.pool[0:5]
    with ExitStack() as tmp:
        qk = sbuf(nc, tmp, "qk", [P, NT, 2 * D])
        part = sbuf(nc, tmp, "qk_sin", [P, NT, 2 * D])
        with nc.Block() as block:
            @block.tensor
            def _(pe):
                for t in range(NT):
                    nc.tensor.matmul(K.ps[:, t, 0:3 * D], K.xnT[:, t * P:(t + 1) * P], K.w0_qkv[:, :],
                                     start=True, stop=True).then_inc(projected, 1)
                for m in range(2):
                    for t in range(NT):
                        pe.wait_ge(rotated, 1)
                        nc.tensor.transpose(K.ps[:, 4 + m, t * P:(t + 1) * P], qk[:, t, m * D:(m + 1) * D],
                                            K.ident[:, :]).then_inc(turned, 1)

            @block.vector
            def _(dve):
                ch = Chain(dve, vec)
                dve.wait_ge(projected, NT)
                for t in range(NT):
                    ch.tick(nc.vector.tensor_tensor(qk[:, t, :], K.ps[:, t, 0:2 * D], K.b0_qkv[:, 0:2 * D], ALU.add))
                    nc.vector.tensor_tensor(K.v32[:, t, :, 0:HD],
                                            K.ps[:, t, 2 * D:3 * D].rearrange("p (h d) -> p h d", d=HD),
                                            K.b0_qkv[:, 2 * D:3 * D].rearrange("p (h d) -> p h d", d=HD),
                                            ALU.add).then_inc(v_free, 1)
                ch.wait()
                for t in range(NT):
                    x4 = qk[:, t, :].rearrange("p (g i two) -> p g i two", two=2, i=HD // 2)
                    y4 = part[:, t, :].rearrange("p (g i two) -> p g i two", two=2, i=HD // 2)
                    for e in range(2):
                        sin = K.rope_sin[:, t, e, :].unsqueeze(1).to_broadcast([P, 2 * H, HD // 2])
                        ch.tick(nc.vector.tensor_tensor(y4[:, :, :, e], x4[:, :, :, 1 - e], sin, ALU.mult))
                ch.wait()
                for t in range(NT):
                    x3 = qk[:, t, :].rearrange("p (g d) -> p g d", d=HD)
                    cos = K.rope_cos[:, t, :].unsqueeze(1).to_broadcast([P, 2 * H, HD])
                    ch.tick(nc.vector.tensor_tensor(x3, x3, cos, ALU.mult))
                ch.wait()
                nc.vector.tensor_tensor(qk[:, :, :], qk[:, :, :], part[:, :, :], ALU.add).then_inc(rotated, 1)
        K.clear()


def project_plain(nc, K, srcT, wq, wk, wv, bv):
    projected, v_free = K.pool[0:2]
    with nc.Block() as block:
        @block.tensor
        def _(pe):
            nc.tensor.matmul(K.ps[:, 4, :], wq[:, :], srcT[:, :], start=True, stop=True)
            nc.tensor.matmul(K.ps[:, 5, :], wk[:, :], srcT[:, :], start=True, stop=True)
            for t in range(NT):
                mm = nc.tensor.matmul(K.ps[:, 0, t * P:(t + 1) * P], srcT[:, t * P:(t + 1) * P], wv[:, :],
                                      start=True, stop=True)
            mm.then_inc(projected, 1)

        @block.vector
        def _(dve):
            dve.wait_ge(projected, 1)
            for t in range(NT):
                v = K.ps[:, 0, t * P:(t + 1) * P].rearrange("p (h d) -> p h d", d=HD)
                if bv is None:
                    nc.vector.tensor_copy(K.v32[:, t, :, 0:HD], v).then_inc(v_free, 1)
                else:
                    nc.vector.tensor_tensor(K.v32[:, t, :, 0:HD], v,
                                            bv[:, :].rearrange("p (h d) -> p h d", d=HD),
                                            ALU.add).then_inc(v_free, 1)
    K.clear()


def spread_parts(nc, K, bq, bk):
    vec, first, left, parts_ready, spread, saved_q, saved_k = K.pool[0:7]
    with ExitStack() as tmp:
        parts = sbuf(nc, tmp, "parts", [P, 2, 3, T], BF16)
        rest = sbuf(nc, tmp, "rest", [P, 2, T])
        with nc.Block() as block:
            @block.scalar
            def _(act):
                for m, b in enumerate((bq, bk)):
                    nc.scalar.activation(parts[:, m, 0, :], K.ps[:, 4 + m, :], ACT.Identity,
                                         bias=0.0 if b is None else b).then_inc(first, 1)
                for m in range(2):
                    act.wait_ge(left, m + 1)
                    nc.scalar.activation(parts[:, m, 1, :], rest[:, m, :], ACT.Identity).then_inc(first, 1)
                act.wait_ge(parts_ready, 2)
                act.dma_start(K.parts_d[1].rearrange("i (h d) t -> (h d) i t", d=HD), parts[:, 1, :, :]).then_inc(saved_k, 16)
                act.wait_ge(saved_k, 16)
                for j in range(3):
                    for i in range(3):
                        r = 24 * i + 8 * j
                        act.dma_start(K.ks[r:r + HD, :, :], K.parts_d[1, j].rearrange(
                            "(h d) t -> d h t", d=HD)).then_inc(spread, 16)
                act.wait_ge(spread, 18 * 16)

            @block.vector
            def _(dve):
                for m, b in enumerate((bq, bk)):
                    dve.wait_ge(first, m + 1)
                    nc.vector.scalar_tensor_tensor(rest[:, m, :], K.ps[:, 4 + m, :], 0.0 if b is None else b,
                                                   parts[:, m, 0, :], ALU.add, ALU.subtract).then_inc(left, 1)
                for m in range(2):
                    dve.wait_ge(first, 3 + m)
                    nc.vector.tensor_tensor(parts[:, m, 2, :], rest[:, m, :], parts[:, m, 1, :],
                                            ALU.subtract).then_inc(parts_ready, 1)

            @block.sync
            def _(sp):
                sp.wait_ge(parts_ready, 1)
                sp.dma_start(K.parts_d[0].rearrange("i (h d) t -> (h d) i t", d=HD), parts[:, 0, :, :]).then_inc(saved_q, 16)
                sp.wait_ge(saved_q, 16)
                for i in range(3):
                    for j in range(3):
                        r = 24 * i + 8 * j
                        sp.dma_start(K.qs[r:r + HD, :, :], K.parts_d[0, i].rearrange(
                            "(h d) t -> d h t", d=HD)).then_inc(spread, 16)
        K.clear()


def row_maxima(nc, K, causal):
    scored, reduced, turned, hi_ready, lo_ready, saved, rows = K.pool[0:7]
    with ExitStack() as tmp:
        nmax = sbuf(nc, tmp, "nmax", [P, NT, H])
        parts = sbuf(nc, tmp, "max_parts", [H, 2, T], BF16)
        with nc.Block() as block:
            @block.tensor
            def _(pe):
                for h in range(H):
                    for u in range(2):
                        n = 2 * h + u
                        if n >= 2:
                            pe.wait_ge(reduced, n - 1)
                        for t in (2 * u, 2 * u + 1):
                            b = 2 * (n % 2) + t % 2
                            keys = (t + 1) * P if causal else T
                            mm = nc.tensor.matmul(K.ps[:, b, 0:keys], K.qs[:, h, t * P:(t + 1) * P],
                                                  K.ks[:, h, 0:keys], start=True, stop=not causal)
                            if causal:
                                mm = nc.tensor.matmul(K.ps[:, b, keys - P:keys], K.identb[:, :], K.mask_q[:, :],
                                                      start=False, stop=True)
                        mm.then_inc(scored, 1)
                pe.wait_ge(reduced, 2 * H)
                for t in range(NT):
                    nc.tensor.transpose(K.ps[0:H, 4, t * P:(t + 1) * P], nmax[:, t, :],
                                        K.ident[:, :]).then_inc(turned, 1)

            @block.vector
            def _(dve):
                for h in range(H):
                    for u in range(2):
                        n = 2 * h + u
                        dve.wait_ge(scored, n + 1)
                        b = 2 * (n % 2)
                        if causal:
                            for t in (2 * u, 2 * u + 1):
                                r = nc.vector.tensor_reduce(nmax[:, t, h:h + 1], K.ps[:, b + t % 2, 0:(t + 1) * P],
                                                            AX.X, ALU.max, negate=True)
                            r.then_inc(reduced, 1)
                        else:
                            nc.vector.tensor_reduce(nmax[:, 2 * u:2 * u + 2, h], K.ps[:, b:b + 2, :],
                                                    AX.X, ALU.max, negate=True).then_inc(reduced, 1)
                dve.wait_ge(hi_ready, 1)
                nc.vector.tensor_tensor(parts[:, 1, :], K.ps[0:H, 4, :], parts[:, 0, :],
                                        ALU.subtract).then_inc(lo_ready, 1)

            @block.scalar
            def _(act):
                act.wait_ge(turned, NT)
                nc.scalar.activation(parts[:, 0, :], K.ps[0:H, 4, :], ACT.Identity).then_inc(hi_ready, 1)

            @block.sync
            def _(sp):
                sp.wait_ge(hi_ready, 1)
                sp.wait_ge(lo_ready, 1)
                sp.dma_start(K.nmax_d[:, :, :].rearrange("i h t -> h i t"), parts[:, :, :]).then_inc(saved, 16)
                sp.wait_ge(saved, 16)
                sp.dma_start(K.qs[96:98, :, :], K.nmax_d[:, :, :]).then_inc(rows, 16)
                sp.wait_ge(rows, 16)
        K.clear()


def attend(nc, K, causal):
    scored, exped, summed, oT_ready, turned, vec, att_ready = K.pool[0:7]
    SLOTS = 6
    scale = float(1.0 / np.sqrt(HD))
    with ExitStack() as tmp:
        probs = sbuf(nc, tmp, "probs", [P, SLOTS, NT, T])
        oT = sbuf(nc, tmp, "oT", [P, 2, T])
        rden = sbuf(nc, tmp, "rden", [P, NT, 4])
        with nc.Block() as block:
            @block.tensor
            def _(pe):
                def scores(h, u):
                    n = 2 * h + u
                    if n >= 2:
                        pe.wait_ge(exped, n - 1)
                    for k in (2 * u, 2 * u + 1):
                        b = 2 * (n % 2) + k % 2
                        q0 = k * P if causal else 0
                        mm = nc.tensor.matmul(K.ps[:, b, q0:T], K.ks[:, h, k * P:(k + 1) * P],
                                              K.qs[:, h, q0:T], start=True, stop=not causal)
                        if causal:
                            mm = nc.tensor.matmul(K.ps[:, b, q0:q0 + P], K.identb[:, :], K.mask_k[:, :],
                                                  start=False, stop=True)
                    mm.then_inc(scored, 1)

                def weigh(g):
                    pe.wait_ge(exped, 8 * (g + 1))
                    if g >= 2:
                        pe.wait_ge(oT_ready, g - 1)
                    for k in range(NT):
                        q0 = k * P if causal else 0
                        for j in range(4):
                            h = 4 * g + j
                            mm = nc.tensor.matmul(K.ps[32 * j:32 * j + 32, 4 + g % 2, q0:T], K.v32[:, k, h, :],
                                                  probs[:, h % SLOTS, k, q0:T], start=(k == 0), stop=(k == NT - 1),
                                                  tile_position=(0, 32 * j))
                    mm.then_inc(summed, 1)

                def turn(g):
                    pe.wait_ge(oT_ready, g + 1)
                    if g >= 2:
                        pe.wait_ge(att_ready, g - 1)
                    for t in range(NT):
                        mm = nc.tensor.transpose(K.ps[:, 6 + g % 2, t * P:(t + 1) * P],
                                                 oT[:, g % 2, t * P:(t + 1) * P], K.ident[:, :])
                    mm.then_inc(turned, 1)

                for h in range(H):
                    scores(h, 0)
                    scores(h, 1)
                    if h % 4 == 0 and h:
                        weigh(h // 4 - 1)
                    if h % 4 == 1 and h > 1:
                        turn(h // 4 - 1)
                weigh(NG - 1)
                turn(NG - 1)

            @block.scalar
            def _(act):
                def copy_sums(g):
                    act.wait_ge(summed, g + 1)
                    if g >= 2:
                        act.wait_ge(turned, g - 1)
                    nc.scalar.activation(oT[:, g % 2, :], K.ps[:, 4 + g % 2, :], ACT.Identity).then_inc(oT_ready, 1)

                for h in range(H):
                    if h >= SLOTS:
                        act.wait_ge(summed, (h - SLOTS) // 4 + 1)
                    for u in range(2):
                        n = 2 * h + u
                        act.wait_ge(scored, n + 1)
                        b = 2 * (n % 2)
                        if causal:
                            for k in (2 * u, 2 * u + 1):
                                a = nc.scalar.activation(probs[:, h % SLOTS, k, k * P:T], K.ps[:, b + k % 2, k * P:T],
                                                         ACT.Exp, scale=scale)
                            a.then_inc(exped, 1)
                        else:
                            nc.scalar.activation(probs[:, h % SLOTS, 2 * u:2 * u + 2, :], K.ps[:, b:b + 2, :],
                                                 ACT.Exp, scale=scale).then_inc(exped, 1)
                    if h % 4 == 1 and h > 1:
                        copy_sums(h // 4 - 1)
                copy_sums(NG - 1)

            @block.vector
            def _(dve):
                ch = Chain(dve, vec)
                for g in range(NG):
                    dve.wait_ge(turned, g + 1)
                    o = K.ps[:, 6 + g % 2, :].rearrange("p (t j d) -> p t j d", t=NT, j=4)
                    ch.do(nc.vector.reciprocal(rden[:, :, :], o[:, :, :, HD]))
                    for t in range(NT):
                        mul = nc.vector.tensor_tensor(
                            K.att[:, t, g * 32:(g + 1) * 32].rearrange("p (j d) -> p j d", d=HD), o[:, t, :, 0:HD],
                            rden[:, t, :].unsqueeze(2).to_broadcast([P, 4, HD]), ALU.mult)
                        if t < NT - 1:
                            ch.tick(mul)
                        else:
                            mul.then_inc(att_ready, 1)
                    dve.wait_ge(att_ready, g + 1)
        K.clear()


def project_out(nc, K, wo, bo):
    turned, copied, projected, vec = K.pool[0:4]
    with ExitStack() as tmp:
        attT = sbuf(nc, tmp, "attT", [P, T])
        with nc.Block() as block:
            @block.tensor
            def _(pe):
                for t in range(NT):
                    mm = nc.tensor.transpose(K.ps[:, 0, t * P:(t + 1) * P], K.att[:, t, :], K.ident[:, :])
                mm.then_inc(turned, 1)
                pe.wait_ge(copied, 1)
                for t in range(NT):
                    mm = nc.tensor.matmul(K.ps[:, 1, t * P:(t + 1) * P], attT[:, t * P:(t + 1) * P], wo[:, :],
                                          start=True, stop=True)
                mm.then_inc(projected, 1)

            @block.scalar
            def _(act):
                act.wait_ge(turned, 1)
                nc.scalar.activation(attT[:, :], K.ps[:, 0, :], ACT.Identity).then_inc(copied, 1)

            @block.vector
            def _(dve):
                ch = Chain(dve, vec)
                dve.wait_ge(projected, 1)
                o = K.ps[:, 1, :].rearrange("p (t d) -> p t d", t=NT)
                if bo is None:
                    nc.vector.tensor_copy(K.att[:, :, :], o)
                else:
                    for t in range(NT):
                        ch.tick(nc.vector.tensor_tensor(K.att[:, t, :], o[:, t, :], bo[:, :], ALU.add))
                    ch.wait()
                    nc.vector.tensor_tensor(K.att[:, :, :], K.att[:, :, :], K.xr[:, :, :], ALU.add)
        K.clear()


def attention(nc, K, causal, bq=None, bk=None):
    spread_parts(nc, K, bq, bk)
    row_maxima(nc, K, causal)
    attend(nc, K, causal)




def ternary_ffn(nc, K):
    gate_up, silu_done, h_ready, hid, gelu_done, out_done, vec, g_in, g_ready = K.pool[0:9]
    with ExitStack() as tmp:
        a = sbuf(nc, tmp, "silu_a", [P, 2, T])
        h = sbuf(nc, tmp, "hid_a", [P, 4, T])
        g = sbuf(nc, tmp, "hid_b", [P, 4, T])
        out = sbuf(nc, tmp, "ffn_out", [P, NT, D])
        with nc.Block() as block:
            @block.tensor
            def _(pe):
                for c in range(4):
                    if c >= 2:
                        pe.wait_ge(h_ready, c - 1)
                    b = 2 * (c % 2)
                    nc.tensor.matmul(K.ps[:, b, :], K.w0_1[:, c * P:(c + 1) * P], K.xnT[:, :], start=True, stop=True)
                    nc.tensor.matmul(K.ps[:, b + 1, :], K.w0_2[:, c * P:(c + 1) * P], K.xnT[:, :],
                                     start=True, stop=True).then_inc(gate_up, 1)
                for layer, (w, src) in enumerate(((K.w0_h1, h), (K.w0_h2, g))):
                    if layer == 0:
                        pe.wait_ge(h_ready, 4)
                    else:
                        pe.wait_ge(gelu_done, 4)
                    for c in range(4):
                        n = 4 * layer + c
                        if n >= 2:
                            pe.wait_ge(gelu_done, n - 1)
                        for k in range(4):
                            mm = nc.tensor.matmul(K.ps[:, 4 + n % 2, :], w[:, k, c * P:(c + 1) * P], src[:, k, :],
                                                  start=(k == 0), stop=(k == 3))
                        mm.then_inc(hid, 1)
                pe.wait_ge(gelu_done, 8)
                for t in range(NT):
                    for k in range(4):
                        mm = nc.tensor.matmul(K.ps[:, 6, t * P:(t + 1) * P], h[:, k, t * P:(t + 1) * P],
                                              K.w0_3[:, k, :], start=(k == 0), stop=(k == 3))
                mm.then_inc(out_done, 1)

            @block.scalar
            def _(act):
                for c in range(4):
                    act.wait_ge(gate_up, c + 1)
                    if c >= 2:
                        act.wait_ge(h_ready, c - 1)
                    nc.scalar.activation(a[:, c % 2, :], K.ps[:, 2 * (c % 2), :], ACT.Silu,
                                         scale=K.s0_1[:, c:c + 1]).then_inc(silu_done, 1)
                for layer, (s, dst) in enumerate(((K.s0_h1, g), (K.s0_h2, h))):
                    for c in range(4):
                        n = 4 * layer + c
                        act.wait_ge(hid, n + 1)
                        if n == 4:
                            act.wait_ge(hid, 4)
                        nc.scalar.activation(dst[:, c, :], K.ps[:, 4 + n % 2, :], ACT.Gelu,
                                             scale=s[:, c:c + 1]).then_inc(gelu_done, 1)
                act.wait_ge(g_in, 1)
                nc.scalar.activation(out[:, :, :], out[:, :, :], ACT.Silu).then_inc(g_ready, 1)

            @block.vector
            def _(dve):
                ch = Chain(dve, vec)
                for c in range(4):
                    dve.wait_ge(silu_done, c + 1)
                    nc.vector.scalar_tensor_tensor(h[:, c, :], K.ps[:, 2 * (c % 2) + 1, :], K.s0_2[:, c:c + 1],
                                                   a[:, c % 2, :], ALU.mult, ALU.mult).then_inc(h_ready, 1)
                dve.wait_ge(out_done, 1)
                for t in range(NT):
                    m = nc.vector.tensor_tensor(out[:, t, :], K.ps[:, 6, t * P:(t + 1) * P], K.s0_3[:, :], ALU.mult)
                    ch.tick(m)
                ch.wait()
                nc.vector.engine_nop().then_inc(g_in, 1)
                dve.wait_ge(g_ready, 1)
                ch.do(nc.vector.tensor_tensor(out[:, :, :], out[:, :, :], K.att[:, :, :], ALU.mult))
                nc.vector.tensor_tensor(K.x[:, :, :], K.x[:, :, :], out[:, :, :], ALU.add)
        K.clear()




def fp4_ffn(nc, K):
    vec, xq_ready, turned, xqT_ready, projected, silu_done, hq_ready, hturned, hT_ready, down, g_ready = K.pool[0:11]
    with ExitStack() as tmp:
        xq = sbuf(nc, tmp, "xq", [P, NT, D])
        xqT = sbuf(nc, tmp, "xqT", [P, T])
        h = sbuf(nc, tmp, "h1", [P, NT, I1])
        hT = sbuf(nc, tmp, "h1T", [P, 3, T])
        out = sbuf(nc, tmp, "ffn_out", [P, NT, D])
        scr = fp4_scratch(nc, tmp, NT * I1)
        with nc.Block() as block:
            @block.vector
            def _(dve):
                ch = Chain(dve, vec)
                fp4_blocks(nc, ch, K.xn[:, :, :].rearrange("p t d -> p (t d)"),
                           xq[:, :, :].rearrange("p t d -> p (t d)"), *scr, P, NT * D)
                nc.vector.engine_nop().then_inc(xq_ready, 1)
                for t in range(NT):
                    dve.wait_ge(silu_done, t + 1)
                    ch.tick(nc.vector.tensor_tensor(h[:, t, :], h[:, t, :], K.ps[:, 2 + t, 0:I1], ALU.mult))
                ch.wait()
                flat = h[:, :, :].rearrange("p t i -> p (t i)")
                fp4_blocks(nc, ch, flat, flat, *scr, P, NT * I1)
                nc.vector.engine_nop().then_inc(hq_ready, 1)
                for c in range(3):
                    dve.wait_ge(hturned, c + 1)
                    n = min(P, I1 - c * P)
                    nc.vector.tensor_copy(hT[0:n, c, :], K.ps[0:n, c, :]).then_inc(hT_ready, 1)
                dve.wait_ge(g_ready, 1)
                ch.do(nc.vector.tensor_tensor(out[:, :, :], out[:, :, :], K.att[:, :, :], ALU.mult))
                nc.vector.tensor_tensor(K.x[:, :, :], K.x[:, :, :], out[:, :, :], ALU.add)

            @block.tensor
            def _(pe):
                pe.wait_ge(xq_ready, 1)
                for t in range(NT):
                    mm = nc.tensor.transpose(K.ps[:, 7, t * P:(t + 1) * P], xq[:, t, :], K.ident[:, :])
                mm.then_inc(turned, 1)
                pe.wait_ge(xqT_ready, 1)
                for t in range(NT):
                    if t >= 2:
                        pe.wait_ge(silu_done, t - 1)
                    nc.tensor.matmul(K.ps[:, t % 2, 0:I1], xqT[:, t * P:(t + 1) * P], K.w_gu[:, 0:I1],
                                     start=True, stop=True)
                    nc.tensor.matmul(K.ps[:, 2 + t, 0:I1], xqT[:, t * P:(t + 1) * P], K.w_gu[:, I1:2 * I1],
                                     start=True, stop=True).then_inc(projected, 1)
                pe.wait_ge(hq_ready, 1)
                for c in range(3):
                    n = min(P, I1 - c * P)
                    for t in range(NT):
                        mm = nc.tensor.transpose(K.ps[0:n, c, t * P:(t + 1) * P], h[:, t, c * P:c * P + n],
                                                 K.ident[:, :])
                    mm.then_inc(hturned, 1)
                pe.wait_ge(hT_ready, 3)
                for t in range(NT):
                    for c in range(3):
                        n = min(P, I1 - c * P)
                        mm = nc.tensor.matmul(K.ps[:, 6, t * P:(t + 1) * P], hT[0:n, c, t * P:(t + 1) * P],
                                              K.w_down[0:n, c, :], start=(c == 0), stop=(c == 2))
                mm.then_inc(down, 1)

            @block.scalar
            def _(act):
                act.wait_ge(turned, 1)
                nc.scalar.activation(xqT[:, :], K.ps[:, 7, :], ACT.Identity).then_inc(xqT_ready, 1)
                for t in range(NT):
                    act.wait_ge(projected, t + 1)
                    nc.scalar.activation(h[:, t, :], K.ps[:, t % 2, 0:I1], ACT.Silu).then_inc(silu_done, 1)
                act.wait_ge(down, 1)
                nc.scalar.activation(out[:, :, :], K.ps[:, 6, :].rearrange("p (t d) -> p t d", t=NT),
                                     ACT.Silu).then_inc(g_ready, 1)
        K.clear()




def shift_tokens(nc, K):
    turned, evac = K.pool[0:2]
    with nc.Block() as block:
        @block.tensor
        def _(pe):
            for t in range(NT):
                mm = nc.tensor.transpose(K.ps[:, 0, t * P:(t + 1) * P], K.y[:, t, :], K.ident[:, :])
            mm.then_inc(turned, 1)

        @block.scalar
        def _(act):
            act.wait_ge(turned, 1)
            nc.scalar.activation(K.shT[0:64, :], K.ps[0:64, 0, :], ACT.Identity).then_inc(evac, 1)

        @block.vector
        def _(dve):
            dve.wait_ge(turned, 1)
            nc.vector.tensor_copy(K.shT[64:128, 1:T], K.ps[64:128, 0, 0:T - 1])
            nc.vector.memset(K.shT[64:128, 0:1], 0.0)
    K.clear()


def local_qkv(nc, K, L):
    projected, squared, v_copied, rotated, summed, rn_ready, ssq_ready, vec = K.pool[0:8]
    w = K.w2_qkv[L]
    with ExitStack() as tmp:
        sq = sbuf(nc, tmp, "sq", [P, 2, INNER])
        rot = sbuf(nc, tmp, "rot", [P, 2, INNER])
        with nc.Block() as block:
            @block.tensor
            def _(pe):
                for t in range(NT):
                    if t >= 2:
                        pe.wait_ge(v_copied, t - 1)
                        pe.wait_ge(rotated, 2 * (t - 1))
                    for m in range(3):
                        mm = nc.tensor.matmul(K.ps[:, 4 * (t % 2) + m, :], K.shT[:, t * P:(t + 1) * P],
                                              w[:, m * INNER:(m + 1) * INNER], start=True, stop=True)
                    mm.then_inc(projected, 1)

            @block.scalar
            def _(act):
                for t in range(NT):
                    act.wait_ge(projected, t + 1)
                    b = 4 * (t % 2)
                    for m in range(2):
                        if t:
                            act.wait_ge(summed, 2 * (t - 1) + m + 1)
                        nc.scalar.activation(sq[:, m, :], K.ps[:, b + m, :], ACT.Square).then_inc(squared, 1)
                    act.wait_ge(squared, 2 * t + 2)
                    nc.scalar.activation(K.v_tm[:, t, :], K.ps[:, b + 2, :], ACT.Identity).then_inc(v_copied, 1)

            @block.vector
            def _(dve):
                ch = Chain(dve, vec)
                for t in range(NT):
                    b = 4 * (t % 2)
                    for m, (dst, cos, sin) in enumerate(((K.q_tm, K.cosq, K.sinq), (K.k_tm, K.cosk, K.sink))):
                        dve.wait_ge(squared, 2 * t + m + 1)
                        nc.vector.tensor_reduce(K.ssq[:, m, t, :], sq[:, m, :].rearrange("p (h d) -> p h d", d=LD),
                                                AX.X, ALU.add).then_inc(summed, 1)
                        src = K.ps[:, b + m, :].rearrange("p (h two d) -> p h two d", two=2, d=LD // 2)
                        rv = rot[:, m, :].rearrange("p (h two d) -> p h two d", two=2, d=LD // 2)
                        for e in range(2):
                            s = sin[L][:, t, 32 * e:32 * e + 32].unsqueeze(1).to_broadcast([P, LH, 32])
                            ch.tick(nc.vector.tensor_tensor(rv[:, :, e, :], src[:, :, 1 - e, :], s, ALU.mult))
                        c = cos[L][:, t, :].unsqueeze(1).to_broadcast([P, LH, LD])
                        ch.tick(nc.vector.tensor_tensor(dst[:, t, :].rearrange("p (h d) -> p h d", d=LD),
                                                        K.ps[:, b + m, :].rearrange("p (h d) -> p h d", d=LD), c,
                                                        ALU.mult))
                        ch.wait()
                        add = nc.vector.tensor_tensor(dst[:, t, :], dst[:, t, :], rot[:, m, :], ALU.add)
                        add.then_inc(rotated, 1)
                        dve.wait_ge(rotated, 2 * t + m + 1)
                dve.wait_ge(summed, 2 * NT)
                nc.vector.tensor_scalar(K.ssq[:, :, :, :], K.ssq[:, :, :, :], 1e-24, None, ALU.max).then_inc(ssq_ready, 1)
                dve.wait_ge(rn_ready, 1)
                ch.tick(nc.vector.tensor_scalar(K.rnq8[:, :, :], K.rn[:, 0, :, :], 8.0, None, ALU.mult))
                for t in range(NT):
                    k3 = K.k_tm[:, t, :].rearrange("p (h d) -> p h d", d=LD)
                    nc.vector.tensor_tensor(k3, k3, K.rn[:, 1, t, :].unsqueeze(2).to_broadcast([P, LH, LD]), ALU.mult)

            @block.gpsimd
            def _(pool):
                pool.wait_ge(ssq_ready, 1)
                nc.gpsimd.tensor_tensor(K.rn[:, :, :, :].rearrange("p m t h -> p (m t h)"),
                                        K.ssq[:, :, :, :].rearrange("p m t h -> p (m t h)"),
                                        K.neghalf[:, 0:2 * NT * LH], ALU.pow).then_inc(rn_ready, 1)
        K.clear()


def local_transpose(nc, K):
    turned, copied, cleared = K.pool[0:3]
    with nc.Block() as block:
        @block.tensor
        def _(pe):
            for p in range(LH // 2):
                for m, src in enumerate((K.q_tm, K.k_tm)):
                    for t in range(NT):
                        mm = nc.tensor.transpose(K.ps[:, 2 * p + m, t * P:(t + 1) * P],
                                                 src[:, t, p * P:(p + 1) * P], K.ident[:, :])
                    mm.then_inc(turned, 1)

        @block.scalar
        def _(act):
            for p in range(LH // 2):
                act.wait_ge(turned, 2 * p + 2)
                nc.scalar.activation(K.kT[:, p, :], K.ps[:, 2 * p + 1, :], ACT.Identity).then_inc(copied, 1)

        @block.vector
        def _(dve):
            for p in range(LH // 2):
                dve.wait_ge(turned, 2 * p + 1)
                for e in range(2):
                    nc.vector.tensor_copy(K.qz[64 * e:64 * e + 64, 2 * p + e, :], K.ps[64 * e:64 * e + 64, 2 * p, :])

        @block.gpsimd
        def _(pool):
            nc.gpsimd.memset(K.qz[64:128, 0:LH:2, :], 0.0).then_inc(cleared, 1)
            pool.wait_ge(cleared, 1)
            nc.gpsimd.memset(K.qz[0:64, 1:LH:2, :], 0.0)
    K.clear()


def local_attention(nc, K):
    scored, reduced, bias_ready, exped, den_ready, normed, turned, copied, summed, oT_ready, zeroed = K.pool[0:11]
    with ExitStack() as tmp:
        nm = sbuf(nc, tmp, "nm", [P, 2, NT])
        nb = sbuf(nc, tmp, "nb", [P, 2, NT])
        den = sbuf(nc, tmp, "den", [P, 2, NT])
        rden = sbuf(nc, tmp, "rden", [P, 2, NT])
        probs = sbuf(nc, tmp, "probs", [P, 2, NT, 2 * P])
        pT = sbuf(nc, tmp, "probsT", [P, 2, NT, 2 * P])
        with nc.Block() as block:
            @block.tensor
            def _(pe):
                def scores(h):
                    if h >= 2:
                        pe.wait_ge(exped, h - 1)
                    for t in range(NT):
                        b = 2 * (h % 2) + t // 2
                        c = 256 * (t % 2)
                        nc.tensor.matmul(K.ps[:, b, c + 64:c + 256], K.identb[:, :],
                                         (K.mask_band if t else K.mask_band0)[:, :], start=True, stop=False)
                        k0 = 64 if t else 128
                        mm = nc.tensor.matmul(K.ps[:, b, c + k0:c + 256], K.qz[:, h, t * P:(t + 1) * P],
                                              K.kT[:, h // 2, t * P - 128 + k0:(t + 1) * P], start=False, stop=True)
                    mm.then_inc(scored, 1)

                def turn(h):
                    pe.wait_ge(normed, h + 1)
                    for t in range(NT):
                        if t % 2 == 0 and (h or t):
                            pe.wait_ge(copied, 2 * h + t // 2 - 1 if t else 2 * h - 1)
                        for e in range(2):
                            mm = nc.tensor.transpose(K.ps[:, 4 + t // 2, (t % 2) * 256 + e * P:(t % 2) * 256 + (e + 1) * P],
                                                     probs[:, h % 2, t, e * P:(e + 1) * P], K.ident[:, :])
                        if t % 2:
                            mm.then_inc(turned, 1)

                def weigh(h):
                    pe.wait_ge(copied, 2 * h + 2)
                    if h >= 4 and h % 2 == 0:
                        pe.wait_ge(oT_ready, h // 2 - 1)
                    e = h % 2
                    for t in range(NT):
                        o = K.ps[64 * e:64 * e + 64, 6 + h // 2 % 2, t * P:(t + 1) * P]
                        if t:
                            nc.tensor.matmul(o, K.v_tm[:, t - 1, h * LD:(h + 1) * LD], pT[:, h % 2, t, 0:P],
                                             start=True, stop=False, tile_position=(0, 64 * e))
                        mm = nc.tensor.matmul(o, K.v_tm[:, t, h * LD:(h + 1) * LD], pT[:, h % 2, t, P:2 * P],
                                              start=(t == 0), stop=True, tile_position=(0, 64 * e))
                    mm.then_inc(summed, 1)

                scores(0)
                for h in range(LH):
                    if h + 1 < LH:
                        scores(h + 1)
                    turn(h)
                    weigh(h)

            @block.vector
            def _(dve):
                for h in range(LH):
                    i = h % 2
                    dve.wait_ge(scored, h + 1)
                    s = K.ps[:, 2 * i:2 * i + 2, :].rearrange("p b (t k) -> p (b t) k", k=256)
                    nc.vector.tensor_reduce(nm[:, i, :], s[:, :, 64:256], AX.X, ALU.max,
                                            negate=True).then_inc(reduced, 1)
                    dve.wait_ge(reduced, h + 1)
                    nc.vector.tensor_tensor(nb[:, i, :], nm[:, i, :], K.rnq8[:, :, h], ALU.mult).then_inc(bias_ready, 1)
                    dve.wait_ge(exped, h + 1)
                    nc.vector.reciprocal(rden[:, i, :], den[:, i, :]).then_inc(den_ready, 1)
                    dve.wait_ge(den_ready, h + 1)
                    nc.vector.tensor_tensor(probs[:, i, :, 64:256], probs[:, i, :, 64:256],
                                            rden[:, i, :].unsqueeze(2).to_broadcast([P, NT, 192]),
                                            ALU.mult).then_inc(normed, 1)
                    for u in range(2):
                        if h >= 2 and u == 0:
                            dve.wait_ge(summed, h - 1)
                        dve.wait_ge(turned, 2 * h + u + 1)
                        nc.vector.tensor_copy(pT[:, i, 2 * u:2 * u + 2, :], K.ps[:, 4 + u, :].rearrange(
                            "p (t k) -> p t k", k=256)).then_inc(copied, 1)

            @block.scalar
            def _(act):
                act.wait_ge(zeroed, 1)
                for h in range(LH):
                    i = h % 2
                    act.wait_ge(bias_ready, h + 1)
                    if h >= 2:
                        act.wait_ge(turned, 2 * (h - 1))
                        act.wait_ge(den_ready, h - 1)
                    for t in range(NT):
                        b, c = 2 * i + t // 2, 256 * (t % 2)
                        a = nc.scalar.activation(probs[:, i, t, 64:256], K.ps[:, b, c + 64:c + 256], ACT.Exp,
                                                 scale=K.rnq8[:, t, h:h + 1], bias=nb[:, i, t:t + 1],
                                                 accum_out=den[:, i, t:t + 1])
                    a.then_inc(exped, 1)
                    if h % 2:
                        act.wait_ge(summed, h + 1)
                        nc.scalar.activation(K.oT[:, h // 2, :], K.ps[:, 6 + h // 2 % 2, :],
                                             ACT.Identity).then_inc(oT_ready, 1)

            @block.gpsimd
            def _(pool):
                nc.gpsimd.memset(probs[:, :, :, 0:64], 0.0).then_inc(zeroed, 1)
        K.clear()


def local_out(nc, K, L):
    projected, = K.pool[0:1]
    with nc.Block() as block:
        @block.tensor
        def _(pe):
            for t in range(NT):
                for p in range(4):
                    mm = nc.tensor.matmul(K.ps[:, 0, t * P:(t + 1) * P], K.oT[:, p, t * P:(t + 1) * P],
                                          K.w2_o[L][:, p, :], start=(p == 0), stop=(p == 3))
            mm.then_inc(projected, 1)

        @block.vector
        def _(dve):
            dve.wait_ge(projected, 1)
            nc.vector.tensor_tensor(K.y[:, :, :], K.y[:, :, :], K.ps[:, 0, :].rearrange("p (t d) -> p t d", t=NT),
                                    ALU.add)
    K.clear()


def glu(nc, K, L):
    back, vec, var_ready, rstd_ready, hn_ready, turned, hnT_ready, up, gelu_done, hid_ready, down = K.pool[0:11]
    NC = [P, P, HID2 - 2 * P]
    with ExitStack() as tmp:
        hn = sbuf(nc, tmp, "hn", [P, NT, D])
        hnT = sbuf(nc, tmp, "hnT", [P, T])
        gl = sbuf(nc, tmp, "gl", [P, 2, T])
        hid = sbuf(nc, tmp, "hid", [P, 3, T])
        with nc.Block() as block:
            @block.tensor
            def _(pe):
                for t in range(NT):
                    mm = nc.tensor.transpose(K.ps[:, 0, t * P:(t + 1) * P], K.shT[:, t * P:(t + 1) * P], K.ident[:, :])
                mm.then_inc(back, 1)
                pe.wait_ge(hn_ready, NT)
                for t in range(NT):
                    mm = nc.tensor.transpose(K.ps[:, 1, t * P:(t + 1) * P], hn[:, t, :], K.ident[:, :])
                mm.then_inc(turned, 1)
                pe.wait_ge(hnT_ready, 1)
                for c in range(3):
                    n = NC[c]
                    if c == 2:
                        pe.wait_ge(hid_ready, 1)
                    for m in range(2):
                        mm = nc.tensor.matmul(K.ps[0:n, 2 + 2 * (c % 2) + m, :],
                                              K.w2_up[L][:, m * HID2 + c * P:m * HID2 + c * P + n], hnT[:, :],
                                              start=True, stop=True)
                    mm.then_inc(up, 1)
                pe.wait_ge(hid_ready, 3)
                for t in range(NT):
                    for c in range(3):
                        mm = nc.tensor.matmul(K.ps[:, 6, t * P:(t + 1) * P], hid[0:NC[c], c, t * P:(t + 1) * P],
                                              K.w2_down[L][0:NC[c], c, :], start=(c == 0), stop=(c == 2))
                mm.then_inc(down, 1)

            @block.vector
            def _(dve):
                ch = Chain(dve, vec)
                dve.wait_ge(back, 1)
                for t in range(NT):
                    ch.tick(nc.vector.bn_stats(K.stats[:, t, :], K.ps[:, 0, t * P:(t + 1) * P]))
                ch.wait()
                for t in range(NT):
                    ch.tick(nc.vector.bn_aggr(K.mv[:, t, :], K.stats[:, t, :]))
                ch.wait()
                nc.vector.tensor_scalar(K.var[:, 0:NT], K.mv[:, :, 1], 1e-5, None, ALU.add).then_inc(var_ready, 1)
                dve.wait_ge(rstd_ready, 1)
                for t in range(NT):
                    nc.vector.tensor_scalar(hn[:, t, :], K.ps[:, 0, t * P:(t + 1) * P], K.mv[:, t, 0:1],
                                            K.rstd[:, t:t + 1], ALU.subtract, ALU.mult).then_inc(hn_ready, 1)
                for c in range(3):
                    n = NC[c]
                    dve.wait_ge(gelu_done, c + 1)
                    nc.vector.scalar_tensor_tensor(hid[0:n, c, :], K.ps[0:n, 2 + 2 * (c % 2), :],
                                                   K.b2_up[L][0:n, c:c + 1], gl[0:n, c % 2, :],
                                                   ALU.add, ALU.mult).then_inc(hid_ready, 1)
                dve.wait_ge(down, 1)
                ch.do(nc.vector.tensor_tensor(K.y[:, :, :], K.y[:, :, :],
                                              K.ps[:, 6, :].rearrange("p (t d) -> p t d", t=NT), ALU.add))
                nc.vector.tensor_tensor(K.y[:, :, :], K.y[:, :, :],
                                        K.b2_down[L][:, :].unsqueeze(1).to_broadcast([P, NT, D]), ALU.add)

            @block.gpsimd
            def _(pool):
                pool.wait_ge(var_ready, 1)
                nc.gpsimd.tensor_tensor(K.rstd[:, 0:NT], K.var[:, 0:NT], K.neghalf[:, 0:NT],
                                        ALU.pow).then_inc(rstd_ready, 1)

            @block.scalar
            def _(act):
                act.wait_ge(turned, 1)
                nc.scalar.activation(hnT[:, :], K.ps[:, 1, :], ACT.Identity, scale=K.ln2_g[L][:, 0:1],
                                     bias=K.ln2_b[L][:, 0:1]).then_inc(hnT_ready, 1)
                for c in range(3):
                    n = NC[c]
                    act.wait_ge(up, c + 1)
                    if c == 2:
                        act.wait_ge(hid_ready, 1)
                    nc.scalar.activation(gl[0:n, c % 2, :], K.ps[0:n, 3 + 2 * (c % 2), :], ACT.Gelu,
                                         bias=K.b2_up[L][0:n, 3 + c:4 + c]).then_inc(gelu_done, 1)
        K.clear()


def gate_residual(nc, K):
    silu_done, vec = K.pool[0:2]
    with nc.Block() as block:
        @block.scalar
        def _(act):
            nc.scalar.activation(K.y[:, :, :], K.y[:, :, :], ACT.Silu).then_inc(silu_done, 1)

        @block.vector
        def _(dve):
            ch = Chain(dve, vec)
            dve.wait_ge(silu_done, 1)
            ch.do(nc.vector.tensor_tensor(K.y[:, :, :], K.y[:, :, :], K.att[:, :, :], ALU.mult))
            nc.vector.tensor_tensor(K.x[:, :, :], K.x[:, :, :], K.y[:, :, :], ALU.add)
    K.clear()


def local_ffn(nc, K):
    with nc.Block() as block:
        @block.vector
        def _(dve):
            nc.vector.tensor_copy(K.y[:, :, :], K.xn[:, :, :])
    for L in range(2):
        shift_tokens(nc, K)
        local_qkv(nc, K, L)
        local_transpose(nc, K)
        local_attention(nc, K)
        local_out(nc, K, L)
        shift_tokens(nc, K)
        glu(nc, K, L)
    gate_residual(nc, K)




def experts(nc, K):
    gated, vec, e_in, e_done, h12, silu_done, hid_ready, out_done, used = K.pool[0:9]
    with ExitStack() as tmp:
        sc = sbuf(nc, tmp, "sc", [P, NT, E3])
        top = sbuf(nc, tmp, "top", [P, NT, 8])
        idx = sbuf(nc, tmp, "idx", [P, NT, 8], U32)
        idf = sbuf(nc, tmp, "idf", [P, NT, 8])
        ex = sbuf(nc, tmp, "ex", [P, NT])
        pr = sbuf(nc, tmp, "pr", [P, 2, NT])
        eq = sbuf(nc, tmp, "eq", [P, 2, NT, E3])
        pb = sbuf(nc, tmp, "pb", [P, NT, E3])
        a = sbuf(nc, tmp, "silu_a", [P, 2, T])
        h = sbuf(nc, tmp, "hid", [P, 2, 2, T])
        with nc.Block() as block:
            @block.tensor
            def _(pe):
                for t in range(NT):
                    mm = nc.tensor.matmul(K.ps[:, 6, t * E3:(t + 1) * E3], K.xnT[:, t * P:(t + 1) * P],
                                          K.w3_gate[:, :], start=True, stop=True)
                mm.then_inc(gated, 1)

                def down(e):
                    pe.wait_ge(hid_ready, 2 * e + 2)
                    if e:
                        pe.wait_ge(used, e)
                    for t in range(NT):
                        for c in range(2):
                            mm = nc.tensor.matmul(K.ps[:, 7, t * P:(t + 1) * P], h[:, e % 2, c, t * P:(t + 1) * P],
                                                  K.w3_down[:, e, c, :], start=(c == 0), stop=(c == 1))
                    mm.then_inc(out_done, 1)

                for e in range(E3):
                    for c in range(2):
                        n = 2 * e + c
                        if n >= 2:
                            pe.wait_ge(hid_ready, n - 1)
                        for m in range(2):
                            mm = nc.tensor.matmul(K.ps[:, 2 * (n % 2) + m, :],
                                                  K.w3_up[:, e, (2 * m + c) * P:(2 * m + c + 1) * P], K.xnT[:, :],
                                                  start=True, stop=True)
                        mm.then_inc(h12, 1)
                    if e:
                        down(e - 1)
                down(E3 - 1)

            @block.scalar
            def _(act):
                act.wait_ge(e_in, 1)
                nc.scalar.activation(ex[:, :], ex[:, :], ACT.Exp).then_inc(e_done, 1)
                for n in range(2 * E3):
                    act.wait_ge(h12, n + 1)
                    if n >= 2:
                        act.wait_ge(hid_ready, n - 1)
                    nc.scalar.activation(a[:, n % 2, :], K.ps[:, 2 * (n % 2), :], ACT.Silu).then_inc(silu_done, 1)

            @block.vector
            def _(dve):
                ch = Chain(dve, vec)
                dve.wait_ge(gated, 1)
                ch.do(nc.vector.tensor_copy(sc[:, :, :], K.ps[:, 6, 0:NT * E3].rearrange("p (t e) -> p t e", t=NT)))
                for t in range(NT):
                    ch.tick(nc.vector.max(top[:, t, :], sc[:, t, :]))
                ch.wait()
                for t in range(NT):
                    ch.tick(nc.vector.max_index(idx[:, t, :], top[:, t, :], sc[:, t, :]))
                ch.tick(nc.vector.tensor_tensor(ex[:, :], top[:, :, 1], top[:, :, 0], ALU.subtract))
                ch.wait()
                nc.vector.tensor_copy(idf[:, :, :], idx[:, :, :]).then_inc(e_in, 1)
                dve.wait_ge(e_done, 1)
                ch.do(nc.vector.tensor_scalar(pr[:, 0, :], ex[:, :], 1.0, None, ALU.add))
                ch.do(nc.vector.reciprocal(pr[:, 0, :], pr[:, 0, :]))
                ch.do(nc.vector.tensor_tensor(pr[:, 1, :], ex[:, :], pr[:, 0, :], ALU.mult))
                for r in range(2):
                    for t in range(NT):
                        ch.tick(nc.vector.tensor_scalar(eq[:, r, t, :], K.iota8[:, :], idf[:, t, r:r + 1],
                                                        pr[:, r, t:t + 1], ALU.is_equal, ALU.mult))
                ch.wait()
                ch.do(nc.vector.tensor_tensor(pb[:, :, :], eq[:, 0, :, :], eq[:, 1, :, :], ALU.add))

                def add_out(e):
                    dve.wait_ge(out_done, e + 1)
                    for t in range(NT):
                        o = K.ps[:, 7, t * P:(t + 1) * P]
                        if e == 0:
                            i = nc.vector.tensor_scalar(K.y[:, t, :], o, pb[:, t, e:e + 1], None, ALU.mult)
                        else:
                            i = nc.vector.scalar_tensor_tensor(K.y[:, t, :], o, pb[:, t, e:e + 1], K.y[:, t, :],
                                                               ALU.mult, ALU.add)
                        if t < NT - 1:
                            ch.tick(i)
                    i.then_inc(used, 1)
                    dve.wait_ge(used, e + 1)
                    ch.wait()

                for e in range(E3):
                    for c in range(2):
                        n = 2 * e + c
                        dve.wait_ge(silu_done, n + 1)
                        if c == 0 and e >= 2:
                            dve.wait_ge(out_done, e - 1)
                        nc.vector.tensor_tensor(h[:, e % 2, c, :], K.ps[:, 2 * (n % 2) + 1, :], a[:, n % 2, :],
                                                ALU.mult).then_inc(hid_ready, 1)
                    if e:
                        add_out(e - 1)
                add_out(E3 - 1)
        K.clear()


def memory_inputs(nc, K, b):
    projected, raw_ready, conv_ready, sig_done, vec, abs_ready, exp_done, ln_done, aet_ready, silu_done, f_ready, \
        stored = K.pool[0:12]
    with ExitStack() as tmp:
        raw = sbuf(nc, tmp, "raw", [96, T + 3])
        conv = sbuf(nc, tmp, "conv", [96, T])
        aet = sbuf(nc, tmp, "aet", [96, T])
        zt = sbuf(nc, tmp, "zt", [96, T])
        za = sbuf(nc, tmp, "za", [96, T])
        fac = sbuf(nc, tmp, "fac", [P, NT, D])
        th = slice(64, 96)
        with nc.Block() as block:
            @block.tensor
            def _(pe):
                nc.tensor.matmul(K.ps[0:96, 0, :], K.w3_kvq[:, :], K.xnT[:, :], start=True, stop=True)
                nc.tensor.matmul(K.ps[0:96, 1, :], K.w3_aet[:, :], K.xnT[:, :], start=True, stop=True)
                for t in range(NT):
                    mm = nc.tensor.matmul(K.ps[:, 2, t * P:(t + 1) * P], K.xnT[:, t * P:(t + 1) * P], K.w3_g[:, :],
                                          start=True, stop=True)
                mm.then_inc(projected, 1)

            @block.scalar
            def _(act):
                act.wait_ge(projected, 1)
                nc.scalar.activation(raw[:, 3:T + 3], K.ps[0:96, 0, :], ACT.Identity).then_inc(raw_ready, 1)
                nc.scalar.activation(aet[0:64, :], K.ps[0:64, 1, :], ACT.Sigmoid,
                                     bias=K.b3_aet[0:64, 0:1]).then_inc(sig_done, 1)
                nc.scalar.activation(K.y[:, :, :], K.y[:, :, :], ACT.Silu).then_inc(silu_done, 1)
                act.wait_ge(abs_ready, 1)
                nc.scalar.activation(za[th, :], za[th, :], ACT.Exp, scale=-1.0).then_inc(exp_done, 1)
                act.wait_ge(exp_done, 1)
                nc.scalar.activation(za[th, :], za[th, :], ACT.Ln, bias=1.0).then_inc(ln_done, 1)

            @block.vector
            def _(dve):
                ch = Chain(dve, vec)
                ch.tick(nc.vector.memset(raw[:, 0:3], 0.0))
                dve.wait_ge(projected, 1)
                ch.do(nc.vector.tensor_scalar(zt[th, :], K.ps[64:96, 1, :], K.b3_aet[th, 0:1], None, ALU.add))
                nc.vector.scalar_tensor_tensor(za[th, :], zt[th, :], -1.0, zt[th, :], ALU.mult, ALU.max).then_inc(abs_ready, 1)
                dve.wait_ge(raw_ready, 1)
                ch.do(nc.vector.tensor_scalar(conv[:, :], raw[:, 0:T], K.conv_w[:, 0:1], K.conv_b[:, 0:1],
                                              ALU.mult, ALU.add))
                for j in range(1, 4):
                    i = nc.vector.scalar_tensor_tensor(conv[:, :], raw[:, j:j + T], K.conv_w[:, j:j + 1], conv[:, :],
                                                       ALU.mult, ALU.add)
                    if j < 3:
                        ch.do(i)
                    else:
                        i.then_inc(conv_ready, 1)
                dve.wait_ge(ln_done, 1)
                nc.vector.scalar_tensor_tensor(aet[th, :], zt[th, :], 0.0, za[th, :], ALU.max,
                                               ALU.add).then_inc(aet_ready, 1)
                for t in range(NT):
                    ch.tick(nc.vector.tensor_tensor(fac[:, t, :], K.ps[:, 2, t * P:(t + 1) * P], K.g3_b[:, :], ALU.add))
                ch.wait()
                for t in range(NT):
                    ch.tick(nc.vector.tensor_tensor(fac[:, t, :], fac[:, t, :], K.norm3[:, :], ALU.mult))
                ch.wait()
                dve.wait_ge(silu_done, 1)
                nc.vector.tensor_tensor(fac[:, :, :], fac[:, :, :], K.y[:, :, :], ALU.mult).then_inc(f_ready, 1)

            @block.sync
            def _(sp):
                sp.dma_start(K.x_d[b, :, :].rearrange("(t p) d -> p t d", p=P), K.x[:, :, :]).then_inc(stored, 16)
                sp.wait_ge(conv_ready, 1)
                sp.dma_start(K.kvq_d[b, :, :], conv[:, :]).then_inc(stored, 16)
                sp.wait_ge(sig_done, 1)
                sp.wait_ge(aet_ready, 1)
                sp.dma_start(K.aet_d[b, :, :], aet[:, :]).then_inc(stored, 16)
                sp.wait_ge(f_ready, 1)
                sp.dma_start(K.fac_d[b, :, :].rearrange("(t p) d -> p t d", p=P), fac[:, :, :]).then_inc(stored, 16)
                sp.wait_ge(stored, 64)
        K.clear()




def memory_coefficients(nc, K, M):
    landed, meant, used, vec, om_ready, th_ready, prep = K.pool[0:7]
    NTOK = BATCH * T
    with ExitStack() as tmp:
        aet = sbuf(nc, tmp, "aet_in", [96, 2, T])
        om = sbuf(nc, tmp, "om", [CH, NTOK])
        et = sbuf(nc, tmp, "et", [CH, NTOK])
        d1 = sbuf(nc, tmp, "d1", [CH, NTOK])
        Es = sbuf(nc, tmp, "Es", [CH, NTOK])
        om_c = om[:, :].rearrange("p (n t) -> p n t", t=CH)
        et_c = et[:, :].rearrange("p (n t) -> p n t", t=CH)
        d1_c = d1[:, :].rearrange("p (n t) -> p n t", t=CH)
        Es_c = Es[:, :].rearrange("p (n t) -> p n t", t=CH)
        om0 = sbuf(nc, tmp, "om0", [CH, BATCH * NCH, 1])
        et0 = sbuf(nc, tmp, "et0", [CH, BATCH * NCH, 1])
        with nc.Block() as block:
            @block.sync
            def _(sp):
                for b in range(BATCH):
                    if b >= 2:
                        sp.wait_ge(meant, b - 1)
                    sp.dma_start(aet[:, b % 2, :], K.aet_d[b, :, :]).then_inc(landed, 16)
                    sp.wait_ge(landed, 16 * (b + 1))
                for m, dst in enumerate((M.k, M.v, M.q)):
                    sp.dma_start(dst[:, :, :], K.kvq_d[:, 32 * m:32 * m + 32, :].rearrange("b p t -> p b t")
                                 ).then_inc(landed, 16)
                sp.wait_ge(landed, 16 * (BATCH + 3))

            @block.tensor
            def _(pe):
                for b in range(BATCH):
                    pe.wait_ge(landed, 16 * (b + 1))
                    if b >= 2:
                        pe.wait_ge(used, 3 * (b - 1))
                    for m in range(3):
                        mm = nc.tensor.matmul(K.ps[0:CH, 4 * (b % 2) + m, :], M.mean_w[:, m, :], aet[:, b % 2, :],
                                              start=True, stop=True)
                    mm.then_inc(meant, 1)

            @block.vector
            def _(dve):
                ch = Chain(dve, vec)
                for b in range(BATCH):
                    dve.wait_ge(meant, b + 1)
                    p = 4 * (b % 2)
                    s = slice(b * T, (b + 1) * T)
                    nc.vector.tensor_scalar(om[:, s], K.ps[0:CH, p, :], -0.1, 1.0, ALU.mult, ALU.add).then_inc(used, 1)
                    nc.vector.tensor_scalar(et[:, s], K.ps[0:CH, p + 1, :], 0.9, 0.05, ALU.mult,
                                            ALU.add).then_inc(used, 1)
                    nc.vector.tensor_scalar(M.nth[:, s], K.ps[0:32, p + 2, :], -0.1, None, ALU.mult).then_inc(used, 1)
                dve.wait_ge(used, 3 * BATCH)
                ch.tick(nc.vector.tensor_copy(om0[:, :, :], om_c[:, :, 0:1]))
                ch.tick(nc.vector.tensor_copy(et0[:, :, :], et_c[:, :, 0:1]))
                ch.tick(nc.vector.tensor_copy(d1_c, K.ident[0:CH, 0:CH].unsqueeze(1).to_broadcast([CH, BATCH * NCH, CH])))
                ch.wait()
                ch.tick(nc.vector.memset(om_c[:, :, 0:1], 0.0))
                ch.tick(nc.vector.memset(et_c[:, :, 0:1], 0.0))
                ch.wait()
                ch.do(nc.vector.tensor_tensor_scan(Es[:, :], et[:, :], d1[:, :], 0.0, ALU.mult, ALU.add))
                ch.do(nc.vector.tensor_tensor_scan(M.C[:, :], om[:, :], Es[:, :], 0.0, ALU.mult, ALU.add))
                ch.do(nc.vector.tensor_copy(M.E_end[:, :, :], Es_c[:, :, CH - 1:CH]))
                ch.do(nc.vector.memset(d1[:, :], 0.0))
                ch.do(nc.vector.tensor_copy(d1_c[:, :, 0:1], et0[:, :, :]))
                ch.do(nc.vector.tensor_tensor_scan(Es[:, :], et[:, :], d1[:, :], 0.0, ALU.mult, ALU.add))
                ch.tick(nc.vector.tensor_copy(M.Eall_end[:, :, :], Es_c[0:32, :, CH - 1:CH]))
                ch.do(nc.vector.tensor_tensor_scan(M.B[:, :], om[0:32, :], Es[0:32, :], 0.0, ALU.mult, ALU.add))
                ch.do(nc.vector.tensor_copy(d1_c[:, :, 0:1], om0[:, :, :]))
                ch.do(nc.vector.tensor_tensor_scan(M.A[:, :], om[0:32, :], d1[0:32, :], 0.0, ALU.mult, ALU.add))
        K.clear()


def memory_chunk(nc, K, M, c):
    sig = K.pool
    (staged, z_done, sg_done, h_done, pred_done, dp_done, dh_done, dz_done, sums_done, sk_done, n2_done, gn_done,
     uw_done, turned, tok_done, vec, g1_done, m1_done, zr_done, hr_done, g2_done, m2_done, r_done, upd_done) = sig
    NB = BATCH * CH

    def at(t, b):
        return t[:, b * CH:(b + 1) * CH]

    with nc.Block() as block:
        @block.scalar
        def _(act):
            for n, (dst, src) in enumerate(((M.kc, M.k), (M.vc, M.v), (M.qc, M.q))):
                nc.scalar.activation(dst[:, :].rearrange("p (b t) -> p b t", b=BATCH),
                                     src[:, :, bass.ds(c * CH, CH)], ACT.Identity).then_inc(staged, 1)
            act.wait_ge(z_done, 1)
            nc.scalar.activation(M.sg[:, :], K.ps[0:32, 0, :], ACT.Sigmoid).then_inc(sg_done, 1)
            act.wait_ge(sums_done, 1)
            nc.scalar.activation(M.s1[:, :], K.ps[0:32, 4, :], ACT.Identity).then_inc(sk_done, 1)
            nc.scalar.activation(M.s2[:, :], K.ps[0:32, 6, :], ACT.Identity).then_inc(sk_done, 1)
            act.wait_ge(n2_done, 1)
            nc.scalar.activation(M.n2[:, :], M.n2[:, :], ACT.Sqrt).then_inc(gn_done, 1)
            act.wait_ge(zr_done, 1)
            nc.scalar.activation(M.sg[:, :], K.ps[0:32, 4, :], ACT.Sigmoid).then_inc(sg_done, 1)

        @block.tensor
        def _(pe):
            pe.wait_ge(staged, 3)
            for b in range(BATCH):
                mm = nc.tensor.matmul(at(K.ps[0:32, 0, :], b), M.W1T[:, b, :], at(M.kc, b), start=True, stop=True)
            mm.then_inc(z_done, 1)
            for b in range(BATCH):
                mm = nc.tensor.matmul(at(K.ps[0:CH, 7, :], b), at(M.kc, b), at(M.qc, b), start=True, stop=True)
            mm.then_inc(g1_done, 1)
            pe.wait_ge(h_done, 1)
            for b in range(BATCH):
                mm = nc.tensor.matmul(at(K.ps[0:32, 1, :], b), M.W2T[:, b, :], at(M.h, b), start=True, stop=True)
            mm.then_inc(pred_done, 1)
            pe.wait_ge(dp_done, 1)
            for b in range(BATCH):
                mm = nc.tensor.matmul(at(K.ps[0:32, 2, :], b), M.W2[:, b, :], at(M.dp, b), start=True, stop=True)
            mm.then_inc(dh_done, 1)
            pe.wait_ge(dz_done, 1)
            for m, q in enumerate((M.qdz, M.qk, M.qdp, M.qh)):
                mm = nc.tensor.matmul(K.ps[0:32, 3 + m, :], K.ones32[:, :], q[:, :], start=True, stop=True)
            mm.then_inc(sums_done, 1)
            pe.wait_ge(uw_done, 1)
            for m, src in enumerate((M.u, M.w, M.h, M.kc)):
                for b in range(BATCH):
                    o = (m % 2) * 256 + b * 32
                    mm = nc.tensor.transpose(K.ps[0:CH, m // 2, o:o + 32], at(src, b), K.ident[0:32, 0:32])
            mm.then_inc(turned, 1)
            pe.wait_ge(m1_done, 1)
            pe.wait_ge(tok_done, 1)
            for b in range(BATCH):
                o = at(K.ps[0:32, 4, :], b)
                nc.tensor.matmul(o, M.W1T[:, b, :], at(M.qa, b), start=True, stop=False)
                nc.tensor.matmul(o, M.S1T[:, b, :], at(M.qb, b), start=False, stop=False)
                mm = nc.tensor.matmul(o, M.tok[:, 0, b, :], at(M.m1, b), start=False, stop=True)
            mm.then_inc(zr_done, 1)
            pe.wait_ge(hr_done, 1)
            for b in range(BATCH):
                mm = nc.tensor.matmul(at(K.ps[0:CH, 5, :], b), at(M.h, b), at(M.hr, b), start=True, stop=True)
            mm.then_inc(g2_done, 1)
            for b in range(BATCH):
                nc.tensor.matmul(K.ps[0:32, 2, b * 64:(b + 1) * 64], M.tok[:, 3, b, :], M.ec[:, 0, b, :],
                                 start=True, stop=True)
            for b in range(BATCH):
                mm = nc.tensor.matmul(K.ps[0:32, 3, b * 64:(b + 1) * 64], M.tok[:, 2, b, :], M.ec[:, 1, b, :],
                                      start=True, stop=True)
            mm.then_inc(upd_done, 1)
            pe.wait_ge(m2_done, 1)
            for b in range(BATCH):
                o = at(K.ps[0:32, 6, :], b)
                nc.tensor.matmul(o, M.W2T[:, b, :], at(M.qa, b), start=True, stop=False)
                nc.tensor.matmul(o, M.S2T[:, b, :], at(M.qb, b), start=False, stop=False)
                mm = nc.tensor.matmul(o, M.tok[:, 1, b, :], at(M.m1, b), start=False, stop=True)
            mm.then_inc(r_done, 1)

        @block.vector
        def _(dve):
            ch = Chain(dve, vec)
            v3 = lambda t: t.rearrange("p (b t) -> p b t", b=BATCH)
            big = lambda t: t[:, :].rearrange("p (b t) -> p b t", b=BATCH)[:, :, bass.ds(c * CH, CH)]
            ends = lambda t: t[:, :, :].rearrange("p (b n) o -> p b (n o)", b=BATCH)[:, :, bass.ds(c, 1)]
            dve.wait_ge(staged, 3)
            ch.tick(nc.vector.tensor_copy(v3(M.cc[:, :]), big(M.C)))
            ch.tick(nc.vector.tensor_copy(v3(M.ac[:, :]), big(M.A)))
            ch.tick(nc.vector.tensor_copy(v3(M.bc[:, :]), big(M.B)))
            ch.tick(nc.vector.tensor_copy(v3(M.tc[:, :]), big(M.nth)))
            ch.tick(nc.vector.tensor_copy(M.e_end[:, :, :], ends(M.E_end)))
            ch.tick(nc.vector.tensor_copy(M.eall_end[:, :, :], ends(M.Eall_end)))
            ch.tick(nc.vector.tensor_tensor(M.qk[:, :], M.kc[:, :], M.kc[:, :], ALU.mult))
            ch.wait()
            ch.tick(nc.vector.tensor_tensor(M.qa[:, :], M.qc[:, :], M.ac[:, :], ALU.mult))
            ch.tick(nc.vector.tensor_tensor(M.qb[:, :], M.qc[:, :], M.bc[:, :], ALU.mult))
            dve.wait_ge(sg_done, 1)
            nc.vector.tensor_tensor(M.h[:, :], K.ps[0:32, 0, :], M.sg[:, :], ALU.mult).then_inc(h_done, 1)
            dve.wait_ge(h_done, 1)
            ch.tick(nc.vector.tensor_tensor(M.t1[:, :], M.h[:, :], M.sg[:, :], ALU.mult))
            ch.tick(nc.vector.tensor_tensor(M.ds[:, :], M.h[:, :], M.sg[:, :], ALU.add))
            ch.tick(nc.vector.tensor_tensor(M.qh[:, :], M.h[:, :], M.h[:, :], ALU.mult))
            ch.wait()
            ch.tick(nc.vector.tensor_tensor(M.ds[:, :], M.ds[:, :], M.t1[:, :], ALU.subtract))
            dve.wait_ge(pred_done, 1)
            ch.do(nc.vector.tensor_tensor(M.dp[:, :], K.ps[0:32, 1, :], M.vc[:, :], ALU.subtract))
            nc.vector.tensor_scalar(M.dp[:, :], M.dp[:, :], 0.2, None, ALU.mult).then_inc(dp_done, 1)
            dve.wait_ge(dp_done, 1)
            ch.tick(nc.vector.tensor_tensor(M.qdp[:, :], M.dp[:, :], M.dp[:, :], ALU.mult))
            dve.wait_ge(dh_done, 1)
            ch.do(nc.vector.tensor_tensor(M.dz[:, :], K.ps[0:32, 2, :], M.ds[:, :], ALU.mult))
            nc.vector.tensor_tensor(M.qdz[:, :], M.dz[:, :], M.dz[:, :], ALU.mult).then_inc(dz_done, 1)
            dve.wait_ge(g1_done, 1)
            nc.vector.tensor_tensor(M.m1[:, :], K.ps[0:CH, 7, :], M.cc[:, :], ALU.mult).then_inc(m1_done, 1)
            dve.wait_ge(sk_done, 2)
            ch.tick(nc.vector.tensor_tensor(M.n2[:, :], K.ps[0:32, 3, :], M.s1[:, :], ALU.mult))
            ch.tick(nc.vector.tensor_tensor(M.t1[:, :], K.ps[0:32, 5, :], M.s2[:, :], ALU.mult))
            ch.wait()
            nc.vector.tensor_tensor(M.n2[:, :], M.n2[:, :], M.t1[:, :], ALU.add).then_inc(n2_done, 1)
            dve.wait_ge(gn_done, 1)
            ch.do(nc.vector.tensor_scalar(M.n2[:, :], M.n2[:, :], 1e-6, None, ALU.max))
            ch.do(nc.vector.reciprocal(M.n2[:, :], M.n2[:, :]))
            ch.do(nc.vector.scalar_tensor_tensor(M.n2[:, :], M.n2[:, :], 1.0, M.tc[:, :], ALU.min, ALU.mult))
            ch.do(nc.vector.tensor_tensor(M.u[:, :], M.dz[:, :], M.n2[:, :], ALU.mult))
            nc.vector.tensor_tensor(M.w[:, :], M.dp[:, :], M.n2[:, :], ALU.mult).then_inc(uw_done, 1)
            dve.wait_ge(turned, 1)
            nc.vector.tensor_copy(M.tok[:, :, :, :], K.ps[0:CH, 0:2, :].rearrange(
                "p a (m b d) -> p (a m) b d", m=2, b=BATCH)).then_inc(tok_done, 1)
            dve.wait_ge(tok_done, 1)
            c_end = M.cc[:, :].rearrange("p (b t) -> p b t", b=BATCH)[:, :, CH - 1:CH].to_broadcast([CH, BATCH, 32])
            for m in range(2):
                ch.tick(nc.vector.tensor_tensor(M.ec[:, m, :, 0:32], M.tok[:, m, :, :],
                                                M.e_end[:, :, :].to_broadcast([CH, BATCH, 32]), ALU.mult))
                ch.tick(nc.vector.tensor_tensor(M.ec[:, m, :, 32:64], M.tok[:, m, :, :], c_end, ALU.mult))
            ch.wait()
            dve.wait_ge(sg_done, 2)
            ch.do(nc.vector.tensor_tensor(M.hr[:, :], K.ps[0:32, 4, :], M.sg[:, :], ALU.mult))
            ch.tick(nc.vector.tensor_tensor(M.qa[:, :], M.hr[:, :], M.ac[:, :], ALU.mult))
            ch.wait()
            nc.vector.tensor_tensor(M.qb[:, :], M.hr[:, :], M.bc[:, :], ALU.mult).then_inc(hr_done, 1)
            dve.wait_ge(g2_done, 1)
            dve.wait_ge(hr_done, 1)
            nc.vector.tensor_tensor(M.m1[:, :], K.ps[0:CH, 5, :], M.cc[:, :], ALU.mult).then_inc(m2_done, 1)
            dve.wait_ge(upd_done, 1)
            dve.wait_ge(r_done, 1)
            nc.vector.tensor_copy(M.ret[:, :, bass.ds(c * CH, CH)], v3(K.ps[0:32, 6, :]))
            a_end = v3(M.ac[:, :])[:, :, CH - 1:CH].to_broadcast([32, BATCH, 32])
            b_end = v3(M.bc[:, :])[:, :, CH - 1:CH].to_broadcast([32, BATCH, 32])
            e_end = M.eall_end[:, :, :].to_broadcast([32, BATCH, 32])
            for W, S, bank in ((M.W1T, M.S1T, 2), (M.W2T, M.S2T, 3)):
                new = K.ps[0:32, bank, :].rearrange("p (b x) -> p b x", b=BATCH)
                ch.do(nc.vector.tensor_tensor(W[:, :, :], W[:, :, :], a_end, ALU.mult))
                ch.do(nc.vector.tensor_tensor(M.t2[:, :, :], S[:, :, :], b_end, ALU.mult))
                ch.do(nc.vector.tensor_tensor(W[:, :, :], W[:, :, :], M.t2[:, :, :], ALU.add))
                ch.do(nc.vector.tensor_tensor(W[:, :, :], W[:, :, :], new[:, :, 32:64], ALU.add))
                ch.do(nc.vector.tensor_tensor(S[:, :, :], S[:, :, :], e_end, ALU.mult))
                ch.do(nc.vector.tensor_tensor(S[:, :, :], S[:, :, :], new[:, :, 0:32], ALU.add))
            nc.vector.transpose(M.W2[:, :, :].rearrange("p b d -> p (b d)"),
                                M.W2T[:, :, :].rearrange("p b d -> p (b d)"))
    K.clear()


def memory_output(nc, K, M, b, out):
    landed, staged, projected, vec, ms_ready, rs_ready, done, stored = K.pool[0:8]
    with ExitStack() as tmp:
        x = sbuf(nc, tmp, "x_back", [P, NT, D])
        fac = sbuf(nc, tmp, "fac_back", [P, NT, D])
        rc = sbuf(nc, tmp, "rc", [32, T])
        with nc.Block() as block:
            @block.sync
            def _(sp):
                sp.dma_start(x[:, :, :], K.x_d[b, :, :].rearrange("(t p) d -> p t d", p=P)).then_inc(landed, 16)
                sp.dma_start(fac[:, :, :], K.fac_d[b, :, :].rearrange("(t p) d -> p t d", p=P)).then_inc(landed, 16)
                sp.wait_ge(done, 1)
                sp.dma_start(out[b, :, :].rearrange("(t p) d -> p t d", p=P), x[:, :, :]).then_inc(stored, 16)
                sp.wait_ge(stored, 16)

            @block.scalar
            def _(act):
                nc.scalar.activation(rc[:, :], M.ret[:, bass.ds(b, 1), :].rearrange("p b t -> p (b t)"),
                                     ACT.Identity).then_inc(staged, 1)

            @block.tensor
            def _(pe):
                pe.wait_ge(staged, 1)
                for t in range(NT):
                    mm = nc.tensor.matmul(K.ps[:, 0, t * P:(t + 1) * P], rc[:, t * P:(t + 1) * P], M.wo[:, :],
                                          start=True, stop=True)
                mm.then_inc(projected, 1)

            @block.vector
            def _(dve):
                ch = Chain(dve, vec)
                dve.wait_ge(projected, 1)
                for t in range(NT):
                    ch.tick(nc.vector.bn_stats(K.stats[:, t, :], K.ps[:, 0, t * P:(t + 1) * P]))
                ch.wait()
                for t in range(NT):
                    ch.tick(nc.vector.bn_aggr(K.mv[:, t, :], K.stats[:, t, :]))
                ch.wait()
                ch.do(nc.vector.tensor_tensor(K.var[:, 0:NT], K.mv[:, :, 0], K.mv[:, :, 0], ALU.mult))
                nc.vector.scalar_tensor_tensor(K.var[:, 0:NT], K.mv[:, :, 1], 1e-6, K.var[:, 0:NT],
                                               ALU.add, ALU.add).then_inc(ms_ready, 1)
                dve.wait_ge(rs_ready, 1)
                dve.wait_ge(landed, 32)
                for t in range(NT):
                    ch.tick(nc.vector.scalar_tensor_tensor(fac[:, t, :], K.ps[:, 0, t * P:(t + 1) * P],
                                                           K.rstd[:, t:t + 1], fac[:, t, :], ALU.mult, ALU.mult))
                ch.wait()
                nc.vector.tensor_tensor(x[:, :, :], x[:, :, :], fac[:, :, :], ALU.add).then_inc(done, 1)

            @block.gpsimd
            def _(pool):
                pool.wait_ge(ms_ready, 1)
                nc.gpsimd.tensor_tensor(K.rstd[:, 0:NT], K.var[:, 0:NT], K.neghalf[:, 0:NT],
                                        ALU.pow).then_inc(rs_ready, 1)
        K.clear()




def rope_tables():
    theta = (np.float32(10000.0) ** (-2.0 * np.arange(HD // 2, dtype=np.float32) / HD)).astype(np.float32)
    ang = np.outer(np.arange(T, dtype=np.float32), theta).astype(np.float32).astype(np.float64)
    cos = np.repeat(np.cos(ang), 2, axis=1).astype(np.float32)
    sin = np.stack([-np.sin(ang), np.sin(ang)], axis=1).astype(np.float32)
    return (np.ascontiguousarray(cos.reshape(NT, P, HD).transpose(1, 0, 2)),
            np.ascontiguousarray(sin.reshape(NT, P, 2, HD // 2).transpose(1, 0, 2, 3)))


def xpos_tables():
    half = np.arange(0, LD, 2, dtype=np.float32)
    inv = (np.float32(1.0) / np.float32(10000.0) ** (half / np.float32(LD))).astype(np.float32)
    t = np.arange(T, dtype=np.float32)
    fr = (t[:, None] * inv[None, :]).astype(np.float32)
    fr = np.concatenate([fr, fr], axis=1).astype(np.float64)
    base = ((half + np.float32(0.4 * LD)) / np.float32(1.4 * LD)).astype(np.float32)
    power = ((t - T // 2) / np.float32(WIN // 2)).astype(np.float32)
    sc = base[None, :].astype(np.float64) ** power[:, None]
    sc = np.concatenate([sc, sc], axis=1)
    sign = np.where(np.arange(LD) < LD // 2, -1.0, 1.0)
    tabs = np.stack([np.cos(fr) * sc, np.sin(fr) * sc * sign, np.cos(fr) / sc, np.sin(fr) / sc * sign])
    return np.ascontiguousarray(tabs.reshape(4, NT, P, LD).transpose(2, 0, 1, 3).astype(np.float32))


def masks():
    r, c = np.arange(P)[:, None], np.arange(P)[None, :]
    mq = np.where(c > r, NEG, 0.0).astype(np.float32)
    c = np.arange(P + WIN)[None, :]
    band = np.where((c < r) | (c > r + WIN), NEG, 0.0).astype(np.float32)
    band0 = np.where(c < WIN, NEG, band).astype(np.float32)
    return np.concatenate([np.eye(P, dtype=np.float32), mq, mq.T, band, band0], axis=1)


def build_kernel(nc, A, out, stop=None):
    NAMED.clear()
    with ExitStack() as ctx:
        K = Kit(nc, ctx)
        K.ps = ctx.enter_context(nc.psum_tensor("banks", [P, 8, 512], F32))
        K.x_d = nc.dram_tensor("x_scratch", [BATCH, T, D], F32, kind="Internal").ap()
        K.fac_d = nc.dram_tensor("factor_scratch", [BATCH, T, D], F32, kind="Internal").ap()
        K.parts_d = nc.dram_tensor("parts_scratch", [2, 3, H * HD, T], BF16, kind="Internal").ap()
        K.nmax_d = nc.dram_tensor("maxima_scratch", [2, H, T], BF16, kind="Internal").ap()
        K.kvq_d = nc.dram_tensor("kvq_scratch", [BATCH, 96, T], F32, kind="Internal").ap()
        K.aet_d = nc.dram_tensor("aet_scratch", [BATCH, 96, T], F32, kind="Internal").ap()

        def sb(name, shape, dt=F32, c=ctx):
            return sbuf(nc, c, name, shape, dt)

        K.ident = sb("ident", [P, P])
        K.neghalf = sb("neghalf", [P, 2 * NT * LH])
        K.ones32 = sb("ones32", [32, 32])
        K.stats = sb("stats", [P, NT, 6])
        K.mv = sb("mv", [P, NT, 2])
        K.var = sb("var", [P, NT])
        K.rstd = sb("rstd", [P, NT])
        with ExitStack() as loop:
            batch_loop(nc, K, loop, A, out, stop)
        if stop is None:
            with ExitStack() as mem:
                memory(nc, K, mem, A, out)


def batch_loop(nc, K, ctx, A, out, stop):
    def sb(name, shape, dt=F32):
        return sbuf(nc, ctx, name, shape, dt)

    loads = []

    def whole(name, src=None, bc=False):
        src = A[name] if src is None else src
        shape = ([P] + list(src.shape)) if bc else list(src.shape)
        t = sb(name + "_s", shape)
        ap = src.partition_broadcast(P) if bc else src
        full = tuple(slice(None) for _ in shape)
        loads.append((t[full], ap[full] if not bc else ap))
        return t

    K.w0_qkv = whole("w0_qkv")
    K.b0_qkv = whole("b0_qkv", bc=True)
    K.w0_1, K.w0_2, K.w0_h1, K.w0_h2, K.w0_3 = [whole(n) for n in ("w0_1", "w0_2", "w0_h1", "w0_h2", "w0_3")]
    K.s0_1, K.s0_2, K.s0_h1, K.s0_h2 = [whole(n) for n in ("s0_1", "s0_2", "s0_h1", "s0_h2")]
    K.s0_3 = whole("s0_3", bc=True)
    K.w1_q, K.w1_k, K.w1_v, K.w1_o = [whole(n) for n in ("w1_q", "w1_k", "w1_v", "w1_o")]
    K.w_gu = sb("w_gu", [P, 2 * I1])
    K.w_down = sb("w_down", [P, 3, D])
    K.w2_q, K.w2_k, K.w2_v, K.w2_ao = [whole(n) for n in ("w2_q", "w2_k", "w2_v", "w2_ao")]
    K.b2_q, K.b2_k = whole("b2_q"), whole("b2_k")
    K.b2_v, K.b2_ao, K.rmsw = [whole(n, bc=True) for n in ("b2_v", "b2_ao", "rmsw")]
    K.w2_qkv, K.w2_o, K.w2_up, K.w2_down, K.b2_up, K.b2_down, K.ln2_g, K.ln2_b = [], [], [], [], [], [], [], []
    for L in range(2):
        K.w2_qkv.append(whole(f"w2_qkv{L}"))
        K.w2_o.append(whole(f"w2_o{L}"))
        K.w2_up.append(whole(f"w2_up{L}"))
        K.b2_up.append(whole(f"b2_up{L}"))
        K.b2_down.append(whole(f"b2_down{L}", bc=True))
        K.ln2_g.append(whole(f"ln2_g{L}"))
        K.ln2_b.append(whole(f"ln2_b{L}"))
        w = sb(f"w2_down{L}_s", [P, 3, D])
        n = HID2 - 2 * P
        loads.append((w[:, 0:2, :], A[f"w2_down{L}"][0:2 * P, :].rearrange("(c p) d -> p c d", p=P)))
        loads.append((w[0:n, 2, :], A[f"w2_down{L}"][2 * P:HID2, :]))
        K.w2_down.append(w)
    K.w3_up, K.w3_down, K.w3_gate, K.w3_kvq, K.w3_aet, K.w3_g = [
        whole(n) for n in ("w3_up", "w3_down", "w3_gate", "w3_kvq", "w3_aet", "w3_g")]
    K.g3_b, K.norm3 = whole("g3_b", bc=True), whole("norm3", bc=True)
    K.conv_w, K.conv_b, K.b3_aet = whole("conv_w"), whole("conv_b"), whole("b3_aet")

    cos, sin = rope_tables()
    K.rope_cos = whole("rope_cos", nc.inline_tensor(cos, name="rope_cos_c").ap())
    K.rope_sin = whole("rope_sin", nc.inline_tensor(sin, name="rope_sin_c").ap())
    K.iota8 = whole("iota8", nc.inline_tensor(np.arange(E3, dtype=np.float32), name="iota8_c").ap(), bc=True)
    K.cosq, K.sinq, K.cosk, K.sink = [[sb(f"{n}{L}", [P, NT, LD]) for L in range(2)]
                                      for n in ("cosq", "sinq", "cosk", "sink")]
    K.x, K.xn, K.att = [sb(n, [P, NT, D]) for n in ("x", "xn", "att")]
    K.xnT = sb("xnT", [P, T])
    K.identb = sb("identb", [P, P], BF16)
    K.mask_q = sb("mask_q", [P, P], BF16)
    K.mask_k = sb("mask_k", [P, P], BF16)
    K.mask_band = sb("mask_band", [P, P + WIN], BF16)
    K.mask_band0 = sb("mask_band0", [P, P + WIN], BF16)
    fills = [(K.neghalf[:, :], -0.5), (K.ones32[:, :], 1.0)]
    with ExitStack() as tmp:
        consts = masks()
        ct = sbuf(nc, tmp, "consts", [P, consts.shape[1]])
        tabs = sbuf(nc, tmp, "tabs", [P, 4, NT, LD])
        qks = sbuf(nc, tmp, "qks", [P, 2, 4, LD])
        K.gate_rows, K.up_rows = [sbuf(nc, tmp, n, [P, 3, D]) for n in ("gate_rows", "up_rows")]
        K.down_rows = sbuf(nc, tmp, "down_rows", [P, I1])
        loads.append((ct[:, :], nc.inline_tensor(consts, name="masks_c").ap()))
        loads.append((K.ident[:, :], nc.inline_tensor(np.eye(P, dtype=np.float32), name="ident_c").ap()))
        loads.append((tabs[:, :, :, :], nc.inline_tensor(xpos_tables(), name="xpos_c").ap()))
        loads.append((qks[:, :, :, :], A["qk_scales"].partition_broadcast(P)))
        for t, n in ((K.gate_rows, "w_gate"), (K.up_rows, "w_up")):
            loads.append((t[:, 0:2, :], A[n][0:2 * P, :].rearrange("(c p) d -> p c d", p=P)))
            loads.append((t[0:I1 - 2 * P, 2, :], A[n][2 * P:I1, :]))
        loads.append((K.down_rows[:, :], A["w_downr"]))
        load_constants(nc, K, loads)
        with nc.Block() as block:
            @block.vector
            def _(dve):
                for dst, value in fills:
                    nc.vector.memset(dst, value)
                o = 0
                for t in (K.identb, K.mask_q, K.mask_k, K.mask_band, K.mask_band0):
                    n = t.shape[1]
                    nc.vector.tensor_copy(t[:, :], ct[:, o:o + n])
                    o += n
                for L in range(2):
                    for m, t in enumerate((K.cosq[L], K.sinq[L], K.cosk[L], K.sink[L])):
                        nc.vector.tensor_tensor(t[:, :, :], tabs[:, m, :, :],
                                                qks[:, L, m, :].unsqueeze(1).to_broadcast([P, NT, LD]), ALU.mult)
        quantize_weights(nc, K, tmp)

    with nc.Fori(0, BATCH) as b:
        def finish():
            stored = K.pool[0]
            with nc.Block() as block:
                @block.sync
                def _(sp):
                    sp.dma_start(out[b, :, :].rearrange("(t p) d -> p t d", p=P), K.x[:, :, :]).then_inc(stored, 16)
                    sp.wait_ge(stored, 16)
            K.clear()

        layer_norm(nc, K, A["x"][b, :, :].rearrange("(t p) d -> p t d", p=P))
        with ExitStack() as atn:
            attention_buffers(nc, K, atn)
            project_rope(nc, K)
            attention(nc, K, False)
        ternary_ffn(nc, K)
        if stop == 0:
            finish()
        if stop is None or stop > 0:
            layer_norm(nc, K)
            with ExitStack() as atn:
                attention_buffers(nc, K, atn)
                project_plain(nc, K, K.xnT, K.w1_q, K.w1_k, K.w1_v, None)
                attention(nc, K, True)
            project_out(nc, K, K.w1_o, None)
            fp4_ffn(nc, K)
            if stop == 1:
                finish()
        if stop is None or stop > 1:
            layer_norm(nc, K)
            with ExitStack() as two:
                K.xr = sbuf(nc, two, "xr", [P, NT, D])
                K.xrT = sbuf(nc, two, "xrT", [P, T])
                rms_norm(nc, K)
                with ExitStack() as atn:
                    attention_buffers(nc, K, atn)
                    project_plain(nc, K, K.xrT, K.w2_q, K.w2_k, K.w2_v, K.b2_v)
                    attention(nc, K, True, K.b2_q[:, 0:1], K.b2_k[:, 0:1])
                project_out(nc, K, K.w2_ao, K.b2_ao)
            with ExitStack() as two:
                K.y = sbuf(nc, two, "y", [P, NT, D])
                K.shT = sbuf(nc, two, "shT", [P, T])
                K.q_tm, K.k_tm, K.v_tm = [sbuf(nc, two, n, [P, NT, INNER]) for n in ("q_tm", "k_tm", "v_tm")]
                K.ssq, K.rn = [sbuf(nc, two, n, [P, 2, NT, LH]) for n in ("ssq", "rn")]
                K.rnq8 = sbuf(nc, two, "rnq8", [P, NT, LH])
                K.qz = sbuf(nc, two, "qz", [P, LH, T])
                K.kT = sbuf(nc, two, "kT", [P, LH // 2, T])
                K.oT = sbuf(nc, two, "oT2", [P, LH // 2, T])
                local_ffn(nc, K)
            if stop == 2:
                finish()
        if stop is None:
            layer_norm(nc, K)
            with ExitStack() as three:
                K.y = sbuf(nc, three, "y3", [P, NT, D])
                experts(nc, K)
                memory_inputs(nc, K, b)


def attention_buffers(nc, K, ctx):
    K.qs = sbuf(nc, ctx, "qs", [P, H, T], BF16)
    K.ks = sbuf(nc, ctx, "ks", [P, H, T], BF16)
    K.v32 = sbuf(nc, ctx, "v32", [P, NT, H, 32])
    with nc.Block() as block:
        @block.gpsimd
        def _(pool):
            nc.gpsimd.memset(K.qs[64:128, :, :], 0.0)

        @block.vector
        def _(dve):
            nc.vector.memset(K.v32[:, :, :, HD:32], 0.0)
            nc.vector.memset(K.ks[64:96, :, :], 0.0)
            nc.vector.memset(K.ks[96:128, :, :], 1.0)
    with nc.Block() as block:
        @block.vector
        def _(dve):
            nc.vector.memset(K.v32[:, :, :, HD:HD + 1], 1.0)
    K.clear()


class Memory:
    pass


def memory(nc, K, ctx, A, out):
    M = Memory()

    def sb(name, shape, dt=F32):
        return sbuf(nc, ctx, name, shape, dt)

    M.wo = sb("wo3", [32, P])
    M.mw = sb("mw", [32, 3, 32])
    M.mean_w = sb("mean_w", [96, 3, CH])
    M.W1T, M.W2T, M.W2, M.S1T, M.S2T = [sb(n, [32, BATCH, 32]) for n in ("W1T", "W2T", "W2", "S1T", "S2T")]
    M.k, M.v, M.q, M.ret = [sb(n, [32, BATCH, T]) for n in ("k_all", "v_all", "q_all", "ret")]
    M.C = sb("C", [CH, BATCH * T])
    M.A, M.B, M.nth = [sb(n, [32, BATCH * T]) for n in ("A_all", "B_all", "nth")]
    M.E_end = sb("E_end", [CH, BATCH * NCH, 1])
    M.Eall_end = sb("Eall_end", [32, BATCH * NCH, 1])
    mean = np.zeros((96, 3, CH), np.float32)
    for m in range(3):
        mean[32 * m:32 * m + 32, m, :] = 1.0 / 32
    load_constants(nc, K, [(M.wo[:, :], A["w3_o"]), (M.mw[:, :, :], A["mem_w"]),
                           (M.mean_w[:, :, :], nc.inline_tensor(mean, name="mean_c").ap())])
    with nc.Block() as block:
        @block.vector
        def _(dve):
            for m, t in enumerate((M.W1T, M.W2T, M.W2)):
                nc.vector.tensor_copy(t[:, :, :], M.mw[:, m, :].unsqueeze(1).to_broadcast([32, BATCH, 32]))
            nc.vector.memset(M.S1T[:, :, :], 0.0)
            nc.vector.memset(M.S2T[:, :, :], 0.0)
    memory_coefficients(nc, K, M)
    with ExitStack() as tmp:
        NB = BATCH * CH
        for names, parts in ((("kc", "vc", "qc", "sg", "h", "dp", "ds", "dz", "t1", "qk", "qh", "qdp", "qdz"), 32),):
            (M.kc, M.vc, M.qc, M.sg, M.h, M.dp, M.ds, M.dz, M.t1, M.qk, M.qh, M.qdp, M.qdz) = [
                sbuf(nc, tmp, n, [parts, NB]) for n in names]
        M.s1, M.s2, M.n2, M.u, M.w, M.hr, M.qa, M.qb, M.ac, M.bc, M.tc = [
            sbuf(nc, tmp, n, [32, NB]) for n in ("s1", "s2", "n2", "u", "w", "hr", "qa", "qb", "ac", "bc", "tc")]
        M.cc, M.m1 = [sbuf(nc, tmp, n, [CH, NB]) for n in ("cc", "m1")]
        M.tok = sbuf(nc, tmp, "tok", [CH, 4, BATCH, 32])
        M.ec = sbuf(nc, tmp, "ec", [CH, 2, BATCH, 64])
        M.t2 = sbuf(nc, tmp, "t2", [32, BATCH, 32])
        M.e_end = sbuf(nc, tmp, "e_end", [CH, BATCH, 1])
        M.eall_end = sbuf(nc, tmp, "eall_end", [32, BATCH, 1])
        with nc.Fori(0, NCH) as c:
            memory_chunk(nc, K, M, c)
    with nc.Fori(0, BATCH) as b:
        memory_output(nc, K, M, b, out)




def lay_out(i):
    c = np.ascontiguousarray
    t = {}
    j = lambda *n: np.concatenate([np.asarray(i[k]) for k in n], axis=0)
    col = lambda v: c(np.asarray(v).reshape(-1, P).T)
    tiles = lambda w: c(np.asarray(w).reshape(-1, P, w.shape[-1]).transpose(1, 0, 2))
    T_ = lambda n: c(np.asarray(i[n]).T)
    t["x"] = c(np.asarray(i["L0_attn_x"]))
    t["w0_qkv"] = c(j("L0_attn_wq_w", "L0_attn_wk_w", "L0_attn_wv_w").T)
    t["b0_qkv"] = j("L0_attn_wq_b", "L0_attn_wk_b", "L0_attn_wv_b")
    t["w0_1"], t["w0_2"] = T_("L0_ffn_w1_w"), T_("L0_ffn_w2_w")
    t["w0_h1"], t["w0_h2"], t["w0_3"] = tiles(T_("L0_ffn_h1_w")), tiles(T_("L0_ffn_h2_w")), tiles(T_("L0_ffn_w3_w"))
    t["s0_1"], t["s0_2"] = col(i["L0_ffn_w1_s"]), col(i["L0_ffn_w2_s"])
    t["s0_h1"], t["s0_h2"] = col(i["L0_ffn_h1_s"]), col(i["L0_ffn_h2_s"])
    t["s0_3"] = c(i["L0_ffn_w3_s"])
    t["w1_q"], t["w1_k"], t["w1_v"], t["w1_o"] = [T_("L1_attn_W" + n) for n in "qkvo"]
    t["w_gate"], t["w_up"], t["w_downr"] = c(i["L1_ffn_w_gate"]), c(i["L1_ffn_w_up"]), c(i["L1_ffn_w_down"])
    t["w2_q"], t["w2_k"], t["w2_v"], t["w2_ao"] = [T_("L2_attn_W" + n) for n in "qkvo"]
    t["b2_q"], t["b2_k"] = col(i["L2_attn_bq"]), col(i["L2_attn_bk"])
    t["b2_v"], t["b2_ao"], t["rmsw"] = c(i["L2_attn_bv"]), c(i["L2_attn_bo"]), c(i["L2_attn_norm_w"])
    half = LD // 2
    sc = []
    for L in range(2):
        t[f"w2_qkv{L}"] = c(i["L2_ffn_wqkv"][L])
        t[f"w2_o{L}"] = tiles(c(i["L2_ffn_wo"][L]))
        t[f"w2_up{L}"] = c(i["L2_ffn_w1"][L])
        t[f"w2_down{L}"] = c(i["L2_ffn_w2"][L])
        b1 = np.asarray(i["L2_ffn_b1"][L])
        up = np.zeros((6, P), b1.dtype)
        for m in range(2):
            up[3 * m:3 * m + 3].reshape(-1)[:HID2] = b1[m * HID2:(m + 1) * HID2]
        t[f"b2_up{L}"] = c(up.T)
        t[f"b2_down{L}"] = c(i["L2_ffn_b2"][L])
        t[f"ln2_g{L}"], t[f"ln2_b{L}"] = col(i["L2_ffn_ln_g"][L]), col(i["L2_ffn_ln_b"][L])
        q, k = np.asarray(i["L2_ffn_q_scale"][L]), np.asarray(i["L2_ffn_k_scale"][L])
        sc.append(np.stack([q, np.concatenate([q[half:], q[:half]]), k, np.concatenate([k[half:], k[:half]])]))
    t["qk_scales"] = c(np.stack(sc))
    t["w3_up"] = c(np.asarray(i["L3_ffn_w12"]).transpose(2, 0, 1))
    t["w3_down"] = c(np.asarray(i["L3_ffn_w3"]).transpose(2, 0, 1).reshape(2, P, E3, D).transpose(1, 2, 0, 3))
    t["w3_gate"] = T_("L3_ffn_gate_w")
    t["w3_kvq"] = c(j("L3_attn_Wk", "L3_attn_Wv", "L3_attn_Wq").T)
    t["w3_aet"] = c(j("L3_attn_aW", "L3_attn_eW", "L3_attn_tW").T)
    t["w3_g"] = T_("L3_attn_gW")
    t["g3_b"], t["norm3"] = c(i["L3_attn_gb"]), c(i["L3_attn_norm_g"])
    t["conv_w"] = j("L3_attn_ckw", "L3_attn_cvw", "L3_attn_cqw")
    t["conv_b"] = j("L3_attn_ckb", "L3_attn_cvb", "L3_attn_cqb").reshape(96, 1)
    t["b3_aet"] = j("L3_attn_ab", "L3_attn_eb", "L3_attn_tb").reshape(96, 1)
    t["w3_o"] = T_("L3_attn_Wo")
    w1, w2 = np.asarray(i["L3_attn_mW1"]), np.asarray(i["L3_attn_mW2"])
    t["mem_w"] = c(np.stack([w1.T, w2.T, w2], axis=1))
    return t




def kernel(**inputs):
    import concourse.bacc as _bacc
    from concourse.bass_utils import run_bass_kernel_spmd as _run

    nc = _bacc.Bacc("TRN2", target_bir_lowering=False, num_devices=1)
    arrays = {f"in_{n}": np.ascontiguousarray(a) for n, a in lay_out(inputs).items()}
    A = {n[3:]: nc.dram_tensor(n, a.shape, mybir.dt.from_np(a.dtype), kind="ExternalInput").ap()
         for n, a in arrays.items()}
    out = nc.dram_tensor("out_0", (BATCH, T, D), F32, kind="ExternalOutput").ap()
    build_kernel(nc, A, out)
    r = _run(nc, [arrays], core_ids=[0])
    return r.results[0]["out_0"]
```

```python
from contextlib import ExitStack

import numpy as np

import concourse.bass as bass
from concourse import mybir

F32 = mybir.dt.float32
BF16 = mybir.dt.bfloat16
U32 = mybir.dt.uint32
ALU = mybir.AluOpType
ACT = mybir.ActivationFunctionType
AX = mybir.AxisListType

P = 128
BATCH, T, D = 8, 512, 128
NT = T // P
H, HD = 16, 8
NG = H // 4
EPS_LN = 1e-5
NEG = -1.0e30
HID0 = 512
I1, BLK = 352, 16
INNER, LH, LD, WIN, HID2 = 512, 8, 64, 64, 341
DM, CH = 32, 64
E3, H3 = 8, 256
NCH = T // CH
POOL = 38


class Chain:

    def __init__(self, eng, sem):
        self.eng, self.sem, self.n = eng, sem, 0

    def tick(self, ins):
        self.n += 1
        ins.then_inc(self.sem, 1)

    def wait(self):
        if self.n:
            self.eng.wait_ge(self.sem, self.n)

    def do(self, ins):
        self.tick(ins)
        self.wait()


class Kit:

    def __init__(self, nc, ctx):
        self.nc = nc
        self.pool = [ctx.enter_context(nc.semaphore(f"sig{i}")) for i in range(POOL)]
        self.saved = ctx.enter_context(nc.semaphore("parts_saved"))
        self.spread = ctx.enter_context(nc.semaphore("parts_spread"))
        first = self.pool[0].num
        assert [s.num for s in self.pool + [self.saved, self.spread]] == list(range(first, first + POOL + 2))

    def clear(self, spread=False):
        first = self.pool[0].num
        self.nc.vector.sem_clear(range(first, first + (POOL + 2 if spread else POOL)))
        self.nc.all_engine_barrier()


NAMED = {}


def sbuf(nc, ctx, name, shape, dt=F32):
    NAMED[name] = NAMED.get(name, 0) + 1
    if NAMED[name] > 1:
        name = f"{name}_{NAMED[name]}"
    return ctx.enter_context(nc.sbuf_tensor(name, shape, dt))




def load_constants(nc, K, loads):
    landed = K.pool[0]
    with nc.Block() as block:
        @block.sync
        def _(sp):
            for dst, src in loads[0::2]:
                sp.dma_start(dst, src).then_inc(landed, 16)
            sp.wait_ge(landed, 16 * len(loads))

        @block.scalar
        def _(act):
            for dst, src in loads[1::2]:
                act.dma_start(dst, src).then_inc(landed, 16)
    K.clear()


def fp4_blocks(nc, ch, V, Q, a, acc, sc, rs, npart, n):
    nb = n // BLK
    v = V.rearrange("p (b k) -> p b k", k=BLK)
    q = Q.rearrange("p (b k) -> p b k", k=BLK)
    A = a[0:npart, 0:n]
    C = acc[0:npart, 0:n]
    s, r = sc[0:npart, 0:nb], rs[0:npart, 0:nb]
    ch.do(nc.vector.tensor_reduce(s, v, AX.X, ALU.max, apply_absolute_value=True))
    yield
    ch.do(nc.vector.tensor_scalar(s, s, 1.0 / 6.0, 1e-12, ALU.mult, ALU.max))
    yield
    ch.do(nc.vector.reciprocal(r, s))
    yield
    ch.do(nc.vector.tensor_tensor(A.rearrange("p (b k) -> p b k", k=BLK), v,
                                  r.unsqueeze(2).to_broadcast([npart, nb, BLK]), ALU.mult))
    yield
    ch.do(nc.vector.scalar_tensor_tensor(A, A, -1.0, A, ALU.mult, ALU.max))
    yield
    ch.do(nc.vector.tensor_scalar(C, A, 5.0, 2.0, ALU.is_gt, ALU.mult))
    yield
    ch.do(nc.vector.scalar_tensor_tensor(C, A, 3.5, C, ALU.is_gt, ALU.add))
    yield
    ch.do(nc.vector.scalar_tensor_tensor(C, A, 2.5, C, ALU.is_gt, ALU.add))
    yield
    ch.do(nc.vector.tensor_scalar(C, C, 2.0, None, ALU.mult))
    yield
    for mid in (1.75, 1.25, 0.75, 0.25):
        ch.do(nc.vector.scalar_tensor_tensor(C, A, mid, C, ALU.is_gt, ALU.add))
        yield
    ch.do(nc.vector.tensor_scalar(A, V, 0.0, 2.0, ALU.is_ge, ALU.mult))
    yield
    ch.do(nc.vector.scalar_tensor_tensor(A, A, 1.0, C, ALU.subtract, ALU.mult))
    yield
    ch.do(nc.vector.tensor_scalar(s, s, 0.5, None, ALU.mult))
    yield
    ch.do(nc.vector.tensor_tensor(q, A.rearrange("p (b k) -> p b k", k=BLK),
                                  s.unsqueeze(2).to_broadcast([npart, nb, BLK]), ALU.mult))
    yield


def quantize_weights(nc, K, ctx):
    with ExitStack() as tmp:
        q = sbuf(nc, tmp, "wq4", [P, 7, I1])
        scr = fp4_scratch(nc, tmp, I1)
        vec, quantized, turned, copied = K.pool[0:4]
        jobs = []
        for m, w in enumerate((K.gate_rows, K.up_rows)):
            for c in range(3):
                n = min(P, I1 - c * P)
                jobs.append((n, w[0:n, c, :], q[0:n, 3 * m + c, 0:D], D))
        jobs.append((P, K.down_rows[:, :], q[:, 6, :], I1))
        turns = []
        for m in range(2):
            for c in range(3):
                n = min(P, I1 - c * P)
                turns.append((q[0:n, 3 * m + c, 0:D], n, K.ps[:, m, c * P:c * P + n],
                              K.w_gu[:, m * I1 + c * P:m * I1 + c * P + n]))
        for c in range(3):
            n = min(P, I1 - c * P)
            turns.append((q[:, 6, c * P:c * P + n], P, K.ps[0:n, 2 + c, 0:P], K.w_down[0:n, c, :]))
        with nc.Block() as block:
            @block.vector
            def _(dve):
                ch = Chain(dve, vec)
                for npart, V, Q, n in jobs:
                    for _ in fp4_blocks(nc, ch, V, Q, *scr, npart, n):
                        pass
                nc.vector.engine_nop().then_inc(quantized, 1)
                dve.wait_ge(turned, len(turns))
                for _, _, ps, dst in turns:
                    nc.vector.tensor_copy(dst, ps).then_inc(copied, 1)

            @block.tensor
            def _(pe):
                pe.wait_ge(quantized, 1)
                for src, n, ps, _ in turns:
                    nc.tensor.transpose(ps, src, K.ident[0:n, 0:n]).then_inc(turned, 1)
        K.clear()


def fp4_scratch(nc, ctx, n, values=None):
    values = sbuf(nc, ctx, "fp4_abs", [P, n]) if values is None else values
    return (values, sbuf(nc, ctx, "fp4_steps", [P, n], BF16),
            sbuf(nc, ctx, "fp4_scale", [P, n // BLK]), sbuf(nc, ctx, "fp4_rscale", [P, n // BLK]))




def layer_norm(nc, K, load=None):
    loaded, vec, var_ready, rstd_ready, xn_ready, turned, evac = K.pool[0:7]
    with nc.Block() as block:
        if load is not None:
            @block.sync
            def _(sp):
                sp.dma_start(K.x[:, :, :], load).then_inc(loaded, 16)

        @block.vector
        def _(dve):
            ch = Chain(dve, vec)
            if load is not None:
                dve.wait_ge(loaded, 16)
            for t in range(NT):
                ch.tick(nc.vector.bn_stats(K.stats[:, t, :], K.x[:, t, :]))
            ch.wait()
            for t in range(NT):
                ch.tick(nc.vector.bn_aggr(K.mv[:, t, :], K.stats[:, t, :]))
            ch.wait()
            nc.vector.tensor_scalar(K.var[:, 0:NT], K.mv[:, :, 1], EPS_LN, None,
                                    ALU.add).then_inc(var_ready, 1)
            dve.wait_ge(rstd_ready, 1)
            for t in range(NT):
                nc.vector.tensor_scalar(K.xn[:, t, :], K.x[:, t, :], K.mv[:, t, 0:1], K.rstd[:, t:t + 1],
                                        ALU.subtract, ALU.mult).then_inc(xn_ready, 1)

        @block.gpsimd
        def _(pool):
            pool.wait_ge(var_ready, 1)
            nc.gpsimd.tensor_tensor(K.rstd[:, 0:NT], K.var[:, 0:NT], K.neghalf[:, 0:NT],
                                    ALU.pow).then_inc(rstd_ready, 1)

        @block.tensor
        def _(pe):
            for t in range(NT):
                pe.wait_ge(xn_ready, t + 1)
                nc.tensor.transpose(K.ps[:, 0, t * P:(t + 1) * P], K.xn[:, t, :], K.ident[:, :]).then_inc(turned, 1)

        @block.scalar
        def _(act):
            act.wait_ge(turned, NT)
            nc.scalar.activation(K.xnT[:, :], K.ps[:, 0, :], ACT.Identity).then_inc(evac, 1)
    K.clear()




def prepare(nc, K, layer, load=None):
    (loaded, vec, var_ready, rstd_ready, xn_ready, turned, xnT_ready, xr_ready, xr_turned, xrT_ready, projected,
     rotated, qk_turned, first, left, parts_ready, rvar_ready, rrstd_ready) = K.pool[0:18]
    rope, rms = layer == 0, layer == 2
    bq = K.b2_q[:, 0:1] if rms else None
    bk = K.b2_k[:, 0:1] if rms else None
    with ExitStack() as tmp:
        qk = sbuf(nc, tmp, "qk", [P, NT, 2 * D]) if rope else None
        part = sbuf(nc, tmp, "qk_sin", [P, NT, 2 * D]) if rope else None
        rest = sbuf(nc, tmp, "rest", [P, 2, T])
        parts = K.parts
        srcT = K.xrT if rms else K.xnT
        with nc.Block() as block:
            @block.sync
            def _(sp):
                if load is not None:
                    sp.dma_start(K.x[:, :, :], load).then_inc(loaded, 16)
                for m in range(2):
                    sp.wait_ge(parts_ready, m + 1)
                    sp.dma_start(K.parts_d[m].rearrange("i (h d) t -> (h d) i t", d=HD),
                                 parts[:, m, :, :]).then_inc(K.saved, 16)

            @block.vector
            def _(dve):
                ch = Chain(dve, vec)
                if load is not None:
                    dve.wait_ge(loaded, 16)

                def statistics(src):
                    for t in range(NT):
                        ch.tick(nc.vector.bn_stats(K.stats[:, t, :], src[:, t, :]))
                    ch.wait()
                    for t in range(NT):
                        ch.tick(nc.vector.bn_aggr(K.mv[:, t, :], K.stats[:, t, :]))
                    ch.wait()

                statistics(K.x)
                nc.vector.tensor_scalar(K.var[:, 0:NT], K.mv[:, :, 1], EPS_LN, None,
                                        ALU.add).then_inc(var_ready, 1)
                dve.wait_ge(rstd_ready, 1)
                for t in range(NT):
                    nc.vector.tensor_scalar(K.xn[:, t, :], K.x[:, t, :], K.mv[:, t, 0:1], K.rstd[:, t:t + 1],
                                            ALU.subtract, ALU.mult).then_inc(xn_ready, 1)
                if rms:
                    dve.wait_ge(xn_ready, NT)
                    statistics(K.xn)
                    ch.do(nc.vector.tensor_tensor(K.var[:, 0:NT], K.mv[:, :, 0], K.mv[:, :, 0], ALU.mult))
                    nc.vector.scalar_tensor_tensor(K.var[:, 0:NT], K.mv[:, :, 1], 1e-6, K.var[:, 0:NT],
                                                   ALU.add, ALU.add).then_inc(rvar_ready, 1)
                    dve.wait_ge(rrstd_ready, 1)
                    for t in range(NT):
                        nc.vector.scalar_tensor_tensor(K.xr[:, t, :], K.xn[:, t, :], K.rstd[:, t:t + 1],
                                                       K.rmsw[:, :], ALU.mult, ALU.mult).then_inc(xr_ready, 1)
                if rope:
                    heads = lambda a: a.rearrange("p (h d) -> p h d", d=HD)
                    dve.wait_ge(projected, NT)
                    for t in range(NT):
                        ch.tick(nc.vector.tensor_tensor(qk[:, t, :], K.ps[:, t, 0:2 * D], K.b0_qkv[:, 0:2 * D],
                                                        ALU.add))
                        ch.tick(nc.vector.tensor_tensor(K.v32[:, t, :, 0:HD], heads(K.ps[:, t, 2 * D:3 * D]),
                                                        heads(K.b0_qkv[:, 2 * D:3 * D]), ALU.add))
                    ch.wait()
                    for t in range(NT):
                        x4 = qk[:, t, :].rearrange("p (g i two) -> p g i two", two=2, i=HD // 2)
                        y4 = part[:, t, :].rearrange("p (g i two) -> p g i two", two=2, i=HD // 2)
                        for e in range(2):
                            sin = K.rope_sin[:, t, e, :].unsqueeze(1).to_broadcast([P, 2 * H, HD // 2])
                            ch.tick(nc.vector.tensor_tensor(y4[:, :, :, e], x4[:, :, :, 1 - e], sin, ALU.mult))
                    ch.wait()
                    for t in range(NT):
                        cos = K.rope_cos[:, t, :].unsqueeze(1).to_broadcast([P, 2 * H, HD])
                        ch.tick(nc.vector.tensor_tensor(heads(qk[:, t, :]), heads(qk[:, t, :]), cos, ALU.mult))
                    ch.wait()
                    nc.vector.tensor_tensor(qk[:, :, :], qk[:, :, :], part[:, :, :], ALU.add).then_inc(rotated, 1)
                else:
                    dve.wait_ge(projected, 3)
                    v = K.ps[:, 2, :].rearrange("p (t h d) -> p t h d", t=NT, d=HD)
                    if rms:
                        for t in range(NT):
                            nc.vector.tensor_tensor(K.v32[:, t, :, 0:HD], v[:, t, :, :],
                                                    K.b2_v[:, :].rearrange("p (h d) -> p h d", d=HD), ALU.add)
                    else:
                        nc.vector.tensor_copy(K.v32[:, :, :, 0:HD], v)
                for m, b in enumerate((bq, bk)):
                    dve.wait_ge(first, m + 1)
                    nc.vector.scalar_tensor_tensor(rest[:, m, :], K.ps[:, 4 + m, :], 0.0 if b is None else b,
                                                   parts[:, m, 0, :], ALU.add, ALU.subtract).then_inc(left, 1)
                for m in range(2):
                    dve.wait_ge(first, 3 + m)
                    nc.vector.tensor_tensor(parts[:, m, 2, :], rest[:, m, :], parts[:, m, 1, :],
                                            ALU.subtract).then_inc(parts_ready, 1)

            @block.gpsimd
            def _(pool):
                pool.wait_ge(var_ready, 1)
                nc.gpsimd.tensor_tensor(K.rstd[:, 0:NT], K.var[:, 0:NT], K.neghalf[:, 0:NT],
                                        ALU.pow).then_inc(rstd_ready, 1)
                if rms:
                    pool.wait_ge(rvar_ready, 1)
                    nc.gpsimd.tensor_tensor(K.rstd[:, 0:NT], K.var[:, 0:NT], K.neghalf[:, 0:NT],
                                            ALU.pow).then_inc(rrstd_ready, 1)

            @block.tensor
            def _(pe):
                for t in range(NT):
                    pe.wait_ge(xn_ready, t + 1)
                    nc.tensor.transpose(K.ps[:, 6, t * P:(t + 1) * P], K.xn[:, t, :], K.ident[:, :]).then_inc(turned, 1)
                if rms:
                    for t in range(NT):
                        pe.wait_ge(xr_ready, t + 1)
                        nc.tensor.transpose(K.ps[:, 7, t * P:(t + 1) * P], K.xr[:, t, :],
                                            K.ident[:, :]).then_inc(xr_turned, 1)
                    pe.wait_ge(xrT_ready, 1)
                else:
                    pe.wait_ge(xnT_ready, 1)
                if rope:
                    for t in range(NT):
                        nc.tensor.matmul(K.ps[:, t, 0:3 * D], srcT[:, t * P:(t + 1) * P], K.w0_qkv[:, :],
                                         start=True, stop=True).then_inc(projected, 1)
                    pe.wait_ge(rotated, 1)
                    for m in range(2):
                        for t in range(NT):
                            mm = nc.tensor.transpose(K.ps[:, 4 + m, t * P:(t + 1) * P], qk[:, t, m * D:(m + 1) * D],
                                                     K.ident[:, :])
                        mm.then_inc(qk_turned, 1)
                else:
                    wq, wk, wv = (K.w2_q, K.w2_k, K.w2_v) if rms else (K.w1_q, K.w1_k, K.w1_v)
                    nc.tensor.matmul(K.ps[:, 4, :], wq[:, :], srcT[:, :], start=True, stop=True).then_inc(projected, 1)
                    nc.tensor.matmul(K.ps[:, 5, :], wk[:, :], srcT[:, :], start=True, stop=True).then_inc(projected, 1)
                    for t in range(NT):
                        mm = nc.tensor.matmul(K.ps[:, 2, t * P:(t + 1) * P], srcT[:, t * P:(t + 1) * P], wv[:, :],
                                              start=True, stop=True)
                    mm.then_inc(projected, 1)

            @block.scalar
            def _(act):
                act.wait_ge(turned, NT)
                nc.scalar.activation(K.xnT[:, :], K.ps[:, 6, :], ACT.Identity).then_inc(xnT_ready, 1)
                if rms:
                    act.wait_ge(xr_turned, NT)
                    nc.scalar.activation(K.xrT[:, :], K.ps[:, 7, :], ACT.Identity).then_inc(xrT_ready, 1)
                for m, b in enumerate((bq, bk)):
                    act.wait_ge(qk_turned if rope else projected, m + 1)
                    nc.scalar.activation(parts[:, m, 0, :], K.ps[:, 4 + m, :], ACT.Identity,
                                         bias=0.0 if b is None else b).then_inc(first, 1)
                for m in range(2):
                    act.wait_ge(left, m + 1)
                    nc.scalar.activation(parts[:, m, 1, :], rest[:, m, :], ACT.Identity).then_inc(first, 1)
        K.clear()


def spread_loads(nc, K, sp):
    sp.dma_start(K.ks[72:74, :, :], K.ones_d).then_inc(K.spread, 16)
    sp.wait_ge(K.saved, 32)
    for i in range(3):
        for j in range(3):
            r = 24 * i + 8 * j
            sp.dma_start(K.qs[r:r + HD, :, :],
                         K.parts_d[0, i].rearrange("(h d) t -> d h t", d=HD)).then_inc(K.spread, 16)
            sp.dma_start(K.ks[r:r + HD, :, :],
                         K.parts_d[1, j].rearrange("(h d) t -> d h t", d=HD)).then_inc(K.spread, 16)


class Beside:

    BEFORE = 0

    def tensor(self, pe):
        return iter(())

    scalar = vector = gpsimd = tensor


def run_beside(work, due, step):
    while due <= step:
        due = next(work, 1 << 30)
    return due


def run_alone(nc, K, work):
    with nc.Block() as block:
        @block.tensor
        def _(pe):
            run_beside(work.tensor(pe), -work.BEFORE, 1 << 20)

        @block.scalar
        def _(act):
            run_beside(work.scalar(act), -work.BEFORE, 1 << 20)

        @block.vector
        def _(dve):
            run_beside(work.vector(dve), -work.BEFORE, 1 << 20)

        @block.gpsimd
        def _(pool):
            run_beside(work.gpsimd(pool), -work.BEFORE, 1 << 20)
    K.clear()


def attention(nc, K, causal, wo=None, bo=None, combine=True, beside=None):
    (scored, reduced, turned, hi_ready, lo_ready, saved, rows, scored2, exped, weighed, oT_ready, oturned, vec,
     att_ready, att_turned, attT_ready, projected) = K.pool[0:17]
    QUADS, LAG, KR = 3, 13, 74
    STEPS = 8 * NG + LAG + 5
    beside = beside or Beside()
    scale = float(1.0 / np.sqrt(HD))

    def at_step(s):
        first = [2 * s, 2 * s + 1] if 0 <= s < 8 * NG else []
        maxima = [g for g in range(NG) if s == 8 * (g + 1)]
        a = s - LAG
        second = [2 * a, 2 * a + 1] if 0 <= a < 8 * NG else []
        weigh = [q for q in range(4 * NG) if a == 2 * q + 2]
        back = [g for g in range(NG) if a == 8 * g + 10]
        return first, maxima, second, weigh, back

    def first_bank(n):
        return (n // 16 * 17 + n % 16) % 2

    def maxima_bank(g):
        return (17 * g + 16) % 2

    with ExitStack() as tmp:
        nmax = sbuf(nc, tmp, "nmax", [P, NT, H])
        mparts = sbuf(nc, tmp, "max_parts", [4, 2, 2, T], BF16)
        probs = sbuf(nc, tmp, "probs", [P, 4 * QUADS, T])
        oT = sbuf(nc, tmp, "oT", [P, 2, T])
        rden = sbuf(nc, tmp, "rden", [P, NT, 4])
        with nc.Block() as block:
            @block.tensor
            def _(pe):
                work = beside.tensor(pe)
                due = run_beside(work, -beside.BEFORE, -1)
                pe.wait_ge(K.spread, 19 * 16)
                for s in range(STEPS):
                    first, maxima, second, weigh, back = at_step(s)
                    for g in maxima:
                        pe.wait_ge(reduced, 16 * (g + 1))
                        for t in range(NT):
                            mm = nc.tensor.transpose(K.ps[0:4, maxima_bank(g), t * P:(t + 1) * P],
                                                     nmax[:, t, 4 * g:4 * g + 4], K.ident[:, :])
                        mm.then_inc(turned, 1)
                    for n in first:
                        g, (j, t) = n // 16, divmod(n % 16, NT)
                        h, b = 4 * g + j, first_bank(n)
                        if g and n % 16 < 2:
                            if n % 16 == 0:
                                pe.wait_ge(reduced, n)
                            else:
                                pe.wait_ge(lo_ready, g)
                        elif n >= 2:
                            pe.wait_ge(reduced, n - 1)
                        keys = (t + 1) * P if causal else T
                        mm = nc.tensor.matmul(K.ps[:, b, 0:keys], K.qs[0:72, h, t * P:(t + 1) * P],
                                              K.ks[0:72, h, 0:keys], start=True, stop=not causal)
                        if causal:
                            mm = nc.tensor.matmul(K.ps[:, b, keys - P:keys], K.identb[:, :], K.mask_q[:, :],
                                                  start=False, stop=True)
                        mm.then_inc(scored, 1)
                    for g in back:
                        pe.wait_ge(oT_ready, g + 1)
                        for t in range(NT):
                            mm = nc.tensor.transpose(K.ps[:, 5, t * P:(t + 1) * P], oT[:, g % 2, t * P:(t + 1) * P],
                                                     K.ident[:, :])
                        mm.then_inc(oturned, 1)
                    for m in second:
                        g, (k, j) = m // 16, divmod(m % 16, 4)
                        h, b = 4 * g + j, 2 + m % 3
                        if m % 16 == 0:
                            pe.wait_ge(rows, 16 * (g + 1))
                        if m >= 3:
                            pe.wait_ge(exped, m - 2)
                        q0 = k * P if causal else 0
                        mm = nc.tensor.matmul(K.ps[:, b, q0:T], K.ks[0:KR, h, k * P:(k + 1) * P],
                                              K.qs[0:KR, h, q0:T], start=True, stop=not causal)
                        if causal:
                            mm = nc.tensor.matmul(K.ps[:, b, q0:q0 + P], K.identb[:, :], K.mask_k[:, :],
                                                  start=False, stop=True)
                        mm.then_inc(scored2, 1)
                    for q in weigh:
                        g, k = divmod(q, NT)
                        pe.wait_ge(exped, 4 * (q + 1))
                        if g and k == 0:
                            pe.wait_ge(att_ready, g)
                        q0 = k * P if causal else 0
                        for j in range(4):
                            mm = nc.tensor.matmul(K.ps[32 * j:32 * j + 32, 5, q0:T], K.v32[:, k, 4 * g + j, :],
                                                  probs[:, 4 * (q % QUADS) + j, q0:T], start=(k == 0),
                                                  stop=(k == NT - 1), tile_position=(0, 32 * j))
                        mm.then_inc(weighed, 1)
                    due = run_beside(work, due, s)
                run_beside(work, due, 1 << 20)
                if wo is not None:
                    pe.wait_ge(att_ready, NG)
                    for t in range(NT):
                        mm = nc.tensor.transpose(K.ps[:, 0, t * P:(t + 1) * P], K.att[:, t, :], K.ident[:, :])
                    mm.then_inc(att_turned, 1)
                    pe.wait_ge(attT_ready, 1)
                    for t in range(NT):
                        mm = nc.tensor.matmul(K.ps[:, 1, t * P:(t + 1) * P], oT[:, 0, t * P:(t + 1) * P], wo[:, :],
                                              start=True, stop=True)
                    mm.then_inc(projected, 1)

            @block.scalar
            def _(act):
                work, due = beside.scalar(act), -beside.BEFORE
                for s in range(-beside.BEFORE, STEPS):
                    _, maxima, second, weigh, _ = at_step(s)
                    for g in maxima:
                        act.wait_ge(turned, g + 1)
                        if g >= 2:
                            act.wait_ge(saved, 16 * (g - 1))
                        nc.scalar.activation(mparts[:, g % 2, 0, :], K.ps[0:4, maxima_bank(g), :],
                                             ACT.Identity).then_inc(hi_ready, 1)
                    for m in second:
                        k = m % 16 // 4
                        q = m // 4
                        if q >= QUADS:
                            act.wait_ge(weighed, q - QUADS + 1)
                        act.wait_ge(scored2, m + 1)
                        q0 = k * P if causal else 0
                        nc.scalar.activation(probs[:, 4 * (q % QUADS) + m % 4, q0:T], K.ps[:, 2 + m % 3, q0:T],
                                             ACT.Exp, scale=scale).then_inc(exped, 1)
                    for q in weigh:
                        g, k = divmod(q, NT)
                        if k == NT - 1:
                            act.wait_ge(weighed, q + 1)
                            if g >= 2:
                                act.wait_ge(oturned, g - 1)
                            nc.scalar.activation(oT[:, g % 2, :], K.ps[:, 5, :], ACT.Identity).then_inc(oT_ready, 1)
                    due = run_beside(work, due, s)
                run_beside(work, due, 1 << 20)
                if wo is not None:
                    act.wait_ge(att_turned, 1)
                    act.wait_ge(oturned, NG)
                    nc.scalar.activation(oT[:, 0, :], K.ps[:, 0, :], ACT.Identity).then_inc(attT_ready, 1)

            @block.sync
            def _(sp):
                spread_loads(nc, K, sp)
                for g in range(NG):
                    sp.wait_ge(hi_ready, g + 1)
                    sp.wait_ge(lo_ready, g + 1)
                    sp.dma_start(K.nmax_d[:, 4 * g:4 * g + 4, :].rearrange("i h t -> h i t"),
                                 mparts[:, g % 2, :, :]).then_inc(saved, 16)
                    sp.wait_ge(saved, 16 * (g + 1))
                    sp.dma_start(K.qs[72:74, 4 * g:4 * g + 4, :], K.nmax_d[:, 4 * g:4 * g + 4, :]).then_inc(rows, 16)
                    sp.wait_ge(rows, 16 * (g + 1))

            @block.gpsimd
            def _(pool):
                run_beside(beside.gpsimd(pool), -beside.BEFORE, 1 << 20)

            @block.vector
            def _(dve):
                ch = Chain(dve, vec)
                work, due = beside.vector(dve), -beside.BEFORE
                for s in range(-beside.BEFORE, STEPS):
                    first, maxima, _, _, back = at_step(s)
                    for g in maxima:
                        dve.wait_ge(hi_ready, g + 1)
                        nc.vector.tensor_tensor(mparts[:, g % 2, 1, :], K.ps[0:4, maxima_bank(g), :],
                                                mparts[:, g % 2, 0, :], ALU.subtract).then_inc(lo_ready, 1)
                    for n in first:
                        g, (j, t) = n // 16, divmod(n % 16, NT)
                        h = 4 * g + j
                        dve.wait_ge(scored, n + 1)
                        keys = (t + 1) * P if causal else T
                        nc.vector.tensor_reduce(nmax[:, t, h:h + 1], K.ps[:, first_bank(n), 0:keys], AX.X, ALU.max,
                                                negate=True).then_inc(reduced, 1)
                    for g in back:
                        dve.wait_ge(oturned, g + 1)
                        o = K.ps[:, 5, :].rearrange("p (t j d) -> p t j d", t=NT, j=4)
                        ch.do(nc.vector.reciprocal(rden[:, :, :], o[:, :, :, HD]))
                        for t in range(NT):
                            mul = nc.vector.tensor_tensor(
                                K.att[:, t, g * 32:(g + 1) * 32].rearrange("p (j d) -> p j d", d=HD),
                                o[:, t, :, 0:HD], rden[:, t, :].unsqueeze(2).to_broadcast([P, 4, HD]), ALU.mult)
                            if t < NT - 1:
                                ch.tick(mul)
                            else:
                                mul.then_inc(att_ready, 1)
                        ch.wait()
                        dve.wait_ge(att_ready, g + 1)
                    due = run_beside(work, due, s)
                run_beside(work, due, 1 << 20)
                if wo is not None:
                    dve.wait_ge(projected, 1)
                    o = K.ps[:, 1, :].rearrange("p (t d) -> p t d", t=NT)
                    ch.do(nc.vector.tensor_copy(K.att[:, :, :], o))
                if bo is not None:
                    ch.do(nc.vector.tensor_tensor(K.att[:, :, :], K.att[:, :, :],
                                                  bo[:, :].unsqueeze(1).to_broadcast([P, NT, D]), ALU.add))
                    nc.vector.tensor_tensor(K.att[:, :, :], K.att[:, :, :], K.xr[:, :, :], ALU.add)
                if combine:
                    dve.wait_ge(beside.g_ready, 1)
                    ch.do(nc.vector.tensor_tensor(K.att[:, :, :], K.att[:, :, :], K.g[:, :, :], ALU.mult))
                    nc.vector.tensor_tensor(K.x[:, :, :], K.x[:, :, :], K.att[:, :, :], ALU.add)
        K.clear(spread=True)




class TernaryFfn(Beside):

    BEFORE = 4

    def __init__(self, nc, K, ctx):
        self.nc, self.K = nc, K
        (self.gate_up, self.silu_done, self.h_ready, self.hid, self.gelu_done, self.out_done, self.g_in,
         self.g_ready) = K.pool[24:32]
        self.a = sbuf(nc, ctx, "silu_a", [P, 2, T])
        self.h = sbuf(nc, ctx, "hid_a", [P, 4, T])
        self.g = sbuf(nc, ctx, "hid_b", [P, 4, T])

    @staticmethod
    def hidden_step(n):
        return 4 * n + n // 4

    OUT_STEP = 35

    def tensor(self, pe):
        nc, K = self.nc, self.K
        for c in range(4):
            yield c - 4
            if c:
                pe.wait_ge(self.h_ready, c)
            nc.tensor.matmul(K.ps[:, 6, :], K.w0_1[:, c * P:(c + 1) * P], K.xnT[:, :], start=True, stop=True)
            nc.tensor.matmul(K.ps[:, 7, :], K.w0_2[:, c * P:(c + 1) * P], K.xnT[:, :],
                             start=True, stop=True).then_inc(self.gate_up, 1)
        for layer, (w, src) in enumerate(((K.w0_h1, self.h), (K.w0_h2, self.g))):
            for c in range(4):
                n = 4 * layer + c
                for k in range(4):
                    yield self.hidden_step(n) + k
                    if n == 0 and k == 0:
                        pe.wait_ge(self.h_ready, 4)
                    if c == 0 and k == 0 and layer:
                        pe.wait_ge(self.gelu_done, 4)
                    elif k == 0 and n >= 2:
                        pe.wait_ge(self.gelu_done, n - 1)
                    mm = nc.tensor.matmul(K.ps[:, 6 + n % 2, :], w[:, k, c * P:(c + 1) * P], src[:, k, :],
                                          start=(k == 0), stop=(k == 3))
                mm.then_inc(self.hid, 1)
        for t in range(NT):
            yield self.OUT_STEP + t
            if t == 0:
                pe.wait_ge(self.gelu_done, 8)
            for k in range(4):
                mm = nc.tensor.matmul(K.ps[:, 6, t * P:(t + 1) * P], self.h[:, k, t * P:(t + 1) * P],
                                      K.w0_3[:, k, :], start=(k == 0), stop=(k == 3))
        mm.then_inc(self.out_done, 1)

    def scalar(self, act):
        nc, K = self.nc, self.K
        for c in range(4):
            yield c - 4
            act.wait_ge(self.gate_up, c + 1)
            if c >= 2:
                act.wait_ge(self.h_ready, c - 1)
            nc.scalar.activation(self.a[:, c % 2, :], K.ps[:, 6, :], ACT.Silu,
                                 scale=K.s0_1[:, c:c + 1]).then_inc(self.silu_done, 1)
        for layer, (s, dst) in enumerate(((K.s0_h1, self.g), (K.s0_h2, self.h))):
            for c in range(4):
                n = 4 * layer + c
                yield self.hidden_step(n) + 3
                act.wait_ge(self.hid, n + 1)
                nc.scalar.activation(dst[:, c, :], K.ps[:, 6 + n % 2, :], ACT.Gelu,
                                     scale=s[:, c:c + 1]).then_inc(self.gelu_done, 1)
        yield 1 << 19
        act.wait_ge(self.g_in, 1)
        nc.scalar.activation(K.g[:, :, :], K.g[:, :, :], ACT.Silu).then_inc(self.g_ready, 1)

    def vector(self, dve):
        nc, K = self.nc, self.K
        for c in range(4):
            yield c - 4
            dve.wait_ge(self.silu_done, c + 1)
            nc.vector.scalar_tensor_tensor(self.h[:, c, :], K.ps[:, 7, :], K.s0_2[:, c:c + 1],
                                           self.a[:, c % 2, :], ALU.mult, ALU.mult).then_inc(self.h_ready, 1)
        yield self.OUT_STEP + NT
        dve.wait_ge(self.out_done, 1)
        nc.vector.tensor_tensor(K.g[:, :, :], K.ps[:, 6, :].rearrange("p (t d) -> p t d", t=NT),
                                K.s0_3[:, :].unsqueeze(1).to_broadcast([P, NT, D]), ALU.mult).then_inc(self.g_in, 1)




class Fp4Ffn(Beside):

    BEFORE = 8
    UP_STEP = 2
    TURN_STEP = 30
    DOWN_STEP = 36

    def __init__(self, nc, K, ctx):
        self.nc, self.K = nc, K
        (self.vec, self.xq_ready, self.turned, self.xqT_ready, self.projected, self.silu_done, self.h_done,
         self.hq_ready, self.hturned, self.hT_ready, self.down, self.g_ready) = K.pool[24:36]
        self.xq = sbuf(nc, ctx, "xq", [P, NT, D])
        self.xqT = sbuf(nc, ctx, "xqT", [P, T])
        self.h = sbuf(nc, ctx, "h1", [P, NT, I1])
        self.hT = sbuf(nc, ctx, "h1T", [P, 3, T])
        self.scr = fp4_scratch(nc, ctx, NT * I1, self.hT[:, :, :].rearrange("p c t -> p (c t)"))

    def tensor(self, pe):
        nc, K = self.nc, self.K
        yield 0
        pe.wait_ge(self.xq_ready, 1)
        for t in range(NT):
            mm = nc.tensor.transpose(K.ps[:, 7, t * P:(t + 1) * P], self.xq[:, t, :], K.ident[:, :])
        mm.then_inc(self.turned, 1)
        for t in range(NT):
            yield self.UP_STEP + 2 * t
            if t == 0:
                pe.wait_ge(self.xqT_ready, 1)
            else:
                pe.wait_ge(self.h_done, t)
            nc.tensor.matmul(K.ps[:, 6, 0:I1], self.xqT[:, t * P:(t + 1) * P], K.w_gu[:, 0:I1],
                             start=True, stop=True)
            nc.tensor.matmul(K.ps[:, 7, 0:I1], self.xqT[:, t * P:(t + 1) * P], K.w_gu[:, I1:2 * I1],
                             start=True, stop=True).then_inc(self.projected, 1)
        for c in range(3):
            yield self.TURN_STEP + c
            if c == 0:
                pe.wait_ge(self.hq_ready, 1)
            if c == 2:
                pe.wait_ge(self.hT_ready, 1)
            n = min(P, I1 - c * P)
            for t in range(NT):
                mm = nc.tensor.transpose(K.ps[0:n, 6 + c % 2, t * P:(t + 1) * P], self.h[:, t, c * P:c * P + n],
                                         K.ident[:, :])
            mm.then_inc(self.hturned, 1)
        for t in range(NT):
            yield self.DOWN_STEP + t
            if t == 0:
                pe.wait_ge(self.hT_ready, 3)
            for c in range(3):
                n = min(P, I1 - c * P)
                mm = nc.tensor.matmul(K.ps[:, 7, t * P:(t + 1) * P], self.hT[0:n, c, t * P:(t + 1) * P],
                                      K.w_down[0:n, c, :], start=(c == 0), stop=(c == 2))
        mm.then_inc(self.down, 1)

    def scalar(self, act):
        nc, K = self.nc, self.K
        yield 0
        act.wait_ge(self.turned, 1)
        nc.scalar.activation(self.xqT[:, :], K.ps[:, 7, :], ACT.Identity).then_inc(self.xqT_ready, 1)
        for t in range(NT):
            yield self.UP_STEP + 2 * t
            act.wait_ge(self.projected, t + 1)
            nc.scalar.activation(self.h[:, t, :], K.ps[:, 6, 0:I1], ACT.Silu).then_inc(self.silu_done, 1)
        for c in range(3):
            yield self.TURN_STEP + c
            act.wait_ge(self.hturned, c + 1)
            n = min(P, I1 - c * P)
            nc.scalar.activation(self.hT[0:n, c, :], K.ps[0:n, 6 + c % 2, :], ACT.Identity).then_inc(self.hT_ready, 1)
        yield 1 << 19
        act.wait_ge(self.down, 1)
        nc.scalar.activation(K.g[:, :, :], K.ps[:, 7, :].rearrange("p (t d) -> p t d", t=NT),
                             ACT.Silu).then_inc(self.g_ready, 1)

    def vector(self, dve):
        nc, K = self.nc, self.K
        ch = Chain(dve, self.vec)
        yield -self.BEFORE
        for _ in fp4_blocks(nc, ch, K.xn[:, :, :].rearrange("p t d -> p (t d)"),
                            self.xq[:, :, :].rearrange("p t d -> p (t d)"), *self.scr, P, NT * D):
            pass
        nc.vector.engine_nop().then_inc(self.xq_ready, 1)
        for t in range(NT):
            yield self.UP_STEP + 2 * t
            dve.wait_ge(self.silu_done, t + 1)
            nc.vector.tensor_tensor(self.h[:, t, :], self.h[:, t, :], K.ps[:, 7, 0:I1],
                                    ALU.mult).then_inc(self.h_done, 1)
        yield self.UP_STEP + 2 * NT - 1
        dve.wait_ge(self.h_done, NT)
        flat = self.h[:, :, :].rearrange("p t i -> p (t i)")
        step = self.UP_STEP + 2 * NT
        for _ in fp4_blocks(nc, ch, flat, flat, *self.scr, P, NT * I1):
            yield step
            step += 1
        nc.vector.engine_nop().then_inc(self.hq_ready, 1)




def copy_shifted(nc, K, turned, shifted, bank):
    def scalar(act):
        act.wait_ge(turned, 1)
        nc.scalar.activation(K.shT[0:64, :], K.ps[0:64, bank, :], ACT.Identity).then_inc(shifted, 1)

    def vector(dve):
        nc.vector.memset(K.shT[64:128, 0:1], 0.0)
        dve.wait_ge(turned, 1)
        nc.vector.tensor_copy(K.shT[64:128, 1:T], K.ps[64:128, bank, 0:T - 1]).then_inc(shifted, 1)

    return scalar, vector


def local_qkv(nc, K, L):
    (turned, shifted, projected, squared, v_copied, summed, clipped, rn_ready, rotated, scaled, qk_turned, copied,
     vec, added, cleared) = K.pool[0:15]
    w = K.w2_qkv[L]
    with ExitStack() as tmp:
        sq = sbuf(nc, tmp, "sq", [P, 2, INNER])
        rot = sbuf(nc, tmp, "rot", [P, 2, 2, INNER])
        qk = sbuf(nc, tmp, "qk_tm", [P, 2, 2, INNER])
        ssq = sbuf(nc, tmp, "ssq", [P, NT, 2, LH])
        rn = sbuf(nc, tmp, "rn", [P, NT, 2, LH])
        shift_act, shift_dve = copy_shifted(nc, K, turned, shifted, 7)
        with nc.Block() as block:
            @block.tensor
            def _(pe):
                for t in range(NT):
                    mm = nc.tensor.transpose(K.ps[:, 7, t * P:(t + 1) * P], (K.y if L else K.xn)[:, t, :],
                                             K.ident[:, :])
                mm.then_inc(turned, 1)
                pe.wait_ge(shifted, 2)

                def project(t):
                    if t >= 2:
                        pe.wait_ge(v_copied, t - 1)
                        pe.wait_ge(rotated, 2 * (t - 1))
                    for m in range(3):
                        mm = nc.tensor.matmul(K.ps[:, 3 * (t % 2) + m, :], K.shT[:, t * P:(t + 1) * P],
                                              w[:, m * INNER:(m + 1) * INNER], start=True, stop=True)
                    mm.then_inc(projected, 1)

                def turn(t):
                    for m in range(2):
                        pe.wait_ge(scaled, 2 * t + m + 1)
                        if t:
                            pe.wait_ge(copied, 3 * t - 1 + m)
                        for p in range(LH // 2):
                            mm = nc.tensor.transpose(K.ps[:, 6 + m, p * P:(p + 1) * P],
                                                     qk[:, t % 2, m, p * P:(p + 1) * P], K.ident[:, :])
                        mm.then_inc(qk_turned, 1)

                project(0)
                project(1)
                for t in range(NT):
                    if t + 2 < NT:
                        project(t + 2)
                    turn(t)

            @block.scalar
            def _(act):
                shift_act(act)

                def copy(t):
                    act.wait_ge(qk_turned, 2 * t + 1)
                    for e in range(2):
                        nc.scalar.activation(K.qz[64 * e:64 * e + 64, e:LH:2, t * P:(t + 1) * P],
                                             K.ps[64 * e:64 * e + 64, 6, :].rearrange("p (h t) -> p h t", t=P),
                                             ACT.Identity).then_inc(copied, 1)
                    act.wait_ge(qk_turned, 2 * t + 2)
                    nc.scalar.activation(K.kT[:, :, t * P:(t + 1) * P],
                                         K.ps[:, 7, :].rearrange("p (h t) -> p h t", t=P),
                                         ACT.Identity).then_inc(copied, 1)

                for t in range(NT):
                    act.wait_ge(projected, t + 1)
                    b = 3 * (t % 2)
                    for m in range(2):
                        if t:
                            act.wait_ge(summed, 2 * (t - 1) + m + 1)
                        nc.scalar.activation(sq[:, m, :], K.ps[:, b + m, :], ACT.Square).then_inc(squared, 1)
                    nc.scalar.activation(K.v_tm[:, t, :, 0:LD], K.ps[:, b + 2, :].rearrange("p (h d) -> p h d", d=LD),
                                         ACT.Identity).then_inc(v_copied, 1)
                    if t:
                        copy(t - 1)
                copy(NT - 1)

            @block.vector
            def _(dve):
                shift_dve(dve)
                nc.vector.memset(K.v_tm[:, :, :, LD:LD + 1], 1.0)
                if L == 0:
                    nc.vector.tensor_copy(K.y[:, :, :], K.xn[:, :, :])
                ch = Chain(dve, vec)

                def scale(t):
                    dve.wait_ge(rn_ready, t + 1)
                    for m in range(2):
                        dve.wait_ge(added, 2 * t + m + 1)
                        x3 = qk[:, t % 2, m, :].rearrange("p (h d) -> p h d", d=LD)
                        nc.vector.tensor_tensor(x3, x3, rn[:, t, m, :].unsqueeze(2).to_broadcast([P, LH, LD]),
                                                ALU.mult).then_inc(scaled, 1)

                for t in range(NT):
                    b = 3 * (t % 2)
                    for m in range(2):
                        dve.wait_ge(squared, 2 * t + m + 1)
                        nc.vector.tensor_reduce(ssq[:, t, m, :], sq[:, m, :].rearrange("p (h d) -> p h d", d=LD),
                                                AX.X, ALU.add).then_inc(summed, 1)
                    dve.wait_ge(summed, 2 * t + 2)
                    nc.vector.tensor_scalar(ssq[:, t, 0, :], ssq[:, t, 0, :], 1e-24, 1.0 / 64, ALU.max,
                                            ALU.mult).then_inc(clipped, 1)
                    nc.vector.tensor_scalar(ssq[:, t, 1, :], ssq[:, t, 1, :], 1e-24, None, ALU.max).then_inc(clipped, 1)
                    if t >= 2:
                        dve.wait_ge(qk_turned, 2 * (t - 1))
                    for m, (cos, sin) in enumerate(((K.cosq, K.sinq), (K.cosk, K.sink))):
                        src = K.ps[:, b + m, :].rearrange("p (h two d) -> p h two d", two=2, d=LD // 2)
                        rv = rot[:, t % 2, m, :].rearrange("p (h two d) -> p h two d", two=2, d=LD // 2)
                        for e in range(2):
                            s = sin[L][:, t, 32 * e:32 * e + 32].unsqueeze(1).to_broadcast([P, LH, 32])
                            ch.tick(nc.vector.tensor_tensor(rv[:, :, e, :], src[:, :, 1 - e, :], s, ALU.mult))
                        ch.wait()
                        c = cos[L][:, t, :].unsqueeze(1).to_broadcast([P, LH, LD])
                        nc.vector.tensor_tensor(qk[:, t % 2, m, :].rearrange("p (h d) -> p h d", d=LD),
                                                K.ps[:, b + m, :].rearrange("p (h d) -> p h d", d=LD), c,
                                                ALU.mult).then_inc(rotated, 1)
                    if t:
                        scale(t - 1)
                scale(NT - 1)

            @block.gpsimd
            def _(pool):
                nc.gpsimd.memset(K.qz[64:128, 0:LH:2, :], 0.0).then_inc(cleared, 1)
                pool.wait_ge(cleared, 1)
                nc.gpsimd.memset(K.qz[0:64, 1:LH:2, :], 0.0).then_inc(cleared, 1)
                pool.wait_ge(cleared, 2)
                for t in range(NT):
                    pool.wait_ge(clipped, 2 * t + 2)
                    nc.gpsimd.tensor_tensor(rn[:, t, :, :].rearrange("p m h -> p (m h)"),
                                            ssq[:, t, :, :].rearrange("p m h -> p (m h)"),
                                            K.neghalf[:, 0:2 * LH], ALU.pow).then_inc(rn_ready, 1)
                    for m in range(2):
                        pool.wait_ge(rotated, 2 * t + m + 1)
                        x = qk[:, t % 2, m, :]
                        nc.gpsimd.tensor_tensor(x, x, rot[:, t % 2, m, :], ALU.add).then_inc(added, 1)
        K.clear()


def local_attention(nc, K, L):
    (scored, reduced, exped, zeroed, turned, copied, summed, divided, vec, oturned, oT_ready, projected) = K.pool[0:12]
    with ExitStack() as tmp:
        nm = sbuf(nc, tmp, "nm", [P, 2, NT])
        rden = sbuf(nc, tmp, "rden", [P, 2, NT])
        probs = sbuf(nc, tmp, "probs", [P, 2, NT, 2 * P])
        pT = sbuf(nc, tmp, "probsT", [P, 2, NT, 2 * P])
        o_tm = sbuf(nc, tmp, "o_tm", [P, NT, INNER])
        with nc.Block() as block:
            @block.tensor
            def _(pe):
                def scores(h):
                    if h >= 2:
                        pe.wait_ge(exped, h - 1)
                    for t in range(NT):
                        b = 2 * (h % 2) + t // 2
                        c = 256 * (t % 2)
                        nc.tensor.matmul(K.ps[:, b, c + 64:c + 256], K.identb[:, :],
                                         (K.mask_band if t else K.mask_band0)[:, :], start=True, stop=False)
                        k0 = 64 if t else 128
                        mm = nc.tensor.matmul(K.ps[:, b, c + k0:c + 256], K.qz[:, h, t * P:(t + 1) * P],
                                              K.kT[:, h // 2, t * P - 128 + k0:(t + 1) * P], start=False, stop=True)
                    mm.then_inc(scored, 1)

                def turn(h):
                    pe.wait_ge(exped, h + 1)
                    if h == 0:
                        pe.wait_ge(zeroed, 1)
                    for u in range(2):
                        if h:
                            pe.wait_ge(copied, 2 * h + u - 1)
                        for t in (2 * u, 2 * u + 1):
                            for e in range(2):
                                o = (t % 2) * 256 + e * P
                                mm = nc.tensor.transpose(K.ps[:, 4 + u, o:o + P], probs[:, h % 2, t, e * P:(e + 1) * P],
                                                         K.ident[:, :])
                        mm.then_inc(turned, 1)

                def weigh(h):
                    pe.wait_ge(copied, 2 * h + 2)
                    if h >= 2:
                        pe.wait_ge(divided, h - 1)
                    for t in range(NT):
                        o = K.ps[:, 6 + h % 2, t * 65:(t + 1) * 65]
                        if t:
                            nc.tensor.matmul(o, pT[:, h % 2, t, 0:P], K.v_tm[:, t - 1, h, :], start=True, stop=False)
                        mm = nc.tensor.matmul(o, pT[:, h % 2, t, P:2 * P], K.v_tm[:, t, h, :],
                                              start=(t == 0), stop=True)
                    mm.then_inc(summed, 1)

                scores(0)
                scores(1)
                for h in range(LH):
                    turn(h)
                    if h + 2 < LH:
                        scores(h + 2)
                    weigh(h)
                for p in range(4):
                    pe.wait_ge(divided, 2 * p + 2)
                    for t in range(NT):
                        mm = nc.tensor.transpose(K.ps[:, p, t * P:(t + 1) * P], o_tm[:, t, p * P:(p + 1) * P],
                                                 K.ident[:, :])
                    mm.then_inc(oturned, 1)
                pe.wait_ge(oT_ready, 4)
                for t in range(NT):
                    for p in range(4):
                        mm = nc.tensor.matmul(K.ps[:, 4, t * P:(t + 1) * P], K.oT[:, p, t * P:(t + 1) * P],
                                              K.w2_o[L][:, p, :], start=(p == 0), stop=(p == 3))
                mm.then_inc(projected, 1)

            @block.vector
            def _(dve):
                ch = Chain(dve, vec)

                def maxima(h):
                    dve.wait_ge(scored, h + 1)
                    s = K.ps[:, 2 * (h % 2):2 * (h % 2) + 2, :].rearrange("p b (t k) -> p (b t) k", k=256)
                    nc.vector.tensor_reduce(nm[:, h % 2, :], s[:, :, 64:256], AX.X, ALU.max,
                                            negate=True).then_inc(reduced, 1)

                def divide(h):
                    i = h % 2
                    dve.wait_ge(summed, h + 1)
                    o = K.ps[:, 6 + i, 0:NT * 65].rearrange("p (t d) -> p t d", d=65)
                    ch.do(nc.vector.reciprocal(rden[:, i, :], o[:, :, LD]))
                    nc.vector.tensor_tensor(o_tm[:, :, h * LD:(h + 1) * LD], o[:, :, 0:LD],
                                            rden[:, i, :].unsqueeze(2).to_broadcast([P, NT, LD]),
                                            ALU.mult).then_inc(divided, 1)

                maxima(0)
                maxima(1)
                for h in range(LH):
                    for u in range(2):
                        dve.wait_ge(turned, 2 * h + u + 1)
                        if h >= 2 and u == 0:
                            dve.wait_ge(summed, h - 1)
                        nc.vector.tensor_copy(pT[:, h % 2, 2 * u:2 * u + 2, :], K.ps[:, 4 + u, :].rearrange(
                            "p (t k) -> p t k", k=256)).then_inc(copied, 1)
                    if h + 2 < LH:
                        maxima(h + 2)
                    if h:
                        divide(h - 1)
                divide(LH - 1)
                dve.wait_ge(projected, 1)
                nc.vector.tensor_tensor(K.y[:, :, :], K.y[:, :, :],
                                        K.ps[:, 4, :].rearrange("p (t d) -> p t d", t=NT), ALU.add)

            @block.scalar
            def _(act):
                for h in range(LH):
                    i = h % 2
                    act.wait_ge(reduced, h + 1)
                    if h >= 2:
                        act.wait_ge(turned, 2 * (h - 1))
                    for t in range(NT):
                        b, c = 2 * i + t // 2, 256 * (t % 2)
                        a = nc.scalar.activation(probs[:, i, t, 64:256], K.ps[:, b, c + 64:c + 256], ACT.Exp,
                                                 bias=nm[:, i, t:t + 1])
                    a.then_inc(exped, 1)
                for p in range(4):
                    act.wait_ge(oturned, p + 1)
                    nc.scalar.activation(K.oT[:, p, :], K.ps[:, p, :], ACT.Identity).then_inc(oT_ready, 1)

            @block.gpsimd
            def _(pool):
                nc.gpsimd.memset(probs[:, :, :, 0:64], 0.0).then_inc(zeroed, 1)
        K.clear()


class Glu(Beside):

    BEFORE = 5
    UP_STEP, DOWN_STEP = 0, 8

    def __init__(self, nc, K, ctx, L, alone):
        self.nc, self.K, self.L = nc, K, L
        (self.back, self.vec, self.var_ready, self.rstd_ready, self.hn_ready, self.turned, self.hnT_ready, self.up,
         self.gelu_done, self.hid_ready, self.down, self.yturned, self.shifted) = K.pool[24:37]
        self.y_bank, self.back_bank, self.turn_bank, self.down_bank = (7, 0, 1, 6) if alone else (7, 6, 7, 6)
        self.up_banks = [(2, 3), (4, 5)] if alone else [(6, 7)]
        self.rows = [P, P, HID2 - 2 * P]
        self.hn = sbuf(nc, ctx, "hn", [P, NT, D])
        self.hnT = sbuf(nc, ctx, "hnT", [P, T])
        self.gl = sbuf(nc, ctx, "gl", [P, 2, T])
        self.hid = sbuf(nc, ctx, "hid", [P, 3, T])
        self.shift_act, self.shift_dve = copy_shifted(nc, K, self.yturned, self.shifted, self.y_bank)

    def tensor(self, pe):
        nc, K, L = self.nc, self.K, self.L
        for t in range(NT):
            mm = nc.tensor.transpose(K.ps[:, self.y_bank, t * P:(t + 1) * P], K.y[:, t, :], K.ident[:, :])
        mm.then_inc(self.yturned, 1)
        yield -4
        pe.wait_ge(self.shifted, 2)
        for t in range(NT):
            mm = nc.tensor.transpose(K.ps[:, self.back_bank, t * P:(t + 1) * P], K.shT[:, t * P:(t + 1) * P],
                                     K.ident[:, :])
        mm.then_inc(self.back, 1)
        yield -2
        pe.wait_ge(self.hn_ready, NT)
        for t in range(NT):
            mm = nc.tensor.transpose(K.ps[:, self.turn_bank, t * P:(t + 1) * P], self.hn[:, t, :], K.ident[:, :])
        mm.then_inc(self.turned, 1)
        for c in range(3):
            n = self.rows[c]
            for m in range(2):
                yield self.UP_STEP + 2 * c + m
                if c == 0 and m == 0:
                    pe.wait_ge(self.hnT_ready, 1)
                if m == 0 and c >= len(self.up_banks):
                    pe.wait_ge(self.hid_ready, c - len(self.up_banks) + 1)
                mm = nc.tensor.matmul(K.ps[0:n, self.up_banks[c % len(self.up_banks)][m], :],
                                      K.w2_up[L][:, m * HID2 + c * P:m * HID2 + c * P + n], self.hnT[:, :],
                                      start=True, stop=True)
            mm.then_inc(self.up, 1)
        for t in range(NT):
            yield self.DOWN_STEP + t
            if t == 0:
                pe.wait_ge(self.hid_ready, 3)
            for c in range(3):
                n = self.rows[c]
                mm = nc.tensor.matmul(K.ps[:, self.down_bank, t * P:(t + 1) * P],
                                      self.hid[0:n, c, t * P:(t + 1) * P], K.w2_down[L][0:n, c, :],
                                      start=(c == 0), stop=(c == 2))
        mm.then_inc(self.down, 1)

    def vector(self, dve):
        nc, K, L = self.nc, self.K, self.L
        self.shift_dve(dve)
        ch = Chain(dve, self.vec)
        yield -4
        dve.wait_ge(self.back, 1)
        for t in range(NT):
            ch.tick(nc.vector.bn_stats(K.stats[:, t, :], K.ps[:, self.back_bank, t * P:(t + 1) * P]))
        ch.wait()
        for t in range(NT):
            ch.tick(nc.vector.bn_aggr(K.mv[:, t, :], K.stats[:, t, :]))
        ch.wait()
        nc.vector.tensor_scalar(K.var[:, 0:NT], K.mv[:, :, 1], 1e-5, None, ALU.add).then_inc(self.var_ready, 1)
        yield -3
        dve.wait_ge(self.rstd_ready, 1)
        for t in range(NT):
            nc.vector.tensor_scalar(self.hn[:, t, :], K.ps[:, self.back_bank, t * P:(t + 1) * P], K.mv[:, t, 0:1],
                                    K.rstd[:, t:t + 1], ALU.subtract, ALU.mult).then_inc(self.hn_ready, 1)
        for c in range(3):
            yield self.UP_STEP + 2 * c + 1
            n = self.rows[c]
            dve.wait_ge(self.gelu_done, c + 1)
            nc.vector.scalar_tensor_tensor(self.hid[0:n, c, :], K.ps[0:n, self.up_banks[c % len(self.up_banks)][0], :],
                                           K.b2_up[L][0:n, c:c + 1], self.gl[0:n, c % 2, :],
                                           ALU.add, ALU.mult).then_inc(self.hid_ready, 1)
        yield self.DOWN_STEP + NT - 1
        dve.wait_ge(self.down, 1)
        ch.do(nc.vector.tensor_tensor(K.y[:, :, :], K.y[:, :, :],
                                      K.ps[:, self.down_bank, :].rearrange("p (t d) -> p t d", t=NT), ALU.add))
        nc.vector.tensor_tensor(K.y[:, :, :], K.y[:, :, :],
                                K.b2_down[L][:, :].unsqueeze(1).to_broadcast([P, NT, D]), ALU.add)

    def gpsimd(self, pool):
        nc, K = self.nc, self.K
        yield -4
        pool.wait_ge(self.var_ready, 1)
        nc.gpsimd.tensor_tensor(K.rstd[:, 0:NT], K.var[:, 0:NT], K.neghalf[:, 0:NT],
                                ALU.pow).then_inc(self.rstd_ready, 1)

    def scalar(self, act):
        nc, K, L = self.nc, self.K, self.L
        self.shift_act(act)
        yield -2
        act.wait_ge(self.turned, 1)
        nc.scalar.activation(self.hnT[:, :], K.ps[:, self.turn_bank, :], ACT.Identity, scale=K.ln2_g[L][:, 0:1],
                             bias=K.ln2_b[L][:, 0:1]).then_inc(self.hnT_ready, 1)
        for c in range(3):
            yield self.UP_STEP + 2 * c + 1
            n = self.rows[c]
            act.wait_ge(self.up, c + 1)
            if c == 2:
                act.wait_ge(self.hid_ready, 1)
            nc.scalar.activation(self.gl[0:n, c % 2, :], K.ps[0:n, self.up_banks[c % len(self.up_banks)][1], :],
                                 ACT.Gelu, bias=K.b2_up[L][0:n, 3 + c:4 + c]).then_inc(self.gelu_done, 1)


def gate_residual(nc, K):
    silu_done, vec = K.pool[0:2]
    with nc.Block() as block:
        @block.scalar
        def _(act):
            nc.scalar.activation(K.y[:, :, :], K.y[:, :, :], ACT.Silu).then_inc(silu_done, 1)

        @block.vector
        def _(dve):
            ch = Chain(dve, vec)
            dve.wait_ge(silu_done, 1)
            ch.do(nc.vector.tensor_tensor(K.y[:, :, :], K.y[:, :, :], K.att[:, :, :], ALU.mult))
            nc.vector.tensor_tensor(K.x[:, :, :], K.x[:, :, :], K.y[:, :, :], ALU.add)
    K.clear()


def local_sublayer(nc, K, L):
    with ExitStack() as tmp:
        K.v_tm = sbuf(nc, tmp, "v_tm", [P, NT, LH, LD + 1])
        K.qz = sbuf(nc, tmp, "qz", [P, LH, T])
        K.kT = sbuf(nc, tmp, "kT", [P, LH // 2, T])
        K.oT = sbuf(nc, tmp, "oT2", [P, LH // 2, T])
        local_qkv(nc, K, L)
        local_attention(nc, K, L)




def experts(nc, K):
    gated, vec, e_in, e_done, h12, silu_done, hid_ready, out_done, used = K.pool[0:9]
    with ExitStack() as tmp:
        sc = sbuf(nc, tmp, "sc", [P, NT, E3])
        top = sbuf(nc, tmp, "top", [P, NT, 8])
        idx = sbuf(nc, tmp, "idx", [P, NT, 8], U32)
        idf = sbuf(nc, tmp, "idf", [P, NT, 8])
        ex = sbuf(nc, tmp, "ex", [P, NT])
        pr = sbuf(nc, tmp, "pr", [P, 2, NT])
        eq = sbuf(nc, tmp, "eq", [P, 2, NT, E3])
        pb = sbuf(nc, tmp, "pb", [P, NT, E3])
        a = sbuf(nc, tmp, "silu_a", [P, 2, T])
        h = sbuf(nc, tmp, "hid", [P, 2, 2, T])
        with nc.Block() as block:
            @block.tensor
            def _(pe):
                for t in range(NT):
                    mm = nc.tensor.matmul(K.ps[:, 6, t * E3:(t + 1) * E3], K.xnT[:, t * P:(t + 1) * P],
                                          K.w3_gate[:, :], start=True, stop=True)
                mm.then_inc(gated, 1)

                def down(e):
                    pe.wait_ge(hid_ready, 2 * e + 2)
                    if e:
                        pe.wait_ge(used, e)
                    for t in range(NT):
                        for c in range(2):
                            mm = nc.tensor.matmul(K.ps[:, 7, t * P:(t + 1) * P], h[:, e % 2, c, t * P:(t + 1) * P],
                                                  K.w3_down[:, e, c, :], start=(c == 0), stop=(c == 1))
                    mm.then_inc(out_done, 1)

                for e in range(E3):
                    for c in range(2):
                        n = 2 * e + c
                        if n >= 2:
                            pe.wait_ge(hid_ready, n - 1)
                        for m in range(2):
                            mm = nc.tensor.matmul(K.ps[:, 2 * (n % 2) + m, :],
                                                  K.w3_up[:, e, (2 * m + c) * P:(2 * m + c + 1) * P], K.xnT[:, :],
                                                  start=True, stop=True)
                        mm.then_inc(h12, 1)
                    if e:
                        down(e - 1)
                down(E3 - 1)

            @block.scalar
            def _(act):
                act.wait_ge(e_in, 1)
                nc.scalar.activation(ex[:, :], ex[:, :], ACT.Exp).then_inc(e_done, 1)
                for n in range(2 * E3):
                    act.wait_ge(h12, n + 1)
                    if n >= 2:
                        act.wait_ge(hid_ready, n - 1)
                    nc.scalar.activation(a[:, n % 2, :], K.ps[:, 2 * (n % 2), :], ACT.Silu).then_inc(silu_done, 1)

            @block.vector
            def _(dve):
                ch = Chain(dve, vec)
                dve.wait_ge(gated, 1)
                ch.do(nc.vector.tensor_copy(sc[:, :, :], K.ps[:, 6, 0:NT * E3].rearrange("p (t e) -> p t e", t=NT)))
                for t in range(NT):
                    ch.tick(nc.vector.max(top[:, t, :], sc[:, t, :]))
                ch.wait()
                for t in range(NT):
                    ch.tick(nc.vector.max_index(idx[:, t, :], top[:, t, :], sc[:, t, :]))
                ch.tick(nc.vector.tensor_tensor(ex[:, :], top[:, :, 1], top[:, :, 0], ALU.subtract))
                ch.wait()
                nc.vector.tensor_copy(idf[:, :, :], idx[:, :, :]).then_inc(e_in, 1)
                dve.wait_ge(e_done, 1)
                ch.do(nc.vector.tensor_scalar(pr[:, 0, :], ex[:, :], 1.0, None, ALU.add))
                ch.do(nc.vector.reciprocal(pr[:, 0, :], pr[:, 0, :]))
                ch.do(nc.vector.tensor_tensor(pr[:, 1, :], ex[:, :], pr[:, 0, :], ALU.mult))
                for r in range(2):
                    for t in range(NT):
                        ch.tick(nc.vector.tensor_scalar(eq[:, r, t, :], K.iota8[:, :], idf[:, t, r:r + 1],
                                                        pr[:, r, t:t + 1], ALU.is_equal, ALU.mult))
                ch.wait()
                ch.do(nc.vector.tensor_tensor(pb[:, :, :], eq[:, 0, :, :], eq[:, 1, :, :], ALU.add))

                def add_out(e):
                    dve.wait_ge(out_done, e + 1)
                    for t in range(NT):
                        o = K.ps[:, 7, t * P:(t + 1) * P]
                        if e == 0:
                            i = nc.vector.tensor_scalar(K.y[:, t, :], o, pb[:, t, e:e + 1], None, ALU.mult)
                        else:
                            i = nc.vector.scalar_tensor_tensor(K.y[:, t, :], o, pb[:, t, e:e + 1], K.y[:, t, :],
                                                               ALU.mult, ALU.add)
                        if t < NT - 1:
                            ch.tick(i)
                    i.then_inc(used, 1)
                    dve.wait_ge(used, e + 1)
                    ch.wait()

                for e in range(E3):
                    for c in range(2):
                        n = 2 * e + c
                        dve.wait_ge(silu_done, n + 1)
                        if c == 0 and e >= 2:
                            dve.wait_ge(out_done, e - 1)
                        nc.vector.tensor_tensor(h[:, e % 2, c, :], K.ps[:, 2 * (n % 2) + 1, :], a[:, n % 2, :],
                                                ALU.mult).then_inc(hid_ready, 1)
                    if e:
                        add_out(e - 1)
                add_out(E3 - 1)
        K.clear()


def memory_inputs(nc, K, b):
    projected, raw_ready, conv_ready, sig_done, vec, abs_ready, exp_done, ln_done, aet_ready, silu_done, f_ready, \
        stored = K.pool[0:12]
    with ExitStack() as tmp:
        raw = sbuf(nc, tmp, "raw", [96, T + 3])
        conv = sbuf(nc, tmp, "conv", [96, T])
        aet = sbuf(nc, tmp, "aet", [96, T])
        zt = sbuf(nc, tmp, "zt", [96, T])
        za = sbuf(nc, tmp, "za", [96, T])
        fac = sbuf(nc, tmp, "fac", [P, NT, D])
        th = slice(64, 96)
        with nc.Block() as block:
            @block.tensor
            def _(pe):
                nc.tensor.matmul(K.ps[0:96, 0, :], K.w3_kvq[:, :], K.xnT[:, :], start=True, stop=True)
                nc.tensor.matmul(K.ps[0:96, 1, :], K.w3_aet[:, :], K.xnT[:, :], start=True, stop=True)
                for t in range(NT):
                    mm = nc.tensor.matmul(K.ps[:, 2, t * P:(t + 1) * P], K.xnT[:, t * P:(t + 1) * P], K.w3_g[:, :],
                                          start=True, stop=True)
                mm.then_inc(projected, 1)

            @block.scalar
            def _(act):
                act.wait_ge(projected, 1)
                nc.scalar.activation(raw[:, 3:T + 3], K.ps[0:96, 0, :], ACT.Identity).then_inc(raw_ready, 1)
                nc.scalar.activation(aet[0:64, :], K.ps[0:64, 1, :], ACT.Sigmoid,
                                     bias=K.b3_aet[0:64, 0:1]).then_inc(sig_done, 1)
                nc.scalar.activation(K.y[:, :, :], K.y[:, :, :], ACT.Silu).then_inc(silu_done, 1)
                act.wait_ge(abs_ready, 1)
                nc.scalar.activation(za[th, :], za[th, :], ACT.Exp, scale=-1.0).then_inc(exp_done, 1)
                act.wait_ge(exp_done, 1)
                nc.scalar.activation(za[th, :], za[th, :], ACT.Ln, bias=1.0).then_inc(ln_done, 1)

            @block.vector
            def _(dve):
                ch = Chain(dve, vec)
                ch.tick(nc.vector.memset(raw[:, 0:3], 0.0))
                dve.wait_ge(projected, 1)
                ch.do(nc.vector.tensor_scalar(zt[th, :], K.ps[64:96, 1, :], K.b3_aet[th, 0:1], None, ALU.add))
                nc.vector.scalar_tensor_tensor(za[th, :], zt[th, :], -1.0, zt[th, :], ALU.mult, ALU.max).then_inc(abs_ready, 1)
                dve.wait_ge(raw_ready, 1)
                ch.do(nc.vector.tensor_scalar(conv[:, :], raw[:, 0:T], K.conv_w[:, 0:1], K.conv_b[:, 0:1],
                                              ALU.mult, ALU.add))
                for j in range(1, 4):
                    i = nc.vector.scalar_tensor_tensor(conv[:, :], raw[:, j:j + T], K.conv_w[:, j:j + 1], conv[:, :],
                                                       ALU.mult, ALU.add)
                    if j < 3:
                        ch.do(i)
                    else:
                        i.then_inc(conv_ready, 1)
                dve.wait_ge(ln_done, 1)
                nc.vector.scalar_tensor_tensor(aet[th, :], zt[th, :], 0.0, za[th, :], ALU.max,
                                               ALU.add).then_inc(aet_ready, 1)
                for t in range(NT):
                    ch.tick(nc.vector.tensor_tensor(fac[:, t, :], K.ps[:, 2, t * P:(t + 1) * P], K.g3_b[:, :], ALU.add))
                ch.wait()
                for t in range(NT):
                    ch.tick(nc.vector.tensor_tensor(fac[:, t, :], fac[:, t, :], K.norm3[:, :], ALU.mult))
                ch.wait()
                dve.wait_ge(silu_done, 1)
                nc.vector.tensor_tensor(fac[:, :, :], fac[:, :, :], K.y[:, :, :], ALU.mult).then_inc(f_ready, 1)

            @block.sync
            def _(sp):
                sp.dma_start(K.x_d[b, :, :].rearrange("(t p) d -> p t d", p=P), K.x[:, :, :]).then_inc(stored, 16)
                sp.wait_ge(conv_ready, 1)
                sp.dma_start(K.kvq_d[b, :, :], conv[:, :]).then_inc(stored, 16)
                sp.wait_ge(sig_done, 1)
                sp.wait_ge(aet_ready, 1)
                sp.dma_start(K.aet_d[b, :, :], aet[:, :]).then_inc(stored, 16)
                sp.wait_ge(f_ready, 1)
                sp.dma_start(K.fac_d[b, :, :].rearrange("(t p) d -> p t d", p=P), fac[:, :, :]).then_inc(stored, 16)
                sp.wait_ge(stored, 64)
        K.clear()




def memory_coefficients(nc, K, M):
    landed, meant, used, vec, spread_meant, spread_used, kvq_landed = K.pool[0:7]
    NTOK = BATCH * T
    with ExitStack() as tmp:
        aet = sbuf(nc, tmp, "aet_in", [96, BATCH, T])
        om = sbuf(nc, tmp, "om", [CH, NTOK])
        et = sbuf(nc, tmp, "et", [CH, NTOK])
        Es = sbuf(nc, tmp, "Es", [CH, NTOK])
        om_s, et_s, Ea, imp = [sbuf(nc, tmp, n, [P, 2 * T]) for n in ("om_s", "et_s", "E_all", "impulse")]
        om0, et0 = [sbuf(nc, tmp, n, [P, 2 * NCH, 1]) for n in ("om0", "et0")]
        by_chunk = lambda a: a[:, :].rearrange("p (n t) -> p n t", t=CH)
        with nc.Block() as block:
            @block.sync
            def _(sp):
                for b in range(BATCH):
                    sp.dma_start(aet[:, b, :], K.aet_d[b, :, :]).then_inc(landed, 16)
                    sp.wait_ge(landed, 16 * (b + 1))

            @block.scalar
            def _(act):
                for m, dst in enumerate((M.k, M.v, M.q)):
                    src = K.kvq_d[:, 32 * m:32 * m + 32, :].rearrange("(g j) p t -> j p g t", j=4)
                    for j in range(4):
                        act.dma_start(dst[32 * j:32 * j + 32, :, :], src[j]).then_inc(kvq_landed, 16)
                act.wait_ge(kvq_landed, 16 * 12)

            @block.tensor
            def _(pe):
                for b in range(BATCH):
                    g, j = divmod(b, 4)
                    pe.wait_ge(landed, 16 * (b + 1))
                    if b >= 2:
                        pe.wait_ge(used, 2 * (b - 1))
                    for m in range(2):
                        mm = nc.tensor.matmul(K.ps[0:CH, 2 * (b % 2) + m, :], M.mean_w[:, m, :], aet[:, b, :],
                                              start=True, stop=True)
                    mm.then_inc(meant, 1)
                    if g and j == 0:
                        pe.wait_ge(spread_used, 3)
                    for m in range(3):
                        mm = nc.tensor.matmul(K.ps[32 * j:32 * j + 32, 4 + m, :], M.mean_w[:, m, 0:32], aet[:, b, :],
                                              start=True, stop=True, tile_position=(0, 32 * j))
                    mm.then_inc(spread_meant, 1)

            @block.vector
            def _(dve):
                ch = Chain(dve, vec)
                for b in range(BATCH):
                    g, j = divmod(b, 4)
                    dve.wait_ge(meant, b + 1)
                    s = slice(b * T, (b + 1) * T)
                    nc.vector.tensor_scalar(om[:, s], K.ps[0:CH, 2 * (b % 2), :], -0.1, 1.0, ALU.mult,
                                            ALU.add).then_inc(used, 1)
                    nc.vector.tensor_scalar(et[:, s], K.ps[0:CH, 2 * (b % 2) + 1, :], 0.9, 0.05, ALU.mult,
                                            ALU.add).then_inc(used, 1)
                    if j == 3:
                        dve.wait_ge(spread_meant, b + 1)
                        s = slice(g * T, (g + 1) * T)
                        nc.vector.tensor_scalar(om_s[:, s], K.ps[:, 4, :], -0.1, 1.0, ALU.mult,
                                                ALU.add).then_inc(spread_used, 1)
                        nc.vector.tensor_scalar(et_s[:, s], K.ps[:, 5, :], 0.9, 0.05, ALU.mult,
                                                ALU.add).then_inc(spread_used, 1)
                        nc.vector.tensor_scalar(M.nth[:, g, :], K.ps[:, 6, :], -0.1, None,
                                                ALU.mult).then_inc(spread_used, 1)
                dve.wait_ge(used, 2 * BATCH)
                dve.wait_ge(spread_used, 6)
                ch.tick(nc.vector.tensor_copy(om0[:, :, :], by_chunk(om_s)[:, :, 0:1]))
                ch.tick(nc.vector.tensor_copy(et0[:, :, :], by_chunk(et_s)[:, :, 0:1]))
                ch.tick(nc.vector.memset(by_chunk(om)[:, :, 0:1], 0.0))
                ch.tick(nc.vector.memset(by_chunk(et)[:, :, 0:1], 0.0))
                ch.tick(nc.vector.tensor_copy(by_chunk(M.C), K.ident[0:CH, 0:CH].unsqueeze(1).to_broadcast(
                    [CH, BATCH * NCH, CH])))
                ch.tick(nc.vector.memset(imp[:, :], 0.0))
                ch.wait()
                ch.tick(nc.vector.memset(by_chunk(om_s)[:, :, 0:1], 0.0))
                ch.tick(nc.vector.memset(by_chunk(et_s)[:, :, 0:1], 0.0))
                ch.tick(nc.vector.tensor_copy(by_chunk(imp)[:, :, 0:1], et0[:, :, :]))
                ch.do(nc.vector.tensor_tensor_scan(Es[:, :], et[:, :], M.C[:, :], 0.0, ALU.mult, ALU.add))
                ch.tick(nc.vector.tensor_tensor_scan(M.C[:, :], om[:, :], Es[:, :], 0.0, ALU.mult, ALU.add))
                ch.tick(nc.vector.tensor_copy(M.E_end[:, :, :], by_chunk(Es)[:, :, CH - 1:CH]))
                ch.do(nc.vector.tensor_tensor_scan(Ea[:, :], et_s[:, :], imp[:, :], 0.0, ALU.mult, ALU.add))
                ch.tick(nc.vector.tensor_copy(M.Eall_end[:, :, :], by_chunk(Ea)[:, :, CH - 1:CH]))
                ch.tick(nc.vector.tensor_copy(by_chunk(imp)[:, :, 0:1], om0[:, :, :]))
                ch.do(nc.vector.tensor_tensor_scan(M.B[:, :], om_s[:, :], Ea[:, :], 0.0, ALU.mult, ALU.add))
                ch.do(nc.vector.tensor_tensor_scan(M.A[:, :], om_s[:, :], imp[:, :], 0.0, ALU.mult, ALU.add))
        K.clear()


def memory_chunk(nc, K, M, c):
    (staged, z_done, sg_done, h_done, pred_done, dp_done, dh_done, dz_done, sums_done, sk_done, n2_done, gn_done,
     uw_done, turned, tok_done, vec, g1_done, m1_done, zr_done, hr_done, g2_done, m2_done, r_done, upd_done,
     qab_done, hab_done, ec_done, coef_staged) = K.pool[0:28]
    NB = 2 * CH
    half = lambda t, g: t[:, g * CH:(g + 1) * CH]
    now = lambda t: t[:, :, bass.ds(c * CH, CH)]
    v3 = lambda t: t.rearrange("p (g t) -> p g t", g=2)

    with nc.Block() as block:
        @block.scalar
        def _(act):
            for dst, src in ((M.kc, M.k), (M.qc, M.q), (M.vc, M.v)):
                nc.scalar.activation(v3(dst[:, :]), now(src), ACT.Identity).then_inc(staged, 1)
            act.wait_ge(z_done, 1)
            nc.scalar.activation(M.sg[:, :], K.ps[:, 0, 0:NB], ACT.Sigmoid).then_inc(sg_done, 1)
            act.wait_ge(sums_done, 1)
            nc.scalar.activation(M.sums[:, :], K.ps[:, 3, 2 * NB:4 * NB], ACT.Identity).then_inc(sk_done, 1)
            act.wait_ge(n2_done, 1)
            nc.scalar.activation(M.n2[:, :], M.n2[:, :], ACT.Sqrt).then_inc(gn_done, 1)
            act.wait_ge(zr_done, 1)
            nc.scalar.activation(M.sg[:, :], K.ps[:, 4, 0:NB], ACT.Sigmoid).then_inc(sg_done, 1)

        @block.tensor
        def _(pe):
            pe.wait_ge(staged, 1)
            for g in range(2):
                mm = nc.tensor.matmul(half(K.ps[:, 0, :], g), M.W1T_bd[:, g, :], half(M.kc, g), start=True, stop=True)
            mm.then_inc(z_done, 1)
            pe.wait_ge(qab_done, 1)
            for g in range(2):
                mm = nc.tensor.matmul(K.ps[0:CH, 7, g * 4 * CH:(g + 1) * 4 * CH], half(M.kc, g), M.q_bd[:, g, :],
                                      start=True, stop=True)
            mm.then_inc(g1_done, 1)
            pe.wait_ge(h_done, 1)
            for g in range(2):
                mm = nc.tensor.matmul(half(K.ps[:, 1, :], g), M.W2T_bd[:, g, :], half(M.h, g), start=True, stop=True)
            mm.then_inc(pred_done, 1)
            pe.wait_ge(dp_done, 1)
            for g in range(2):
                mm = nc.tensor.matmul(half(K.ps[:, 2, :], g), M.W2_bd[:, g, :], half(M.dp, g), start=True, stop=True)
            mm.then_inc(dh_done, 1)
            pe.wait_ge(dz_done, 1)
            for m, q in enumerate((M.qdz, M.qdp, M.qk, M.qh)):
                mm = nc.tensor.matmul(K.ps[:, 3, m * NB:(m + 1) * NB], M.ones_bd[:, :], q[:, :], start=True, stop=True)
            mm.then_inc(sums_done, 1)
            pe.wait_ge(uw_done, 1)
            for m, src in enumerate((M.u, M.w, M.h, M.kc)):
                for g in range(2):
                    o = (m % 2) * 256 + g * P
                    mm = nc.tensor.transpose(K.ps[0:CH, m // 2, o:o + P], half(src, g), K.ident[:, :])
            mm.then_inc(turned, 1)
            pe.wait_ge(m1_done, 1)
            pe.wait_ge(tok_done, 1)

            def retrieve(bank, W, S, m, done):
                for g in range(2):
                    o = half(K.ps[:, bank, :], g)
                    nc.tensor.matmul(o, W[:, g, :], half(M.qa, g), start=True, stop=False)
                    nc.tensor.matmul(o, S[:, g, :], half(M.qb, g), start=False, stop=False)
                    for j in range(4):
                        b = 4 * g + j
                        mm = nc.tensor.matmul(K.ps[32 * j:32 * j + 32, bank, g * CH:(g + 1) * CH], M.tok[:, m, b, :],
                                              M.m1[:, b * CH:(b + 1) * CH], start=False, stop=True,
                                              tile_position=(0, 32 * j))
                mm.then_inc(done, 1)

            retrieve(4, M.W1T_bd, M.S1T_bd, 0, zr_done)
            pe.wait_ge(ec_done, 1)
            for m, bank in ((0, 2), (1, 3)):
                for b in range(BATCH):
                    g, j = divmod(b, 4)
                    mm = nc.tensor.matmul(K.ps[32 * j:32 * j + 32, bank, g * 64:(g + 1) * 64], M.tok[:, 3 - m, b, :],
                                          M.ec[:, m, b, :], start=True, stop=True, tile_position=(0, 32 * j))
            mm.then_inc(upd_done, 1)
            pe.wait_ge(hr_done, 1)
            for g in range(2):
                mm = nc.tensor.matmul(K.ps[0:CH, 5, g * 4 * CH:(g + 1) * 4 * CH], half(M.h, g), M.q_bd[:, g, :],
                                      start=True, stop=True)
            mm.then_inc(g2_done, 1)
            pe.wait_ge(m2_done, 1)
            pe.wait_ge(hab_done, 1)
            retrieve(6, M.W2T_bd, M.S2T_bd, 1, r_done)

        @block.gpsimd
        def _(pool):
            nc.gpsimd.tensor_copy(v3(M.ac[:, :]), M.A[:, :].rearrange("p (g t) -> p g t", g=2)[:, :, bass.ds(c * CH, CH)]
                                  ).then_inc(coef_staged, 1)
            nc.gpsimd.tensor_copy(v3(M.bc[:, :]), M.B[:, :].rearrange("p (g t) -> p g t", g=2)[:, :, bass.ds(c * CH, CH)]
                                  ).then_inc(coef_staged, 1)
            nc.gpsimd.tensor_copy(v3(M.tc[:, :]), now(M.nth)).then_inc(coef_staged, 1)

        @block.vector
        def _(dve):
            ch = Chain(dve, vec)
            C_now = M.C[:, :].rearrange("p (b t) -> p b t", b=BATCH)[:, :, bass.ds(c * CH, CH)]
            bd4 = lambda t: t.unsqueeze(2).to_broadcast([P, 2, 4, t.shape[-1]])

            def diagonal(dst, src):
                n = src.shape[-1]
                return nc.vector.tensor_tensor(dst[:, :, :].rearrange("p g (j n) -> p g j n", j=4), bd4(src),
                                               M.blocks[:, :, :, 0:n], ALU.mult)

            ends = lambda t, parts: t[:, :, :].rearrange("p (b n) o -> p b (n o)", n=NCH)[:, :, bass.ds(c, 1)]
            ch.tick(nc.vector.tensor_copy(M.e_end[:, :, :], ends(M.E_end, CH)))
            ch.tick(nc.vector.tensor_copy(M.eall_end[:, :, :], ends(M.Eall_end, P)))
            dve.wait_ge(staged, 2)
            diagonal(M.q_bd, v3(M.qc[:, :])).then_inc(qab_done, 1)
            ch.tick(nc.vector.tensor_tensor(M.qk[:, :], M.kc[:, :], M.kc[:, :], ALU.mult))
            dve.wait_ge(coef_staged, 3)
            ch.tick(nc.vector.tensor_tensor(M.qa[:, :], M.qc[:, :], M.ac[:, :], ALU.mult))
            ch.tick(nc.vector.tensor_tensor(M.qb[:, :], M.qc[:, :], M.bc[:, :], ALU.mult))
            dve.wait_ge(sg_done, 1)
            nc.vector.tensor_tensor(M.h[:, :], K.ps[:, 0, 0:NB], M.sg[:, :], ALU.mult).then_inc(h_done, 1)
            dve.wait_ge(h_done, 1)
            ch.tick(nc.vector.tensor_tensor(M.t1[:, :], M.h[:, :], M.sg[:, :], ALU.mult))
            ch.tick(nc.vector.tensor_tensor(M.ds[:, :], M.h[:, :], M.sg[:, :], ALU.add))
            ch.tick(nc.vector.tensor_tensor(M.qh[:, :], M.h[:, :], M.h[:, :], ALU.mult))
            ch.wait()
            ch.tick(nc.vector.tensor_tensor(M.ds[:, :], M.ds[:, :], M.t1[:, :], ALU.subtract))
            dve.wait_ge(pred_done, 1)
            dve.wait_ge(staged, 3)
            ch.do(nc.vector.tensor_tensor(M.dp[:, :], K.ps[:, 1, 0:NB], M.vc[:, :], ALU.subtract))
            nc.vector.tensor_scalar(M.dp[:, :], M.dp[:, :], 0.2, None, ALU.mult).then_inc(dp_done, 1)
            dve.wait_ge(dp_done, 1)
            ch.tick(nc.vector.tensor_tensor(M.qdp[:, :], M.dp[:, :], M.dp[:, :], ALU.mult))
            dve.wait_ge(dh_done, 1)
            ch.do(nc.vector.tensor_tensor(M.dz[:, :], K.ps[:, 2, 0:NB], M.ds[:, :], ALU.mult))
            nc.vector.tensor_tensor(M.qdz[:, :], M.dz[:, :], M.dz[:, :], ALU.mult).then_inc(dz_done, 1)
            dve.wait_ge(g1_done, 1)
            m1 = M.m1[:, :].rearrange("p (b t) -> p b t", b=BATCH)
            nc.vector.tensor_tensor(m1, K.ps[0:CH, 7, :].rearrange("p (b t) -> p b t", b=BATCH), C_now,
                                    ALU.mult).then_inc(m1_done, 1)
            dve.wait_ge(sk_done, 1)
            ch.do(nc.vector.tensor_tensor(M.sums[:, :], K.ps[:, 3, 0:2 * NB], M.sums[:, :], ALU.mult))
            nc.vector.tensor_tensor(M.n2[:, :], M.sums[:, 0:NB], M.sums[:, NB:2 * NB], ALU.add).then_inc(n2_done, 1)
            dve.wait_ge(gn_done, 1)
            ch.do(nc.vector.tensor_scalar(M.n2[:, :], M.n2[:, :], 1e-6, None, ALU.max))
            ch.do(nc.vector.reciprocal(M.n2[:, :], M.n2[:, :]))
            ch.do(nc.vector.scalar_tensor_tensor(M.n2[:, :], M.n2[:, :], 1.0, M.tc[:, :], ALU.min, ALU.mult))
            ch.do(nc.vector.tensor_tensor(M.u[:, :], M.dz[:, :], M.n2[:, :], ALU.mult))
            nc.vector.tensor_tensor(M.w[:, :], M.dp[:, :], M.n2[:, :], ALU.mult).then_inc(uw_done, 1)
            dve.wait_ge(turned, 1)
            nc.vector.tensor_copy(M.tok[:, :, :, :], K.ps[0:CH, 0:2, :].rearrange(
                "p a (m b d) -> p (a m) b d", m=2, b=BATCH)).then_inc(tok_done, 1)
            dve.wait_ge(tok_done, 1)
            c_end = M.C[:, :].rearrange("p (b t) -> p b t", b=BATCH)[:, :, bass.ds(c * CH + CH - 1, 1)].to_broadcast(
                [CH, BATCH, 32])
            for m in range(2):
                ch.tick(nc.vector.tensor_tensor(M.ec[:, m, :, 0:32], M.tok[:, m, :, :],
                                                M.e_end[:, :, :].to_broadcast([CH, BATCH, 32]), ALU.mult))
                i = nc.vector.tensor_tensor(M.ec[:, m, :, 32:64], M.tok[:, m, :, :], c_end, ALU.mult)
                if m == 0:
                    ch.tick(i)
                else:
                    i.then_inc(ec_done, 1)
            ch.wait()
            dve.wait_ge(ec_done, 1)
            dve.wait_ge(sg_done, 2)
            ch.do(nc.vector.tensor_tensor(M.hr[:, :], K.ps[:, 4, 0:NB], M.sg[:, :], ALU.mult))
            diagonal(M.q_bd, v3(M.hr[:, :])).then_inc(hr_done, 1)
            ch.tick(nc.vector.tensor_tensor(M.qa[:, :], M.hr[:, :], M.ac[:, :], ALU.mult))
            nc.vector.tensor_tensor(M.qb[:, :], M.hr[:, :], M.bc[:, :], ALU.mult).then_inc(hab_done, 1)
            ch.wait()
            dve.wait_ge(g2_done, 1)
            nc.vector.tensor_tensor(m1, K.ps[0:CH, 5, :].rearrange("p (b t) -> p b t", b=BATCH), C_now,
                                    ALU.mult).then_inc(m2_done, 1)
            dve.wait_ge(upd_done, 1)
            a_end = v3(M.ac[:, :])[:, :, CH - 1:CH].to_broadcast([P, 2, 32])
            b_end = v3(M.bc[:, :])[:, :, CH - 1:CH].to_broadcast([P, 2, 32])
            e_end = M.eall_end[:, :, :].to_broadcast([P, 2, 32])
            for W, S, bank in ((M.W1T, M.S1T, 2), (M.W2T, M.S2T, 3)):
                new = K.ps[:, bank, 0:P].rearrange("p (g x) -> p g x", g=2)
                ch.tick(nc.vector.tensor_tensor(W[:, :, :], W[:, :, :], a_end, ALU.mult))
                ch.do(nc.vector.tensor_tensor(M.t2[:, :, :], S[:, :, :], b_end, ALU.mult))
                ch.tick(nc.vector.tensor_tensor(W[:, :, :], W[:, :, :], M.t2[:, :, :], ALU.add))
                ch.do(nc.vector.tensor_tensor(S[:, :, :], S[:, :, :], e_end, ALU.mult))
                ch.tick(nc.vector.tensor_tensor(W[:, :, :], W[:, :, :], new[:, :, 32:64], ALU.add))
                ch.do(nc.vector.tensor_tensor(S[:, :, :], S[:, :, :], new[:, :, 0:32], ALU.add))
            ch.do(nc.vector.transpose(M.W2[:, :, :].rearrange("p b d -> p (b d)"),
                                      M.W2T[:, :, :].rearrange("p b d -> p (b d)")))
            dve.wait_ge(r_done, 1)
            for dst, src in ((M.W1T_bd, M.W1T), (M.W2T_bd, M.W2T), (M.W2_bd, M.W2), (M.S1T_bd, M.S1T),
                             (M.S2T_bd, M.S2T)):
                diagonal(dst, src[:, :, :])
            nc.vector.tensor_copy(now(M.ret), v3(K.ps[:, 6, 0:NB]))
    K.clear()


def memory_output(nc, K, M, g, out):
    landed, staged, projected, vec, ms_ready, rs_ready, done, stored = K.pool[0:8]
    of = lambda a, j: a.rearrange("(g j) (t p) d -> j g p t d", j=4, p=P)[j, g]
    with ExitStack() as tmp:
        x, fac = [sbuf(nc, tmp, n, [P, 4, NT, D]) for n in ("x_back", "fac_back")]
        rc = sbuf(nc, tmp, "rc", [P, T])
        var, rstd = [sbuf(nc, tmp, n, [P, 4, NT]) for n in ("out_var", "out_rstd")]
        with nc.Block() as block:
            @block.sync
            def _(sp):
                for j in range(4):
                    sp.dma_start(x[:, j, :, :], of(K.x_d, j)).then_inc(landed, 16)
                    sp.dma_start(fac[:, j, :, :], of(K.fac_d, j)).then_inc(landed, 16)
                    sp.wait_ge(landed, 32 * (j + 1))
                for j in range(4):
                    sp.wait_ge(done, j + 1)
                    sp.dma_start(of(out, j), x[:, j, :, :]).then_inc(stored, 16)
                sp.wait_ge(stored, 64)

            @block.scalar
            def _(act):
                nc.scalar.activation(rc[:, :], M.ret[:, bass.ds(g, 1), :].rearrange("p b t -> p (b t)"),
                                     ACT.Identity).then_inc(staged, 1)

            @block.tensor
            def _(pe):
                pe.wait_ge(staged, 1)
                for j in range(4):
                    q = slice(32 * j, 32 * j + 32)
                    for t in range(NT):
                        mm = nc.tensor.matmul(K.ps[:, j, t * P:(t + 1) * P], rc[q, t * P:(t + 1) * P], M.wo[q, :],
                                              start=True, stop=True, tile_position=(32 * j, 0))
                    mm.then_inc(projected, 1)

            @block.vector
            def _(dve):
                ch = Chain(dve, vec)
                for j in range(4):
                    dve.wait_ge(projected, j + 1)
                    for t in range(NT):
                        ch.tick(nc.vector.bn_stats(K.stats[:, t, :], K.ps[:, j, t * P:(t + 1) * P]))
                    ch.wait()
                    for t in range(NT):
                        ch.tick(nc.vector.bn_aggr(K.mv[:, t, :], K.stats[:, t, :]))
                    ch.wait()
                    ch.do(nc.vector.tensor_tensor(var[:, j, :], K.mv[:, :, 0], K.mv[:, :, 0], ALU.mult))
                    nc.vector.scalar_tensor_tensor(var[:, j, :], K.mv[:, :, 1], 1e-6, var[:, j, :],
                                                   ALU.add, ALU.add).then_inc(ms_ready, 1)
                    dve.wait_ge(ms_ready, j + 1)
                for j in range(4):
                    dve.wait_ge(rs_ready, j + 1)
                    dve.wait_ge(landed, 32 * (j + 1))
                    for t in range(NT):
                        ch.tick(nc.vector.scalar_tensor_tensor(fac[:, j, t, :], K.ps[:, j, t * P:(t + 1) * P],
                                                               rstd[:, j, t:t + 1], fac[:, j, t, :], ALU.mult,
                                                               ALU.mult))
                    ch.wait()
                    nc.vector.tensor_tensor(x[:, j, :, :], x[:, j, :, :], fac[:, j, :, :], ALU.add).then_inc(done, 1)

            @block.gpsimd
            def _(pool):
                for j in range(4):
                    pool.wait_ge(ms_ready, j + 1)
                    nc.gpsimd.tensor_tensor(rstd[:, j, :], var[:, j, :], K.neghalf[:, 0:NT],
                                            ALU.pow).then_inc(rs_ready, 1)
        K.clear()




def rope_tables():
    theta = (np.float32(10000.0) ** (-2.0 * np.arange(HD // 2, dtype=np.float32) / HD)).astype(np.float32)
    ang = np.outer(np.arange(T, dtype=np.float32), theta).astype(np.float32).astype(np.float64)
    cos = np.repeat(np.cos(ang), 2, axis=1).astype(np.float32)
    sin = np.stack([-np.sin(ang), np.sin(ang)], axis=1).astype(np.float32)
    return (np.ascontiguousarray(cos.reshape(NT, P, HD).transpose(1, 0, 2)),
            np.ascontiguousarray(sin.reshape(NT, P, 2, HD // 2).transpose(1, 0, 2, 3)))


def xpos_tables():
    half = np.arange(0, LD, 2, dtype=np.float32)
    inv = (np.float32(1.0) / np.float32(10000.0) ** (half / np.float32(LD))).astype(np.float32)
    t = np.arange(T, dtype=np.float32)
    fr = (t[:, None] * inv[None, :]).astype(np.float32)
    fr = np.concatenate([fr, fr], axis=1).astype(np.float64)
    base = ((half + np.float32(0.4 * LD)) / np.float32(1.4 * LD)).astype(np.float32)
    power = ((t - T // 2) / np.float32(WIN // 2)).astype(np.float32)
    sc = base[None, :].astype(np.float64) ** power[:, None]
    sc = np.concatenate([sc, sc], axis=1)
    sign = np.where(np.arange(LD) < LD // 2, -1.0, 1.0)
    tabs = np.stack([np.cos(fr) * sc, np.sin(fr) * sc * sign, np.cos(fr) / sc, np.sin(fr) / sc * sign])
    return np.ascontiguousarray(tabs.reshape(4, NT, P, LD).transpose(2, 0, 1, 3).astype(np.float32))


def masks():
    r, c = np.arange(P)[:, None], np.arange(P)[None, :]
    mq = np.where(c > r, NEG, 0.0).astype(np.float32)
    c = np.arange(P + WIN)[None, :]
    band = np.where((c < r) | (c > r + WIN), NEG, 0.0).astype(np.float32)
    band0 = np.where(c < WIN, NEG, band).astype(np.float32)
    return np.concatenate([np.eye(P, dtype=np.float32), mq, mq.T, band, band0], axis=1)


def build_kernel(nc, A, out):
    NAMED.clear()
    with ExitStack() as ctx:
        K = Kit(nc, ctx)
        K.ps = ctx.enter_context(nc.psum_tensor("banks", [P, 8, 512], F32))
        K.x_d = nc.dram_tensor("x_scratch", [BATCH, T, D], F32, kind="Internal").ap()
        K.fac_d = nc.dram_tensor("factor_scratch", [BATCH, T, D], F32, kind="Internal").ap()
        K.parts_d = nc.dram_tensor("parts_scratch", [2, 3, H * HD, T], BF16, kind="Internal").ap()
        K.nmax_d = nc.dram_tensor("maxima_scratch", [2, H, T], BF16, kind="Internal").ap()
        K.ones_d = nc.dram_tensor("ones_scratch", [2, H, T], BF16, kind="Internal").ap()
        K.kvq_d = nc.dram_tensor("kvq_scratch", [BATCH, 96, T], F32, kind="Internal").ap()
        K.aet_d = nc.dram_tensor("aet_scratch", [BATCH, 96, T], F32, kind="Internal").ap()

        def sb(name, shape, dt=F32, c=ctx):
            return sbuf(nc, c, name, shape, dt)

        K.ident = sb("ident", [P, P])
        K.neghalf = sb("neghalf", [P, 2 * NT * LH])
        K.stats = sb("stats", [P, NT, 6])
        K.mv = sb("mv", [P, NT, 2])
        K.var = sb("var", [P, NT])
        K.rstd = sb("rstd", [P, NT])
        with ExitStack() as loop:
            batch_loop(nc, K, loop, A, out)
        with ExitStack() as mem:
            memory(nc, K, mem, A, out)


def batch_loop(nc, K, ctx, A, out):
    def sb(name, shape, dt=F32):
        return sbuf(nc, ctx, name, shape, dt)

    loads = []

    def whole(name, src=None, bc=False):
        src = A[name] if src is None else src
        shape = ([P] + list(src.shape)) if bc else list(src.shape)
        t = sb(name + "_s", shape)
        ap = src.partition_broadcast(P) if bc else src
        full = tuple(slice(None) for _ in shape)
        loads.append((t[full], ap[full] if not bc else ap))
        return t

    K.w0_qkv = whole("w0_qkv")
    K.b0_qkv = whole("b0_qkv", bc=True)
    K.w0_1, K.w0_2, K.w0_h1, K.w0_h2, K.w0_3 = [whole(n) for n in ("w0_1", "w0_2", "w0_h1", "w0_h2", "w0_3")]
    K.s0_1, K.s0_2, K.s0_h1, K.s0_h2 = [whole(n) for n in ("s0_1", "s0_2", "s0_h1", "s0_h2")]
    K.s0_3 = whole("s0_3", bc=True)
    K.w1_q, K.w1_k, K.w1_v, K.w1_o = [whole(n) for n in ("w1_q", "w1_k", "w1_v", "w1_o")]
    K.w_gu = sb("w_gu", [P, 2 * I1])
    K.w_down = sb("w_down", [P, 3, D])
    K.w2_q, K.w2_k, K.w2_v, K.w2_ao = [whole(n) for n in ("w2_q", "w2_k", "w2_v", "w2_ao")]
    K.b2_q, K.b2_k = whole("b2_q"), whole("b2_k")
    K.b2_v, K.b2_ao, K.rmsw = [whole(n, bc=True) for n in ("b2_v", "b2_ao", "rmsw")]
    K.w2_qkv, K.w2_o, K.w2_up, K.w2_down, K.b2_up, K.b2_down, K.ln2_g, K.ln2_b = [], [], [], [], [], [], [], []
    for L in range(2):
        K.w2_qkv.append(whole(f"w2_qkv{L}"))
        K.w2_o.append(whole(f"w2_o{L}"))
        K.w2_up.append(whole(f"w2_up{L}"))
        K.b2_up.append(whole(f"b2_up{L}"))
        K.b2_down.append(whole(f"b2_down{L}", bc=True))
        K.ln2_g.append(whole(f"ln2_g{L}"))
        K.ln2_b.append(whole(f"ln2_b{L}"))
        w = sb(f"w2_down{L}_s", [P, 3, D])
        n = HID2 - 2 * P
        loads.append((w[:, 0:2, :], A[f"w2_down{L}"][0:2 * P, :].rearrange("(c p) d -> p c d", p=P)))
        loads.append((w[0:n, 2, :], A[f"w2_down{L}"][2 * P:HID2, :]))
        K.w2_down.append(w)
    K.w3_up, K.w3_down, K.w3_gate, K.w3_kvq, K.w3_aet, K.w3_g = [
        whole(n) for n in ("w3_up", "w3_down", "w3_gate", "w3_kvq", "w3_aet", "w3_g")]
    K.g3_b, K.norm3 = whole("g3_b", bc=True), whole("norm3", bc=True)
    K.conv_w, K.conv_b, K.b3_aet = whole("conv_w"), whole("conv_b"), whole("b3_aet")

    cos, sin = rope_tables()
    K.rope_cos = whole("rope_cos", nc.inline_tensor(cos, name="rope_cos_c").ap())
    K.rope_sin = whole("rope_sin", nc.inline_tensor(sin, name="rope_sin_c").ap())
    K.iota8 = whole("iota8", nc.inline_tensor(np.arange(E3, dtype=np.float32), name="iota8_c").ap(), bc=True)
    K.cosq, K.sinq, K.cosk, K.sink = [[sb(f"{n}{L}", [P, NT, LD]) for L in range(2)]
                                      for n in ("cosq", "sinq", "cosk", "sink")]
    K.x, K.xn, K.att, K.g = [sb(n, [P, NT, D]) for n in ("x", "xn", "att", "g")]
    K.v32 = sb("v32", [P, NT, H, 32])
    K.xnT = sb("xnT", [P, T])
    K.identb = sb("identb", [P, P], BF16)
    K.mask_q = sb("mask_q", [P, P], BF16)
    K.mask_k = sb("mask_k", [P, P], BF16)
    K.mask_band = sb("mask_band", [P, P + WIN], BF16)
    K.mask_band0 = sb("mask_band0", [P, P + WIN], BF16)
    fills = [(K.neghalf[:, :], -0.5), (K.v32[:, :, :, :], 0.0),
             (K.v32[:, :, :, HD:HD + 1], 1.0)]
    with ExitStack() as tmp:
        consts = masks()
        ct = sbuf(nc, tmp, "consts", [P, consts.shape[1]])
        tabs = sbuf(nc, tmp, "tabs", [P, 4, NT, LD])
        qks = sbuf(nc, tmp, "qks", [P, 2, 4, LD])
        ones = sbuf(nc, tmp, "ones_rows", [2, H, T], BF16)
        K.gate_rows, K.up_rows = [sbuf(nc, tmp, n, [P, 3, D]) for n in ("gate_rows", "up_rows")]
        K.down_rows = sbuf(nc, tmp, "down_rows", [P, I1])
        loads.append((ct[:, :], nc.inline_tensor(consts, name="masks_c").ap()))
        loads.append((K.ident[:, :], nc.inline_tensor(np.eye(P, dtype=np.float32), name="ident_c").ap()))
        loads.append((tabs[:, :, :, :], nc.inline_tensor(xpos_tables(), name="xpos_c").ap()))
        loads.append((qks[:, :, :, :], A["qk_scales"].partition_broadcast(P)))
        for t, n in ((K.gate_rows, "w_gate"), (K.up_rows, "w_up")):
            loads.append((t[:, 0:2, :], A[n][0:2 * P, :].rearrange("(c p) d -> p c d", p=P)))
            loads.append((t[0:I1 - 2 * P, 2, :], A[n][2 * P:I1, :]))
        loads.append((K.down_rows[:, :], A["w_downr"]))
        load_constants(nc, K, loads)
        filled, vec, ones_stored = K.pool[0:3]
        with nc.Block() as block:
            @block.sync
            def _(sp):
                sp.wait_ge(filled, 1)
                sp.dma_start(K.ones_d, ones[:, :, :]).then_inc(ones_stored, 16)
                sp.wait_ge(ones_stored, 16)

            @block.vector
            def _(dve):
                ch = Chain(dve, vec)
                nc.vector.memset(ones[:, :, :], 1.0).then_inc(filled, 1)
                for dst, value in fills:
                    ch.do(nc.vector.memset(dst, value))
                o = 0
                for t in (K.identb, K.mask_q, K.mask_k, K.mask_band, K.mask_band0):
                    n = t.shape[1]
                    nc.vector.tensor_copy(t[:, :], ct[:, o:o + n])
                    o += n
                for L in range(2):
                    for m, t in enumerate((K.cosq[L], K.sinq[L], K.cosk[L], K.sink[L])):
                        nc.vector.tensor_tensor(t[:, :, :], tabs[:, m, :, :],
                                                qks[:, L, m, :].unsqueeze(1).to_broadcast([P, NT, LD]), ALU.mult)
        K.clear()
        quantize_weights(nc, K, tmp)

    with nc.Fori(0, BATCH) as b:
        def rows():
            c = ExitStack()
            K.qs = sbuf(nc, c, "qs", [P, H, T], BF16)
            K.ks = sbuf(nc, c, "ks", [P, H, T], BF16)
            return c

        with rows():
            with ExitStack() as prep:
                K.parts = sbuf(nc, prep, "parts", [P, 2, 3, T], BF16)
                prepare(nc, K, 0, A["x"][b, :, :].rearrange("(t p) d -> p t d", p=P))
                attention(nc, K, False, beside=TernaryFfn(nc, K, prep))
        with rows():
            with ExitStack() as prep:
                K.parts = sbuf(nc, prep, "parts", [P, 2, 3, T], BF16)
                prepare(nc, K, 1)
                attention(nc, K, True, K.w1_o, beside=Fp4Ffn(nc, K, prep))
        with ExitStack() as two:
            K.xr, K.y = [sbuf(nc, two, n, [P, NT, D]) for n in ("xr", "y")]
            K.shT = sbuf(nc, two, "shT", [P, T])
            with ExitStack() as prep:
                K.xrT = sbuf(nc, prep, "xrT", [P, T])
                K.parts = sbuf(nc, prep, "parts", [P, 2, 3, T], BF16)
                prepare(nc, K, 2)
                local_sublayer(nc, K, 0)
            with rows() as both:
                attention(nc, K, True, K.w2_ao, K.b2_ao, combine=False, beside=Glu(nc, K, both, 0, False))
            local_sublayer(nc, K, 1)
            with ExitStack() as tmp:
                run_alone(nc, K, Glu(nc, K, tmp, 1, True))
            gate_residual(nc, K)
        layer_norm(nc, K)
        with ExitStack() as three:
            K.y = sbuf(nc, three, "y3", [P, NT, D])
            experts(nc, K)
            memory_inputs(nc, K, b)


class Memory:
    pass


def memory(nc, K, ctx, A, out):
    M = Memory()

    def sb(name, shape, dt=F32):
        return sbuf(nc, ctx, name, shape, dt)

    M.wo = sb("wo3", [P, P])
    M.mw = sb("mw", [P, 3, 32])
    M.mean_w = sb("mean_w", [96, 3, CH])
    M.ones_bd = sb("ones_bd", [P, P])
    M.blocks = sb("blocks", [P, 2, 4, CH])
    M.W1T, M.W2T, M.W2, M.S1T, M.S2T = [sb(n, [P, 2, 32]) for n in ("W1T", "W2T", "W2", "S1T", "S2T")]
    M.W1T_bd, M.W2T_bd, M.W2_bd, M.S1T_bd, M.S2T_bd = [
        sb(n + "_bd", [P, 2, P]) for n in ("W1T", "W2T", "W2", "S1T", "S2T")]
    M.k, M.v, M.q, M.ret, M.nth = [sb(n, [P, 2, T]) for n in ("k_all", "v_all", "q_all", "ret", "nth")]
    M.C = sb("C", [CH, BATCH * T])
    M.A, M.B = [sb(n, [P, 2 * T]) for n in ("A_all", "B_all")]
    M.E_end = sb("E_end", [CH, BATCH * NCH, 1])
    M.Eall_end = sb("Eall_end", [P, 2 * NCH, 1])
    mean = np.full((96, 3, CH), 0.0, np.float32)
    for m in range(3):
        mean[32 * m:32 * m + 32, m, :] = 1.0 / 32
    ones = np.kron(np.eye(4, dtype=np.float32), np.ones((32, 32), np.float32))
    blocks = np.kron(np.eye(4, dtype=np.float32), np.ones((32, CH), np.float32)).reshape(P, 1, 4, CH)
    blocks = np.ascontiguousarray(np.concatenate([blocks, blocks], axis=1))
    loads = [(M.mean_w[:, :, :], nc.inline_tensor(mean, name="mean_c").ap()),
             (M.ones_bd[:, :], nc.inline_tensor(ones, name="ones_bd_c").ap()),
             (M.blocks[:, :, :, :], nc.inline_tensor(blocks, name="blocks_c").ap())]
    for j in range(4):
        q = slice(32 * j, 32 * j + 32)
        loads += [(M.wo[q, :], A["w3_o"]), (M.mw[q, :, :], A["mem_w"])]
    load_constants(nc, K, loads)
    copied, = K.pool[0:1]
    with nc.Block() as block:
        @block.vector
        def _(dve):
            ch = Chain(dve, copied)
            for m, t in enumerate((M.W1T, M.W2T, M.W2)):
                ch.tick(nc.vector.tensor_copy(t[:, :, :], M.mw[:, m, :].unsqueeze(1).to_broadcast([P, 2, 32])))
            for t in (M.S1T, M.S2T):
                nc.vector.memset(t[:, :, :], 0.0)
            for t in (M.S1T_bd, M.S2T_bd):
                nc.vector.memset(t[:, :, :], 0.0)
            ch.wait()
            for dst, src in ((M.W1T_bd, M.W1T), (M.W2T_bd, M.W2T), (M.W2_bd, M.W2)):
                nc.vector.tensor_tensor(dst[:, :, :].rearrange("p g (j n) -> p g j n", j=4),
                                        src[:, :, :].unsqueeze(2).to_broadcast([P, 2, 4, 32]),
                                        M.blocks[:, :, :, 0:32], ALU.mult)
    K.clear()
    memory_coefficients(nc, K, M)
    with ExitStack() as tmp:
        names = ("kc", "vc", "qc", "sg", "h", "dp", "ds", "dz", "t1", "qk", "qh", "qdp", "qdz", "n2", "u", "w", "hr",
                 "qa", "qb", "ac", "bc", "tc")
        (M.kc, M.vc, M.qc, M.sg, M.h, M.dp, M.ds, M.dz, M.t1, M.qk, M.qh, M.qdp, M.qdz, M.n2, M.u, M.w, M.hr,
         M.qa, M.qb, M.ac, M.bc, M.tc) = [sbuf(nc, tmp, n, [P, 2 * CH]) for n in names]
        M.sums = sbuf(nc, tmp, "sums", [P, 4 * CH])
        M.q_bd = sbuf(nc, tmp, "q_bd", [P, 2, 4 * CH])
        M.m1 = sbuf(nc, tmp, "m1", [CH, BATCH * CH])
        M.tok = sbuf(nc, tmp, "tok", [CH, 4, BATCH, 32])
        M.ec = sbuf(nc, tmp, "ec", [CH, 2, BATCH, 64])
        M.t2 = sbuf(nc, tmp, "t2", [P, 2, 32])
        M.e_end = sbuf(nc, tmp, "e_end", [CH, BATCH, 1])
        M.eall_end = sbuf(nc, tmp, "eall_end", [P, 2, 1])
        with nc.Fori(0, NCH) as c:
            memory_chunk(nc, K, M, c)
    with nc.Fori(0, 2) as g:
        memory_output(nc, K, M, g, out)




def lay_out(i):
    c = np.ascontiguousarray
    t = {}
    j = lambda *n: np.concatenate([np.asarray(i[k]) for k in n], axis=0)
    col = lambda v: c(np.asarray(v).reshape(-1, P).T)
    tiles = lambda w: c(np.asarray(w).reshape(-1, P, w.shape[-1]).transpose(1, 0, 2))
    T_ = lambda n: c(np.asarray(i[n]).T)
    t["x"] = c(np.asarray(i["L0_attn_x"]))
    t["w0_qkv"] = c(j("L0_attn_wq_w", "L0_attn_wk_w", "L0_attn_wv_w").T)
    t["b0_qkv"] = j("L0_attn_wq_b", "L0_attn_wk_b", "L0_attn_wv_b")
    t["w0_1"], t["w0_2"] = T_("L0_ffn_w1_w"), T_("L0_ffn_w2_w")
    t["w0_h1"], t["w0_h2"], t["w0_3"] = tiles(T_("L0_ffn_h1_w")), tiles(T_("L0_ffn_h2_w")), tiles(T_("L0_ffn_w3_w"))
    t["s0_1"], t["s0_2"] = col(i["L0_ffn_w1_s"]), col(i["L0_ffn_w2_s"])
    t["s0_h1"], t["s0_h2"] = col(i["L0_ffn_h1_s"]), col(i["L0_ffn_h2_s"])
    t["s0_3"] = c(i["L0_ffn_w3_s"])
    t["w1_q"], t["w1_k"], t["w1_v"], t["w1_o"] = [T_("L1_attn_W" + n) for n in "qkvo"]
    t["w_gate"], t["w_up"], t["w_downr"] = c(i["L1_ffn_w_gate"]), c(i["L1_ffn_w_up"]), c(i["L1_ffn_w_down"])
    t["w2_q"], t["w2_k"], t["w2_v"], t["w2_ao"] = [T_("L2_attn_W" + n) for n in "qkvo"]
    t["b2_q"], t["b2_k"] = col(i["L2_attn_bq"]), col(i["L2_attn_bk"])
    t["b2_v"], t["b2_ao"], t["rmsw"] = c(i["L2_attn_bv"]), c(i["L2_attn_bo"]), c(i["L2_attn_norm_w"])
    half = LD // 2
    sc = []
    for L in range(2):
        t[f"w2_qkv{L}"] = c(i["L2_ffn_wqkv"][L])
        t[f"w2_o{L}"] = tiles(c(i["L2_ffn_wo"][L]))
        t[f"w2_up{L}"] = c(i["L2_ffn_w1"][L])
        t[f"w2_down{L}"] = c(i["L2_ffn_w2"][L])
        b1 = np.asarray(i["L2_ffn_b1"][L])
        up = np.zeros((6, P), b1.dtype)
        for m in range(2):
            up[3 * m:3 * m + 3].reshape(-1)[:HID2] = b1[m * HID2:(m + 1) * HID2]
        t[f"b2_up{L}"] = c(up.T)
        t[f"b2_down{L}"] = c(i["L2_ffn_b2"][L])
        t[f"ln2_g{L}"], t[f"ln2_b{L}"] = col(i["L2_ffn_ln_g"][L]), col(i["L2_ffn_ln_b"][L])
        q, k = np.asarray(i["L2_ffn_q_scale"][L]), np.asarray(i["L2_ffn_k_scale"][L])
        sc.append(np.stack([q, np.concatenate([q[half:], q[:half]]), k, np.concatenate([k[half:], k[:half]])]))
    t["qk_scales"] = c(np.stack(sc))
    t["w3_up"] = c(np.asarray(i["L3_ffn_w12"]).transpose(2, 0, 1))
    t["w3_down"] = c(np.asarray(i["L3_ffn_w3"]).transpose(2, 0, 1).reshape(2, P, E3, D).transpose(1, 2, 0, 3))
    t["w3_gate"] = T_("L3_ffn_gate_w")
    t["w3_kvq"] = c(j("L3_attn_Wk", "L3_attn_Wv", "L3_attn_Wq").T)
    t["w3_aet"] = c(j("L3_attn_aW", "L3_attn_eW", "L3_attn_tW").T)
    t["w3_g"] = T_("L3_attn_gW")
    t["g3_b"], t["norm3"] = c(i["L3_attn_gb"]), c(i["L3_attn_norm_g"])
    t["conv_w"] = j("L3_attn_ckw", "L3_attn_cvw", "L3_attn_cqw")
    t["conv_b"] = j("L3_attn_ckb", "L3_attn_cvb", "L3_attn_cqb").reshape(96, 1)
    t["b3_aet"] = j("L3_attn_ab", "L3_attn_eb", "L3_attn_tb").reshape(96, 1)
    t["w3_o"] = T_("L3_attn_Wo")
    w1, w2 = np.asarray(i["L3_attn_mW1"]), np.asarray(i["L3_attn_mW2"])
    t["mem_w"] = c(np.stack([w1.T, w2.T, w2], axis=1))
    return t


def kernel(**inputs):
    import concourse.bacc as _bacc
    from concourse.bass_utils import run_bass_kernel_spmd as _run

    nc = _bacc.Bacc("TRN2", target_bir_lowering=False, num_devices=1)
    arrays = {f"in_{n}": np.ascontiguousarray(a) for n, a in lay_out(inputs).items()}
    A = {n[3:]: nc.dram_tensor(n, a.shape, mybir.dt.from_np(a.dtype), kind="ExternalInput").ap()
         for n, a in arrays.items()}
    out = nc.dram_tensor("out_0", (BATCH, T, D), F32, kind="ExternalOutput").ap()
    build_kernel(nc, A, out)
    r = _run(nc, [arrays], core_ids=[0])
    return r.results[0]["out_0"]
```

```python
from contextlib import ExitStack

import numpy as np

import concourse.bass as bass
from concourse import mybir

F32 = mybir.dt.float32
BF16 = mybir.dt.bfloat16
U32 = mybir.dt.uint32
ALU = mybir.AluOpType
ACT = mybir.ActivationFunctionType
AX = mybir.AxisListType

P = 128
BATCH, T, D = 8, 512, 128
NT = T // P
H, HD = 16, 8
NG = H // 4
EPS_LN = 1e-5
NEG = -1.0e30
HID0 = 512
I1, BLK = 352, 16
INNER, LH, LD, WIN, HID2 = 512, 8, 64, 64, 341
DM, CH = 32, 64
E3, H3 = 8, 256
NCH = T // CH
PREPARED = -11
POOL = 56


class Chain:

    def __init__(self, eng, sem):
        self.eng, self.sem, self.n = eng, sem, 0

    def tick(self, ins):
        self.n += 1
        ins.then_inc(self.sem, 1)

    def wait(self):
        if self.n:
            self.eng.wait_ge(self.sem, self.n)

    def do(self, ins):
        self.tick(ins)
        self.wait()


class Kit:

    def __init__(self, nc, ctx):
        self.nc = nc
        self.pool = [ctx.enter_context(nc.semaphore(f"sig{i}")) for i in range(POOL)]
        self.saved = ctx.enter_context(nc.semaphore("parts_saved"))
        self.spread = ctx.enter_context(nc.semaphore("parts_spread"))
        self.factor_stored = ctx.enter_context(nc.semaphore("factor_stored"))
        first = self.pool[0].num
        assert [s.num for s in self.pool + [self.saved, self.spread, self.factor_stored]] == list(range(first, first + POOL + 3))

    def clear(self, spread=False):
        first = self.pool[0].num
        self.nc.vector.sem_clear(range(first, first + (POOL + 3 if spread else POOL)))
        self.nc.all_engine_barrier()


NAMED = {}


def sbuf(nc, ctx, name, shape, dt=F32):
    NAMED[name] = NAMED.get(name, 0) + 1
    if NAMED[name] > 1:
        name = f"{name}_{NAMED[name]}"
    return ctx.enter_context(nc.sbuf_tensor(name, shape, dt))




def load_constants(nc, K, loads):
    landed = K.pool[0]
    with nc.Block() as block:
        @block.sync
        def _(sp):
            for dst, src in loads[0::2]:
                sp.dma_start(dst, src).then_inc(landed, 16)
            sp.wait_ge(landed, 16 * len(loads))

        @block.scalar
        def _(act):
            for dst, src in loads[1::2]:
                act.dma_start(dst, src).then_inc(landed, 16)
    K.clear()


def fp4_blocks(nc, ch, V, Q, a, acc, sc, rs, npart, n):
    nb = n // BLK
    v = V.rearrange("p (b k) -> p b k", k=BLK)
    q = Q.rearrange("p (b k) -> p b k", k=BLK)
    A = a[0:npart, 0:n]
    C = acc[0:npart, 0:n]
    s, r = sc[0:npart, 0:nb], rs[0:npart, 0:nb]
    ch.do(nc.vector.tensor_reduce(s, v, AX.X, ALU.max, apply_absolute_value=True))
    yield
    ch.do(nc.vector.tensor_scalar(s, s, 1.0 / 6.0, 1e-12, ALU.mult, ALU.max))
    yield
    ch.do(nc.vector.reciprocal(r, s))
    yield
    ch.do(nc.vector.tensor_tensor(A.rearrange("p (b k) -> p b k", k=BLK), v,
                                  r.unsqueeze(2).to_broadcast([npart, nb, BLK]), ALU.mult))
    yield
    ch.do(nc.vector.scalar_tensor_tensor(A, A, -1.0, A, ALU.mult, ALU.max))
    yield
    ch.do(nc.vector.tensor_scalar(C, A, 5.0, 2.0, ALU.is_gt, ALU.mult))
    yield
    ch.do(nc.vector.scalar_tensor_tensor(C, A, 3.5, C, ALU.is_gt, ALU.add))
    yield
    ch.do(nc.vector.scalar_tensor_tensor(C, A, 2.5, C, ALU.is_gt, ALU.add))
    yield
    ch.do(nc.vector.tensor_scalar(C, C, 2.0, None, ALU.mult))
    yield
    for mid in (1.75, 1.25, 0.75, 0.25):
        ch.do(nc.vector.scalar_tensor_tensor(C, A, mid, C, ALU.is_gt, ALU.add))
        yield
    ch.do(nc.vector.tensor_scalar(A, V, 0.0, 2.0, ALU.is_ge, ALU.mult))
    yield
    ch.do(nc.vector.scalar_tensor_tensor(A, A, 1.0, C, ALU.subtract, ALU.mult))
    yield
    ch.do(nc.vector.tensor_scalar(s, s, 0.5, None, ALU.mult))
    yield
    ch.do(nc.vector.tensor_tensor(q, A.rearrange("p (b k) -> p b k", k=BLK),
                                  s.unsqueeze(2).to_broadcast([npart, nb, BLK]), ALU.mult))
    yield


def quantize_weights(nc, K, ctx):
    with ExitStack() as tmp:
        q = sbuf(nc, tmp, "wq4", [P, 7, I1])
        scr = fp4_scratch(nc, tmp, I1)
        vec, quantized, turned, copied = K.pool[0:4]
        jobs = []
        for m, w in enumerate((K.gate_rows, K.up_rows)):
            for c in range(3):
                n = min(P, I1 - c * P)
                jobs.append((n, w[0:n, c, :], q[0:n, 3 * m + c, 0:D], D))
        jobs.append((P, K.down_rows[:, :], q[:, 6, :], I1))
        turns = []
        for m in range(2):
            for c in range(3):
                n = min(P, I1 - c * P)
                turns.append((q[0:n, 3 * m + c, 0:D], n, K.ps[:, m, c * P:c * P + n],
                              K.w_gu[:, m * I1 + c * P:m * I1 + c * P + n]))
        for c in range(3):
            n = min(P, I1 - c * P)
            turns.append((q[:, 6, c * P:c * P + n], P, K.ps[0:n, 2 + c, 0:P], K.w_down[0:n, c, :]))
        with nc.Block() as block:
            @block.vector
            def _(dve):
                ch = Chain(dve, vec)
                for npart, V, Q, n in jobs:
                    for _ in fp4_blocks(nc, ch, V, Q, *scr, npart, n):
                        pass
                nc.vector.engine_nop().then_inc(quantized, 1)
                dve.wait_ge(turned, len(turns))
                for _, _, ps, dst in turns:
                    nc.vector.tensor_copy(dst, ps).then_inc(copied, 1)

            @block.tensor
            def _(pe):
                pe.wait_ge(quantized, 1)
                for src, n, ps, _ in turns:
                    nc.tensor.transpose(ps, src, K.ident[0:n, 0:n]).then_inc(turned, 1)
        K.clear()


def fp4_scratch(nc, ctx, n, values=None):
    values = sbuf(nc, ctx, "fp4_abs", [P, n]) if values is None else values
    return (values, sbuf(nc, ctx, "fp4_steps", [P, n], BF16),
            sbuf(nc, ctx, "fp4_scale", [P, n // BLK]), sbuf(nc, ctx, "fp4_rscale", [P, n // BLK]))




def gated_layer_norm(nc, K):
    silu_done, vec, var_ready, rstd_ready, xn_ready, turned, evac = K.pool[0:7]
    with nc.Block() as block:
        @block.vector
        def _(dve):
            ch = Chain(dve, vec)
            dve.wait_ge(silu_done, 1)
            ch.do(nc.vector.tensor_tensor(K.y[:, :, :], K.y[:, :, :], K.att[:, :, :], ALU.mult))
            ch.do(nc.vector.tensor_tensor(K.x[:, :, :], K.x[:, :, :], K.y[:, :, :], ALU.add))
            for t in range(NT):
                ch.tick(nc.vector.bn_stats(K.stats[:, t, :], K.x[:, t, :]))
            ch.wait()
            for t in range(NT):
                ch.tick(nc.vector.bn_aggr(K.mv[:, t, :], K.stats[:, t, :]))
            ch.wait()
            nc.vector.tensor_scalar(K.var[:, 0:NT], K.mv[:, :, 1], EPS_LN, None,
                                    ALU.add).then_inc(var_ready, 1)
            dve.wait_ge(rstd_ready, 1)
            for t in range(NT):
                nc.vector.tensor_scalar(K.xn[:, t, :], K.x[:, t, :], K.mv[:, t, 0:1], K.rstd[:, t:t + 1],
                                        ALU.subtract, ALU.mult).then_inc(xn_ready, 1)

        @block.gpsimd
        def _(pool):
            pool.wait_ge(var_ready, 1)
            nc.gpsimd.tensor_tensor(K.rstd[:, 0:NT], K.var[:, 0:NT], K.neghalf[:, 0:NT],
                                    ALU.pow).then_inc(rstd_ready, 1)

        @block.tensor
        def _(pe):
            for t in range(NT):
                pe.wait_ge(xn_ready, t + 1)
                nc.tensor.transpose(K.ps[:, 0, t * P:(t + 1) * P], K.xn[:, t, :], K.ident[:, :]).then_inc(turned, 1)

        @block.scalar
        def _(act):
            nc.scalar.activation(K.y[:, :, :], K.y[:, :, :], ACT.Silu).then_inc(silu_done, 1)
            act.wait_ge(turned, NT)
            nc.scalar.activation(K.xnT[:, :], K.ps[:, 0, :], ACT.Identity).then_inc(evac, 1)
    K.clear()




def prepare(nc, K, layer, beside=None, then=None):
    (vec, var_ready, rstd_ready, xn_ready, turned, xnT_ready, xr_ready, xr_turned, xrT_ready, projected,
     rotated, qk_turned, first, left, parts_ready, rvar_ready, rrstd_ready) = K.pool[38:55]
    v_used = K.pool[37]
    beside = beside or Beside().start(nc)
    rope, rms = layer == 0, layer == 2
    bq = K.b2_q[:, 0:1] if rms else None
    bk = K.b2_k[:, 0:1] if rms else None
    with ExitStack() as tmp:
        qk = sbuf(nc, tmp, "qk", [P, NT, 2 * D]) if rope else None
        part = sbuf(nc, tmp, "qk_sin", [P, NT, 2 * D]) if rope else None
        rest = sbuf(nc, tmp, "rest", [P, 2, T])
        parts = K.parts
        srcT = K.xrT if rms else K.xnT
        with nc.Block() as block:
            @block.sync
            def _(sp):
                for m in range(2):
                    sp.wait_ge(parts_ready, m + 1)
                    sp.dma_start(K.parts_d[m].rearrange("i (h d) t -> (h d) i t", d=HD),
                                 parts[:, m, :, :]).then_inc(K.saved, 16)

            @block.vector
            def _(dve):
                ch = Chain(dve, vec)

                def statistics(src):
                    for t in range(NT):
                        ch.tick(nc.vector.bn_stats(K.stats[:, t, :], src[:, t, :]))
                    ch.wait()
                    for t in range(NT):
                        ch.tick(nc.vector.bn_aggr(K.mv[:, t, :], K.stats[:, t, :]))
                    ch.wait()

                statistics(K.x)
                nc.vector.tensor_scalar(K.var[:, 0:NT], K.mv[:, :, 1], EPS_LN, None,
                                        ALU.add).then_inc(var_ready, 1)
                dve.wait_ge(rstd_ready, 1)
                for t in range(NT):
                    nc.vector.tensor_scalar(K.xn[:, t, :], K.x[:, t, :], K.mv[:, t, 0:1], K.rstd[:, t:t + 1],
                                            ALU.subtract, ALU.mult).then_inc(xn_ready, 1)
                if layer == 1:
                    dve.wait_ge(xn_ready, NT)
                    beside.run(beside.on_vector, -14)
                if rms:
                    dve.wait_ge(xn_ready, NT)
                    statistics(K.xn)
                    ch.do(nc.vector.tensor_tensor(K.var[:, 0:NT], K.mv[:, :, 0], K.mv[:, :, 0], ALU.mult))
                    nc.vector.scalar_tensor_tensor(K.var[:, 0:NT], K.mv[:, :, 1], 1e-6, K.var[:, 0:NT],
                                                   ALU.add, ALU.add).then_inc(rvar_ready, 1)
                    dve.wait_ge(rrstd_ready, 1)
                    for t in range(NT):
                        nc.vector.scalar_tensor_tensor(K.xr[:, t, :], K.xn[:, t, :], K.rstd[:, t:t + 1],
                                                       K.rmsw[:, :], ALU.mult, ALU.mult).then_inc(xr_ready, 1)
                if rope:
                    heads = lambda a: a.rearrange("p (h d) -> p h d", d=HD)
                    for t in range(NT):
                        dve.wait_ge(projected, t + 1)
                        ch.tick(nc.vector.tensor_tensor(qk[:, t, :], K.ps[:, t, 0:2 * D], K.b0_qkv[:, 0:2 * D],
                                                        ALU.add))
                        ch.tick(nc.vector.tensor_tensor(K.v32[:, t, :, 0:HD], heads(K.ps[:, t, 2 * D:3 * D]),
                                                        heads(K.b0_qkv[:, 2 * D:3 * D]), ALU.add))
                    ch.wait()
                    for t in range(NT):
                        x4 = qk[:, t, :].rearrange("p (g i two) -> p g i two", two=2, i=HD // 2)
                        y4 = part[:, t, :].rearrange("p (g i two) -> p g i two", two=2, i=HD // 2)
                        for e in range(2):
                            sin = K.rope_sin[:, t, e, :].unsqueeze(1).to_broadcast([P, 2 * H, HD // 2])
                            ch.tick(nc.vector.tensor_tensor(y4[:, :, :, e], x4[:, :, :, 1 - e], sin, ALU.mult))
                    ch.wait()
                    beside.run(beside.on_vector, -20)
                    for t in range(NT):
                        cos = K.rope_cos[:, t, :].unsqueeze(1).to_broadcast([P, 2 * H, HD])
                        ch.tick(nc.vector.tensor_tensor(heads(qk[:, t, :]), heads(qk[:, t, :]), cos, ALU.mult))
                    ch.wait()
                    beside.run(beside.on_vector, -19)
                    nc.vector.tensor_tensor(qk[:, :, :], qk[:, :, :], part[:, :, :], ALU.add).then_inc(rotated, 1)
                    beside.run(beside.on_vector, -18)
                else:
                    dve.wait_ge(projected, 3)
                    v = K.ps[:, 2, :].rearrange("p (t h d) -> p t h d", t=NT, d=HD)
                    if rms:
                        for t in range(NT):
                            nc.vector.tensor_tensor(K.v32[:, t, :, 0:HD], v[:, t, :, :],
                                                    K.b2_v[:, :].rearrange("p (h d) -> p h d", d=HD), ALU.add).then_inc(v_used, 1)
                    else:
                        nc.vector.tensor_copy(K.v32[:, :, :, 0:HD], v)
                        beside.run(beside.on_vector, -10)
                for m, b in enumerate((bq, bk)):
                    dve.wait_ge(first, m + 1)
                    nc.vector.scalar_tensor_tensor(rest[:, m, :], K.ps[:, 4 + m, :], 0.0 if b is None else b,
                                                   parts[:, m, 0, :], ALU.add, ALU.subtract).then_inc(left, 1)
                if rope:
                    beside.run(beside.on_vector, -17)
                for m in range(2):
                    dve.wait_ge(first, 3 + m)
                    nc.vector.tensor_tensor(parts[:, m, 2, :], rest[:, m, :], parts[:, m, 1, :],
                                            ALU.subtract).then_inc(parts_ready, 1)
                if then:
                    then[2](dve)

            @block.gpsimd
            def _(pool):
                pool.wait_ge(var_ready, 1)
                nc.gpsimd.tensor_tensor(K.rstd[:, 0:NT], K.var[:, 0:NT], K.neghalf[:, 0:NT],
                                        ALU.pow).then_inc(rstd_ready, 1)
                if rms:
                    pool.wait_ge(rvar_ready, 1)
                    nc.gpsimd.tensor_tensor(K.rstd[:, 0:NT], K.var[:, 0:NT], K.neghalf[:, 0:NT],
                                            ALU.pow).then_inc(rrstd_ready, 1)
                if then:
                    pool.wait_ge(rrstd_ready, 1)
                    then[3](pool)

            @block.tensor
            def _(pe):
                for t in range(NT):
                    pe.wait_ge(xn_ready, t + 1)
                    nc.tensor.transpose(K.ps[:, 6, t * P:(t + 1) * P], K.xn[:, t, :], K.ident[:, :]).then_inc(turned, 1)
                if rms:
                    for t in range(NT):
                        pe.wait_ge(xr_ready, t + 1)
                        nc.tensor.transpose(K.ps[:, 7, t * P:(t + 1) * P], K.xr[:, t, :],
                                            K.ident[:, :]).then_inc(xr_turned, 1)
                    pe.wait_ge(xrT_ready, 1)
                else:
                    pe.wait_ge(xnT_ready, 1)
                if rope:
                    for t in range(NT):
                        nc.tensor.matmul(K.ps[:, t, 0:3 * D], srcT[:, t * P:(t + 1) * P], K.w0_qkv[:, :],
                                         start=True, stop=True).then_inc(projected, 1)
                    beside.run(beside.on_tensor, -18)
                    pe.wait_ge(rotated, 1)
                    for m in range(2):
                        for t in range(NT):
                            mm = nc.tensor.transpose(K.ps[:, 4 + m, t * P:(t + 1) * P], qk[:, t, m * D:(m + 1) * D],
                                                     K.ident[:, :])
                        mm.then_inc(qk_turned, 1)
                    beside.run(beside.on_tensor, PREPARED)
                else:
                    wq, wk, wv = (K.w2_q, K.w2_k, K.w2_v) if rms else (K.w1_q, K.w1_k, K.w1_v)
                    nc.tensor.matmul(K.ps[:, 4, :], wq[:, :], srcT[:, :], start=True, stop=True).then_inc(projected, 1)
                    nc.tensor.matmul(K.ps[:, 5, :], wk[:, :], srcT[:, :], start=True, stop=True).then_inc(projected, 1)
                    for t in range(NT):
                        mm = nc.tensor.matmul(K.ps[:, 2, t * P:(t + 1) * P], srcT[:, t * P:(t + 1) * P], wv[:, :],
                                              start=True, stop=True)
                    mm.then_inc(projected, 1)

                def banks_free():
                    pe.wait_ge(v_used, NT)
                    pe.wait_ge(left, 2)

                if then:
                    then[0](pe, banks_free)

            @block.scalar
            def _(act):
                act.wait_ge(turned, NT)
                nc.scalar.activation(K.xnT[:, :], K.ps[:, 6, :], ACT.Identity).then_inc(xnT_ready, 1)
                if rms:
                    act.wait_ge(xr_turned, NT)
                    nc.scalar.activation(K.xrT[:, :], K.ps[:, 7, :], ACT.Identity).then_inc(xrT_ready, 1)
                if rope:
                    beside.run(beside.on_scalar, -18)
                for m, b in enumerate((bq, bk)):
                    act.wait_ge(qk_turned if rope else projected, m + 1)
                    nc.scalar.activation(parts[:, m, 0, :], K.ps[:, 4 + m, :], ACT.Identity,
                                         bias=0.0 if b is None else b).then_inc(first, 1)
                for m in range(2):
                    act.wait_ge(left, m + 1)
                    nc.scalar.activation(parts[:, m, 1, :], rest[:, m, :], ACT.Identity).then_inc(first, 1)
                if rope:
                    beside.run(beside.on_scalar, PREPARED)
                if then:
                    then[1](act)


def spread_loads(nc, K, sp):
    sp.dma_start(K.ks[72:74, :, :], K.ones_d).then_inc(K.spread, 16)
    sp.wait_ge(K.saved, 32)
    for i in range(3):
        for j in range(3):
            r = 24 * i + 8 * j
            sp.dma_start(K.qs[r:r + HD, :, :],
                         K.parts_d[0, i].rearrange("(h d) t -> d h t", d=HD)).then_inc(K.spread, 16)
            sp.dma_start(K.ks[r:r + HD, :, :],
                         K.parts_d[1, j].rearrange("(h d) t -> d h t", d=HD)).then_inc(K.spread, 16)


class Beside:

    BEFORE = 0
    started = False

    def tensor(self, pe):
        return iter(())

    scalar = vector = gpsimd = tensor

    def run(self, work, step=1 << 20):
        while self.due.setdefault(id(work), -(1 << 10)) <= step:
            self.due[id(work)] = next(work, 1 << 30)

    def start(self, nc):
        self.due, self.started = {}, True
        self.on_tensor, self.on_scalar = self.tensor(nc.tensor), self.scalar(nc.scalar)
        self.on_vector, self.on_gpsimd = self.vector(nc.vector), self.gpsimd(nc.gpsimd)
        return self


def run_alone(nc, K, beside):
    beside.start(nc)
    with nc.Block() as block:
        @block.tensor
        def _(pe):
            beside.run(beside.on_tensor)

        @block.scalar
        def _(act):
            beside.run(beside.on_scalar)

        @block.vector
        def _(dve):
            beside.run(beside.on_vector)

        @block.gpsimd
        def _(pool):
            beside.run(beside.on_gpsimd)
    K.clear()


def attention(nc, K, causal, wo=None, bo=None, combine=True, beside=None, after_store=False):
    (scored, reduced, turned, hi_ready, lo_ready, saved, rows, scored2, exped, weighed, oT_ready, oturned, vec,
     att_ready, att_turned, attT_ready, projected) = K.pool[0:17]
    QUADS, LAG, KR = 3, 13, 74
    STEPS = 8 * NG + LAG + 5
    beside = beside or Beside()
    if not beside.started:
        beside.start(nc)
    scale = float(1.0 / np.sqrt(HD))

    def at_step(s):
        first = [2 * s, 2 * s + 1] if 0 <= s < 8 * NG else []
        maxima = [g for g in range(NG) if s == 8 * (g + 1)]
        a = s - LAG
        second = [2 * a, 2 * a + 1] if 0 <= a < 8 * NG else []
        weigh = [q for q in range(4 * NG) if a == 2 * q + 2]
        back = [g for g in range(NG) if a == 8 * g + 10]
        return first, maxima, second, weigh, back

    def first_bank(n):
        return (n // 16 * 17 + n % 16) % 2

    def maxima_bank(g):
        return (17 * g + 16) % 2

    with ExitStack() as tmp:
        nmax = sbuf(nc, tmp, "nmax", [P, NT, H])
        mparts = sbuf(nc, tmp, "max_parts", [4, 2, 2, T], BF16)
        probs = sbuf(nc, tmp, "probs", [P, 4 * QUADS, T])
        oT = sbuf(nc, tmp, "oT", [P, 2, T])
        rden = sbuf(nc, tmp, "rden", [P, NT, 4])
        with nc.Block() as block:
            @block.tensor
            def _(pe):
                def first_scores(n):
                    g, (j, t) = n // 16, divmod(n % 16, NT)
                    h, b = 4 * g + j, first_bank(n)
                    if g and n % 16 < 2:
                        if n % 16 == 0:
                            pe.wait_ge(reduced, n)
                        else:
                            pe.wait_ge(lo_ready, g)
                    elif n >= 2:
                        pe.wait_ge(reduced, n - 1)
                    keys = (t + 1) * P if causal else T
                    mm = nc.tensor.matmul(K.ps[:, b, 0:keys], K.qs[0:72, h, t * P:(t + 1) * P],
                                          K.ks[0:72, h, 0:keys], start=True, stop=not causal)
                    if causal:
                        mm = nc.tensor.matmul(K.ps[:, b, keys - P:keys], K.identb[:, :], K.mask_q[:, :],
                                              start=False, stop=True)
                    mm.then_inc(scored, 1)

                def second_scores(m):
                    g, (k, j) = m // 16, divmod(m % 16, 4)
                    h, b = 4 * g + j, 2 + m % 3
                    if m % 16 == 0:
                        pe.wait_ge(rows, 16 * (g + 1))
                    if m >= 3:
                        pe.wait_ge(exped, m - 2)
                    q0 = k * P if causal else 0
                    mm = nc.tensor.matmul(K.ps[:, b, q0:T], K.ks[0:KR, h, k * P:(k + 1) * P],
                                          K.qs[0:KR, h, q0:T], start=True, stop=not causal)
                    if causal:
                        mm = nc.tensor.matmul(K.ps[:, b, q0:q0 + P], K.identb[:, :], K.mask_k[:, :],
                                              start=False, stop=True)
                    mm.then_inc(scored2, 1)

                beside.run(beside.on_tensor, -1)
                pe.wait_ge(K.spread, 19 * 16)
                for s in range(STEPS):
                    first, maxima, second, weigh, back = at_step(s)
                    for g in maxima:
                        pe.wait_ge(reduced, 16 * (g + 1))
                        for t in range(NT):
                            mm = nc.tensor.transpose(K.ps[0:4, maxima_bank(g), t * P:(t + 1) * P],
                                                     nmax[:, t, 4 * g:4 * g + 4], K.ident[:, :])
                        mm.then_inc(turned, 1)
                    for g in back:
                        pe.wait_ge(oT_ready, g + 1)
                        for t in range(NT):
                            mm = nc.tensor.transpose(K.ps[:, 5, t * P:(t + 1) * P], oT[:, g % 2, t * P:(t + 1) * P],
                                                     K.ident[:, :])
                        mm.then_inc(oturned, 1)
                    for n, m in zip(first or [None, None], second or [None, None]):
                        if n is not None:
                            first_scores(n)
                        if m is not None:
                            second_scores(m)
                    for q in weigh:
                        g, k = divmod(q, NT)
                        pe.wait_ge(exped, 4 * (q + 1))
                        if g and k == 0:
                            pe.wait_ge(att_ready, g)
                        q0 = k * P if causal else 0
                        for j in range(4):
                            mm = nc.tensor.matmul(K.ps[32 * j:32 * j + 32, 5, q0:T], K.v32[:, k, 4 * g + j, :],
                                                  probs[:, 4 * (q % QUADS) + j, q0:T], start=(k == 0),
                                                  stop=(k == NT - 1), tile_position=(0, 32 * j))
                        mm.then_inc(weighed, 1)
                    beside.run(beside.on_tensor, s)
                beside.run(beside.on_tensor)
                if wo is not None:
                    pe.wait_ge(att_ready, NG)
                    for t in range(NT):
                        mm = nc.tensor.transpose(K.ps[:, 0, t * P:(t + 1) * P], K.att[:, t, :], K.ident[:, :])
                    mm.then_inc(att_turned, 1)
                    pe.wait_ge(attT_ready, 1)
                    for t in range(NT):
                        mm = nc.tensor.matmul(K.ps[:, 1, t * P:(t + 1) * P], oT[:, 0, t * P:(t + 1) * P], wo[:, :],
                                              start=True, stop=True)
                    mm.then_inc(projected, 1)

            @block.scalar
            def _(act):
                for s in range(-beside.BEFORE, STEPS):
                    _, maxima, second, weigh, _ = at_step(s)
                    for g in maxima:
                        act.wait_ge(turned, g + 1)
                        if g >= 2:
                            act.wait_ge(saved, 16 * (g - 1))
                        nc.scalar.activation(mparts[:, g % 2, 0, :], K.ps[0:4, maxima_bank(g), :],
                                             ACT.Identity).then_inc(hi_ready, 1)
                    for m in second:
                        k = m % 16 // 4
                        q = m // 4
                        if q >= QUADS:
                            act.wait_ge(weighed, q - QUADS + 1)
                        act.wait_ge(scored2, m + 1)
                        q0 = k * P if causal else 0
                        nc.scalar.activation(probs[:, 4 * (q % QUADS) + m % 4, q0:T], K.ps[:, 2 + m % 3, q0:T],
                                             ACT.Exp, scale=scale).then_inc(exped, 1)
                    for q in weigh:
                        g, k = divmod(q, NT)
                        if k == NT - 1:
                            act.wait_ge(weighed, q + 1)
                            if g >= 2:
                                act.wait_ge(oturned, g - 1)
                            nc.scalar.activation(oT[:, g % 2, :], K.ps[:, 5, :], ACT.Identity).then_inc(oT_ready, 1)
                    beside.run(beside.on_scalar, s)
                beside.run(beside.on_scalar)
                if wo is not None:
                    act.wait_ge(att_turned, 1)
                    act.wait_ge(oturned, NG)
                    nc.scalar.activation(oT[:, 0, :], K.ps[:, 0, :], ACT.Identity).then_inc(attT_ready, 1)

            @block.sync
            def _(sp):
                if after_store:
                    sp.wait_ge(K.factor_stored, 16)
                spread_loads(nc, K, sp)
                for g in range(NG):
                    sp.wait_ge(hi_ready, g + 1)
                    sp.wait_ge(lo_ready, g + 1)
                    sp.dma_start(K.nmax_d[:, 4 * g:4 * g + 4, :].rearrange("i h t -> h i t"),
                                 mparts[:, g % 2, :, :]).then_inc(saved, 16)
                    sp.wait_ge(saved, 16 * (g + 1))
                    sp.dma_start(K.qs[72:74, 4 * g:4 * g + 4, :], K.nmax_d[:, 4 * g:4 * g + 4, :]).then_inc(rows, 16)
                    sp.wait_ge(rows, 16 * (g + 1))

            @block.gpsimd
            def _(pool):
                beside.run(beside.on_gpsimd)

            @block.vector
            def _(dve):
                ch = Chain(dve, vec)
                for s in range(-beside.BEFORE, STEPS):
                    first, maxima, _, _, back = at_step(s)
                    for g in maxima:
                        dve.wait_ge(hi_ready, g + 1)
                        nc.vector.tensor_tensor(mparts[:, g % 2, 1, :], K.ps[0:4, maxima_bank(g), :],
                                                mparts[:, g % 2, 0, :], ALU.subtract).then_inc(lo_ready, 1)
                    for n in first:
                        g, (j, t) = n // 16, divmod(n % 16, NT)
                        h = 4 * g + j
                        dve.wait_ge(scored, n + 1)
                        keys = (t + 1) * P if causal else T
                        nc.vector.tensor_reduce(nmax[:, t, h:h + 1], K.ps[:, first_bank(n), 0:keys], AX.X, ALU.max,
                                                negate=True).then_inc(reduced, 1)
                    for g in back:
                        dve.wait_ge(oturned, g + 1)
                        o = K.ps[:, 5, :].rearrange("p (t j d) -> p t j d", t=NT, j=4)
                        ch.do(nc.vector.reciprocal(rden[:, :, :], o[:, :, :, HD]))
                        for t in range(NT):
                            mul = nc.vector.tensor_tensor(
                                K.att[:, t, g * 32:(g + 1) * 32].rearrange("p (j d) -> p j d", d=HD),
                                o[:, t, :, 0:HD], rden[:, t, :].unsqueeze(2).to_broadcast([P, 4, HD]), ALU.mult)
                            if t < NT - 1:
                                ch.tick(mul)
                            else:
                                mul.then_inc(att_ready, 1)
                        ch.wait()
                        dve.wait_ge(att_ready, g + 1)
                    beside.run(beside.on_vector, s)
                beside.run(beside.on_vector)
                if wo is not None:
                    dve.wait_ge(projected, 1)
                    o = K.ps[:, 1, :].rearrange("p (t d) -> p t d", t=NT)
                    ch.do(nc.vector.tensor_copy(K.att[:, :, :], o))
                if bo is not None:
                    ch.do(nc.vector.tensor_tensor(K.att[:, :, :], K.att[:, :, :],
                                                  bo[:, :].unsqueeze(1).to_broadcast([P, NT, D]), ALU.add))
                    nc.vector.tensor_tensor(K.att[:, :, :], K.att[:, :, :], K.xr[:, :, :], ALU.add)
                if combine:
                    dve.wait_ge(beside.g_ready, 1)
                    ch.do(nc.vector.tensor_tensor(K.att[:, :, :], K.att[:, :, :], K.g[:, :, :], ALU.mult))
                    nc.vector.tensor_tensor(K.x[:, :, :], K.x[:, :, :], K.att[:, :, :], ALU.add)
        K.clear(spread=True)




class TernaryFfn(Beside):

    BEFORE = 20

    def __init__(self, nc, K, ctx):
        self.nc, self.K = nc, K
        (self.gate_up, self.silu_done, self.h_ready, self.hid, self.gelu_done, self.out_done, self.g_in,
         self.g_ready) = K.pool[24:32]
        self.a = sbuf(nc, ctx, "silu_a", [P, 2, T])
        self.h = sbuf(nc, ctx, "hid_a", [P, 4, T])
        self.g = sbuf(nc, ctx, "hid_b", [P, 4, T])

    @staticmethod
    def hidden_step(n):
        return 4 * n - 16

    OUT_STEP = 18

    def tensor(self, pe):
        nc, K = self.nc, self.K
        for c in range(4):
            yield c - 20
            if c:
                pe.wait_ge(self.h_ready, c)
            nc.tensor.matmul(K.ps[:, 6, :], K.w0_1[:, c * P:(c + 1) * P], K.xnT[:, :], start=True, stop=True)
            nc.tensor.matmul(K.ps[:, 7, :], K.w0_2[:, c * P:(c + 1) * P], K.xnT[:, :],
                             start=True, stop=True).then_inc(self.gate_up, 1)
        for layer, (w, src) in enumerate(((K.w0_h1, self.h), (K.w0_h2, self.g))):
            for c in range(4):
                n = 4 * layer + c
                for k in range(4):
                    yield self.hidden_step(n) + k
                    if n == 0 and k == 0:
                        pe.wait_ge(self.h_ready, 4)
                    if c == 0 and k == 0 and layer:
                        pe.wait_ge(self.gelu_done, 4)
                    elif k == 0 and n >= 2:
                        pe.wait_ge(self.gelu_done, n - 1)
                    mm = nc.tensor.matmul(K.ps[:, 6 + n % 2, :], w[:, k, c * P:(c + 1) * P], src[:, k, :],
                                          start=(k == 0), stop=(k == 3))
                mm.then_inc(self.hid, 1)
        for t in range(NT):
            yield self.OUT_STEP + t
            if t == 0:
                pe.wait_ge(self.gelu_done, 8)
            for k in range(4):
                mm = nc.tensor.matmul(K.ps[:, 6, t * P:(t + 1) * P], self.h[:, k, t * P:(t + 1) * P],
                                      K.w0_3[:, k, :], start=(k == 0), stop=(k == 3))
        mm.then_inc(self.out_done, 1)

    def scalar(self, act):
        nc, K = self.nc, self.K
        for c in range(4):
            yield c - 20
            act.wait_ge(self.gate_up, c + 1)
            if c >= 2:
                act.wait_ge(self.h_ready, c - 1)
            nc.scalar.activation(self.a[:, c % 2, :], K.ps[:, 6, :], ACT.Silu,
                                 scale=K.s0_1[:, c:c + 1]).then_inc(self.silu_done, 1)
        for layer, (s, dst) in enumerate(((K.s0_h1, self.g), (K.s0_h2, self.h))):
            for c in range(4):
                n = 4 * layer + c
                yield self.hidden_step(n) + 3
                act.wait_ge(self.hid, n + 1)
                nc.scalar.activation(dst[:, c, :], K.ps[:, 6 + n % 2, :], ACT.Gelu,
                                     scale=s[:, c:c + 1]).then_inc(self.gelu_done, 1)
        yield 1 << 19
        act.wait_ge(self.g_in, 1)
        nc.scalar.activation(K.g[:, :, :], K.g[:, :, :], ACT.Silu).then_inc(self.g_ready, 1)

    def vector(self, dve):
        nc, K = self.nc, self.K
        for c in range(4):
            yield c - 20
            dve.wait_ge(self.silu_done, c + 1)
            nc.vector.scalar_tensor_tensor(self.h[:, c, :], K.ps[:, 7, :], K.s0_2[:, c:c + 1],
                                           self.a[:, c % 2, :], ALU.mult, ALU.mult).then_inc(self.h_ready, 1)
        yield self.OUT_STEP + NT
        dve.wait_ge(self.out_done, 1)
        nc.vector.tensor_tensor(K.g[:, :, :], K.ps[:, 6, :].rearrange("p (t d) -> p t d", t=NT),
                                K.s0_3[:, :].unsqueeze(1).to_broadcast([P, NT, D]), ALU.mult).then_inc(self.g_in, 1)




class Fp4Ffn(Beside):

    BEFORE = 20
    XQ_STEP = -5
    UP_STEPS = -4, -3, 3, 7
    QUANT_STEP = 30
    TURN_STEP = 44
    DOWN_STEP = 48

    def __init__(self, nc, K, ctx):
        self.nc, self.K = nc, K
        (self.vec, self.xq_ready, self.turned, self.xqT_ready, self.projected, self.silu_done, self.h_done,
         self.hq_ready, self.hturned, self.hT_ready, self.down, self.g_ready) = K.pool[24:36]
        self.xq = sbuf(nc, ctx, "xq", [P, NT, D])
        self.xqT = sbuf(nc, ctx, "xqT", [P, T])
        self.h = sbuf(nc, ctx, "h1", [P, NT, I1])
        self.hT = sbuf(nc, ctx, "h1T", [P, 3, T])
        self.scr = fp4_scratch(nc, ctx, NT * I1, self.hT[:, :, :].rearrange("p c t -> p (c t)"))

    def tensor(self, pe):
        nc, K = self.nc, self.K
        yield self.XQ_STEP
        pe.wait_ge(self.xq_ready, 1)
        for t in range(NT):
            mm = nc.tensor.transpose(K.ps[:, 7, t * P:(t + 1) * P], self.xq[:, t, :], K.ident[:, :])
        mm.then_inc(self.turned, 1)
        for t in range(NT):
            yield self.UP_STEPS[t]
            if t == 0:
                pe.wait_ge(self.xqT_ready, 1)
            else:
                pe.wait_ge(self.h_done, t)
            nc.tensor.matmul(K.ps[:, 6, 0:I1], self.xqT[:, t * P:(t + 1) * P], K.w_gu[:, 0:I1],
                             start=True, stop=True)
            nc.tensor.matmul(K.ps[:, 7, 0:I1], self.xqT[:, t * P:(t + 1) * P], K.w_gu[:, I1:2 * I1],
                             start=True, stop=True).then_inc(self.projected, 1)
        for c in range(3):
            yield self.TURN_STEP + c
            if c == 0:
                pe.wait_ge(self.hq_ready, 1)
            if c == 2:
                pe.wait_ge(self.hT_ready, 1)
            n = min(P, I1 - c * P)
            for t in range(NT):
                mm = nc.tensor.transpose(K.ps[0:n, 6 + c % 2, t * P:(t + 1) * P], self.h[:, t, c * P:c * P + n],
                                         K.ident[:, :])
            mm.then_inc(self.hturned, 1)
        for t in range(NT):
            yield self.DOWN_STEP + t
            if t == 0:
                pe.wait_ge(self.hT_ready, 3)
            for c in range(3):
                n = min(P, I1 - c * P)
                mm = nc.tensor.matmul(K.ps[:, 7, t * P:(t + 1) * P], self.hT[0:n, c, t * P:(t + 1) * P],
                                      K.w_down[0:n, c, :], start=(c == 0), stop=(c == 2))
        mm.then_inc(self.down, 1)

    def scalar(self, act):
        nc, K = self.nc, self.K
        yield self.XQ_STEP
        act.wait_ge(self.turned, 1)
        nc.scalar.activation(self.xqT[:, :], K.ps[:, 7, :], ACT.Identity).then_inc(self.xqT_ready, 1)
        for t in range(NT):
            yield self.UP_STEPS[t]
            act.wait_ge(self.projected, t + 1)
            nc.scalar.activation(self.h[:, t, :], K.ps[:, 6, 0:I1], ACT.Silu).then_inc(self.silu_done, 1)
        for c in range(3):
            yield self.TURN_STEP + c
            act.wait_ge(self.hturned, c + 1)
            n = min(P, I1 - c * P)
            nc.scalar.activation(self.hT[0:n, c, :], K.ps[0:n, 6 + c % 2, :], ACT.Identity).then_inc(self.hT_ready, 1)
        yield 1 << 19
        act.wait_ge(self.down, 1)
        nc.scalar.activation(K.g[:, :, :], K.ps[:, 7, :].rearrange("p (t d) -> p t d", t=NT),
                             ACT.Silu).then_inc(self.g_ready, 1)

    def vector(self, dve):
        nc, K = self.nc, self.K
        ch = Chain(dve, self.vec)
        step = -self.BEFORE
        yield step
        for _ in fp4_blocks(nc, ch, K.xn[:, :, :].rearrange("p t d -> p (t d)"),
                            self.xq[:, :, :].rearrange("p t d -> p (t d)"), *self.scr, P, NT * D):
            step += 1
            yield step
        nc.vector.engine_nop().then_inc(self.xq_ready, 1)
        for t in range(NT):
            yield self.UP_STEPS[t]
            dve.wait_ge(self.silu_done, t + 1)
            nc.vector.tensor_tensor(self.h[:, t, :], self.h[:, t, :], K.ps[:, 7, 0:I1],
                                    ALU.mult).then_inc(self.h_done, 1)
        yield self.UP_STEPS[-1]
        dve.wait_ge(self.h_done, NT)
        flat = self.h[:, :, :].rearrange("p t i -> p (t i)")
        step = self.QUANT_STEP
        for _ in fp4_blocks(nc, ch, flat, flat, *self.scr, P, NT * I1):
            yield step
            step += 1
        nc.vector.engine_nop().then_inc(self.hq_ready, 1)




def copy_shifted(nc, K, turned, shifted, bank):
    def scalar(act):
        act.wait_ge(turned, 1)
        nc.scalar.activation(K.shT[0:64, :], K.ps[0:64, bank, :], ACT.Identity).then_inc(shifted, 1)

    def vector(dve):
        nc.vector.memset(K.shT[64:128, 0:1], 0.0)
        dve.wait_ge(turned, 1)
        nc.vector.tensor_copy(K.shT[64:128, 1:T], K.ps[64:128, bank, 0:T - 1]).then_inc(shifted, 1)

    return scalar, vector


def local_qkv(nc, K, ctx, L):
    (turned, shifted, projected, squared, v_copied, summed, clipped, rn_ready, rotated, q_scaled, k_scaled,
     qk_turned, copied, vec, added, cleared) = K.pool[0:16]
    w = K.w2_qkv[L]
    sq = sbuf(nc, ctx, "sq", [P, 2, INNER])
    rot = sbuf(nc, ctx, "rot", [P, 2, 2, INNER])
    qk = sbuf(nc, ctx, "qk_tm", [P, 2, 2, INNER])
    ssq = sbuf(nc, ctx, "ssq", [P, NT, 2, LH])
    rn = sbuf(nc, ctx, "rn", [P, NT, 2, LH])
    shift_act, shift_dve = copy_shifted(nc, K, turned, shifted, 7)

    def scale_heads(engine, t, m):
        x3 = qk[:, t % 2, m, :].rearrange("p (h d) -> p h d", d=LD)
        return engine.tensor_tensor(x3, x3, rn[:, t, m, :].unsqueeze(2).to_broadcast([P, LH, LD]), ALU.mult)

    def tensor(pe, banks_free=None):
        for t in range(NT):
            mm = nc.tensor.transpose(K.ps[:, 7, t * P:(t + 1) * P], (K.y if L else K.xn)[:, t, :],
                                     K.ident[:, :])
        mm.then_inc(turned, 1)
        if banks_free:
            banks_free()
        pe.wait_ge(shifted, 2)

        def project(t):
            if t >= 2:
                pe.wait_ge(v_copied, t - 1)
                pe.wait_ge(rotated, 2 * (t - 1))
            for m in range(3):
                mm = nc.tensor.matmul(K.ps[:, 3 * (t % 2) + m, :], K.shT[:, t * P:(t + 1) * P],
                                      w[:, m * INNER:(m + 1) * INNER], start=True, stop=True)
            mm.then_inc(projected, 1)

        def turn(t):
            for m in range(2):
                pe.wait_ge((q_scaled, k_scaled)[m], t + 1)
                if t:
                    pe.wait_ge(copied, 3 * t - 1 + m)
                for p in range(LH // 2):
                    mm = nc.tensor.transpose(K.ps[:, 6 + m, p * P:(p + 1) * P],
                                             qk[:, t % 2, m, p * P:(p + 1) * P], K.ident[:, :])
                mm.then_inc(qk_turned, 1)

        project(0)
        project(1)
        for t in range(NT):
            if t + 2 < NT:
                project(t + 2)
            turn(t)

    def scalar(act):
        shift_act(act)

        def copy(t):
            act.wait_ge(qk_turned, 2 * t + 1)
            for e in range(2):
                nc.scalar.activation(K.qz[64 * e:64 * e + 64, e:LH:2, t * P:(t + 1) * P],
                                     K.ps[64 * e:64 * e + 64, 6, :].rearrange("p (h t) -> p h t", t=P),
                                     ACT.Identity).then_inc(copied, 1)
            act.wait_ge(qk_turned, 2 * t + 2)
            nc.scalar.activation(K.kT[:, :, t * P:(t + 1) * P],
                                 K.ps[:, 7, :].rearrange("p (h t) -> p h t", t=P),
                                 ACT.Identity).then_inc(copied, 1)

        for t in range(NT):
            act.wait_ge(projected, t + 1)
            b = 3 * (t % 2)
            for m in range(2):
                if t:
                    act.wait_ge(summed, 2 * (t - 1) + m + 1)
                nc.scalar.activation(sq[:, m, :], K.ps[:, b + m, :], ACT.Square).then_inc(squared, 1)
            nc.scalar.activation(K.v_tm[:, t, :, 0:LD], K.ps[:, b + 2, :].rearrange("p (h d) -> p h d", d=LD),
                                 ACT.Identity).then_inc(v_copied, 1)
            act.wait_ge(clipped, t + 1)
            nc.scalar.activation(rn[:, t, :, :], ssq[:, t, :, :], ACT.Sqrt).then_inc(rn_ready, 1)
            if t >= 2:
                copy(t - 2)
        copy(NT - 2)
        copy(NT - 1)

    def vector(dve):
        shift_dve(dve)
        nc.vector.memset(K.v_tm[:, :, :, LD:LD + 1], 1.0)
        if L == 0:
            nc.vector.tensor_copy(K.y[:, :, :], K.xn[:, :, :])
        ch = Chain(dve, vec)

        def scale(t):
            dve.wait_ge(rn_ready, t + 1)
            dve.wait_ge(added, 2 * t + 1)
            scale_heads(nc.vector, t, 0).then_inc(q_scaled, 1)

        for t in range(NT):
            b = 3 * (t % 2)
            for m in range(2):
                dve.wait_ge(squared, 2 * t + m + 1)
                nc.vector.tensor_reduce(ssq[:, t, m, :], sq[:, m, :].rearrange("p (h d) -> p h d", d=LD),
                                        AX.X, ALU.add).then_inc(summed, 1)
            dve.wait_ge(summed, 2 * t + 2)
            ch.tick(nc.vector.tensor_scalar(ssq[:, t, 0, :], ssq[:, t, 0, :], 1e-24, 1.0 / 64, ALU.max,
                                            ALU.mult))
            ch.do(nc.vector.tensor_scalar(ssq[:, t, 1, :], ssq[:, t, 1, :], 1e-24, None, ALU.max))
            nc.vector.reciprocal(ssq[:, t, :, :], ssq[:, t, :, :]).then_inc(clipped, 1)
            if t >= 2:
                dve.wait_ge(qk_turned, 2 * (t - 1))
            for m, (cos, sin) in enumerate(((K.cosq, K.sinq), (K.cosk, K.sink))):
                src = K.ps[:, b + m, :].rearrange("p (h two d) -> p h two d", two=2, d=LD // 2)
                rv = rot[:, t % 2, m, :].rearrange("p (h two d) -> p h two d", two=2, d=LD // 2)
                for e in range(2):
                    s = sin[L][:, t, 32 * e:32 * e + 32].unsqueeze(1).to_broadcast([P, LH, 32])
                    ch.tick(nc.vector.tensor_tensor(rv[:, :, e, :], src[:, :, 1 - e, :], s, ALU.mult))
                ch.wait()
                c = cos[L][:, t, :].unsqueeze(1).to_broadcast([P, LH, LD])
                nc.vector.tensor_tensor(qk[:, t % 2, m, :].rearrange("p (h d) -> p h d", d=LD),
                                        K.ps[:, b + m, :].rearrange("p (h d) -> p h d", d=LD), c,
                                        ALU.mult).then_inc(rotated, 1)
            if t:
                scale(t - 1)
        scale(NT - 1)

    def gpsimd(pool):
        nc.gpsimd.memset(K.qz[64:128, 0:LH:2, :], 0.0).then_inc(cleared, 1)
        pool.wait_ge(cleared, 1)
        nc.gpsimd.memset(K.qz[0:64, 1:LH:2, :], 0.0).then_inc(cleared, 1)
        pool.wait_ge(cleared, 2)
        for t in range(NT):
            for m in range(2):
                pool.wait_ge(rotated, 2 * t + m + 1)
                x = qk[:, t % 2, m, :]
                nc.gpsimd.tensor_tensor(x, x, rot[:, t % 2, m, :], ALU.add).then_inc(added, 1)
            pool.wait_ge(rn_ready, t + 1)
            pool.wait_ge(added, 2 * t + 2)
            scale_heads(nc.gpsimd, t, 1).then_inc(k_scaled, 1)

    return tensor, scalar, vector, gpsimd


def local_attention(nc, K, L):
    (scored, reduced, exped, zeroed, turned, copied, summed, divided, vec, oturned, oT_ready, projected) = K.pool[0:12]
    with ExitStack() as tmp:
        nm = sbuf(nc, tmp, "nm", [P, 2, NT])
        rden = sbuf(nc, tmp, "rden", [P, 2, NT])
        probs = sbuf(nc, tmp, "probs", [P, 2, NT, 2 * P])
        pT = sbuf(nc, tmp, "probsT", [P, 2, NT, 2 * P])
        o_tm = sbuf(nc, tmp, "o_tm", [P, NT, INNER])
        with nc.Block() as block:
            @block.tensor
            def _(pe):
                def scores(h):
                    if h >= 2:
                        pe.wait_ge(exped, h - 1)
                    for t in range(NT):
                        b = 2 * (h % 2) + t // 2
                        c = 256 * (t % 2)
                        nc.tensor.matmul(K.ps[:, b, c + 64:c + 256], K.identb[:, :],
                                         (K.mask_band if t else K.mask_band0)[:, :], start=True, stop=False)
                        k0 = 64 if t else 128
                        mm = nc.tensor.matmul(K.ps[:, b, c + k0:c + 256], K.qz[:, h, t * P:(t + 1) * P],
                                              K.kT[:, h // 2, t * P - 128 + k0:(t + 1) * P], start=False, stop=True)
                    mm.then_inc(scored, 1)

                def turn(h):
                    pe.wait_ge(exped, h + 1)
                    if h == 0:
                        pe.wait_ge(zeroed, 1)
                    for u in range(2):
                        if h:
                            pe.wait_ge(copied, 2 * h + u - 1)
                        for t in (2 * u, 2 * u + 1):
                            for e in range(2):
                                o = (t % 2) * 256 + e * P
                                mm = nc.tensor.transpose(K.ps[:, 4 + u, o:o + P], probs[:, h % 2, t, e * P:(e + 1) * P],
                                                         K.ident[:, :])
                        mm.then_inc(turned, 1)

                def weigh(h):
                    pe.wait_ge(copied, 2 * h + 2)
                    if h >= 2:
                        pe.wait_ge(divided, h - 1)
                    for t in range(NT):
                        o = K.ps[:, 6 + h % 2, t * 65:(t + 1) * 65]
                        if t:
                            nc.tensor.matmul(o, pT[:, h % 2, t, 0:P], K.v_tm[:, t - 1, h, :], start=True, stop=False)
                        mm = nc.tensor.matmul(o, pT[:, h % 2, t, P:2 * P], K.v_tm[:, t, h, :],
                                              start=(t == 0), stop=True)
                    mm.then_inc(summed, 1)

                scores(0)
                scores(1)
                for h in range(LH):
                    turn(h)
                    if h + 2 < LH:
                        scores(h + 2)
                    weigh(h)
                for p in range(4):
                    pe.wait_ge(divided, 2 * p + 2)
                    for t in range(NT):
                        mm = nc.tensor.transpose(K.ps[:, p, t * P:(t + 1) * P], o_tm[:, t, p * P:(p + 1) * P],
                                                 K.ident[:, :])
                    mm.then_inc(oturned, 1)
                pe.wait_ge(oT_ready, 4)
                for t in range(NT):
                    for p in range(4):
                        mm = nc.tensor.matmul(K.ps[:, 4, t * P:(t + 1) * P], K.oT[:, p, t * P:(t + 1) * P],
                                              K.w2_o[L][:, p, :], start=(p == 0), stop=(p == 3))
                mm.then_inc(projected, 1)

            @block.vector
            def _(dve):
                ch = Chain(dve, vec)

                def maxima(h):
                    dve.wait_ge(scored, h + 1)
                    s = K.ps[:, 2 * (h % 2):2 * (h % 2) + 2, :].rearrange("p b (t k) -> p (b t) k", k=256)
                    nc.vector.tensor_reduce(nm[:, h % 2, :], s[:, :, 64:256], AX.X, ALU.max,
                                            negate=True).then_inc(reduced, 1)

                def divide(h):
                    i = h % 2
                    dve.wait_ge(summed, h + 1)
                    o = K.ps[:, 6 + i, 0:NT * 65].rearrange("p (t d) -> p t d", d=65)
                    ch.do(nc.vector.reciprocal(rden[:, i, :], o[:, :, LD]))
                    nc.vector.tensor_tensor(o_tm[:, :, h * LD:(h + 1) * LD], o[:, :, 0:LD],
                                            rden[:, i, :].unsqueeze(2).to_broadcast([P, NT, LD]),
                                            ALU.mult).then_inc(divided, 1)

                maxima(0)
                maxima(1)
                for h in range(LH):
                    for u in range(2):
                        dve.wait_ge(turned, 2 * h + u + 1)
                        if h >= 2 and u == 0:
                            dve.wait_ge(summed, h - 1)
                        nc.vector.tensor_copy(pT[:, h % 2, 2 * u:2 * u + 2, :], K.ps[:, 4 + u, :].rearrange(
                            "p (t k) -> p t k", k=256)).then_inc(copied, 1)
                    if h + 2 < LH:
                        maxima(h + 2)
                    if h:
                        divide(h - 1)
                divide(LH - 1)
                dve.wait_ge(projected, 1)
                nc.vector.tensor_tensor(K.y[:, :, :], K.y[:, :, :],
                                        K.ps[:, 4, :].rearrange("p (t d) -> p t d", t=NT), ALU.add)

            @block.scalar
            def _(act):
                for h in range(LH):
                    i = h % 2
                    act.wait_ge(reduced, h + 1)
                    if h >= 2:
                        act.wait_ge(turned, 2 * (h - 1))
                    for t in range(NT):
                        b, c = 2 * i + t // 2, 256 * (t % 2)
                        a = nc.scalar.activation(probs[:, i, t, 64:256], K.ps[:, b, c + 64:c + 256], ACT.Exp,
                                                 bias=nm[:, i, t:t + 1])
                    a.then_inc(exped, 1)
                for p in range(4):
                    act.wait_ge(oturned, p + 1)
                    nc.scalar.activation(K.oT[:, p, :], K.ps[:, p, :], ACT.Identity).then_inc(oT_ready, 1)

            @block.gpsimd
            def _(pool):
                nc.gpsimd.memset(probs[:, :, :, 0:64], 0.0).then_inc(zeroed, 1)
        K.clear()


class Glu(Beside):

    BEFORE = 5
    UP_STEP, DOWN_STEP = 0, 8

    def __init__(self, nc, K, ctx, L, alone):
        self.nc, self.K, self.L = nc, K, L
        (self.back, self.vec, self.var_ready, self.rstd_ready, self.hn_ready, self.turned, self.hnT_ready, self.up,
         self.gelu_done, self.hid_ready, self.down, self.yturned, self.shifted) = K.pool[24:37]
        self.y_bank, self.back_bank, self.turn_bank, self.down_bank = (7, 0, 1, 6) if alone else (7, 6, 7, 6)
        self.up_banks = [(2, 3), (4, 5)] if alone else [(6, 7)]
        self.rows = [P, P, HID2 - 2 * P]
        self.hn = sbuf(nc, ctx, "hn", [P, NT, D])
        self.hnT = sbuf(nc, ctx, "hnT", [P, T])
        self.gl = sbuf(nc, ctx, "gl", [P, 2, T])
        self.hid = sbuf(nc, ctx, "hid", [P, 3, T])
        self.shift_act, self.shift_dve = copy_shifted(nc, K, self.yturned, self.shifted, self.y_bank)

    def tensor(self, pe):
        nc, K, L = self.nc, self.K, self.L
        for t in range(NT):
            mm = nc.tensor.transpose(K.ps[:, self.y_bank, t * P:(t + 1) * P], K.y[:, t, :], K.ident[:, :])
        mm.then_inc(self.yturned, 1)
        yield -4
        pe.wait_ge(self.shifted, 2)
        for t in range(NT):
            mm = nc.tensor.transpose(K.ps[:, self.back_bank, t * P:(t + 1) * P], K.shT[:, t * P:(t + 1) * P],
                                     K.ident[:, :])
        mm.then_inc(self.back, 1)
        yield -2
        pe.wait_ge(self.hn_ready, NT)
        for t in range(NT):
            mm = nc.tensor.transpose(K.ps[:, self.turn_bank, t * P:(t + 1) * P], self.hn[:, t, :], K.ident[:, :])
        mm.then_inc(self.turned, 1)
        for c in range(3):
            n = self.rows[c]
            for m in range(2):
                yield self.UP_STEP + 2 * c + m
                if c == 0 and m == 0:
                    pe.wait_ge(self.hnT_ready, 1)
                if m == 0 and c >= len(self.up_banks):
                    pe.wait_ge(self.hid_ready, c - len(self.up_banks) + 1)
                mm = nc.tensor.matmul(K.ps[0:n, self.up_banks[c % len(self.up_banks)][m], :],
                                      K.w2_up[L][:, m * HID2 + c * P:m * HID2 + c * P + n], self.hnT[:, :],
                                      start=True, stop=True)
            mm.then_inc(self.up, 1)
        for t in range(NT):
            yield self.DOWN_STEP + t
            if t == 0:
                pe.wait_ge(self.hid_ready, 3)
            for c in range(3):
                n = self.rows[c]
                mm = nc.tensor.matmul(K.ps[:, self.down_bank, t * P:(t + 1) * P],
                                      self.hid[0:n, c, t * P:(t + 1) * P], K.w2_down[L][0:n, c, :],
                                      start=(c == 0), stop=(c == 2))
        mm.then_inc(self.down, 1)

    def vector(self, dve):
        nc, K, L = self.nc, self.K, self.L
        self.shift_dve(dve)
        ch = Chain(dve, self.vec)
        yield -4
        dve.wait_ge(self.back, 1)
        for t in range(NT):
            ch.tick(nc.vector.bn_stats(K.stats[:, t, :], K.ps[:, self.back_bank, t * P:(t + 1) * P]))
        ch.wait()
        for t in range(NT):
            ch.tick(nc.vector.bn_aggr(K.mv[:, t, :], K.stats[:, t, :]))
        ch.wait()
        nc.vector.tensor_scalar(K.var[:, 0:NT], K.mv[:, :, 1], 1e-5, None, ALU.add).then_inc(self.var_ready, 1)
        yield -3
        dve.wait_ge(self.rstd_ready, 1)
        for t in range(NT):
            nc.vector.tensor_scalar(self.hn[:, t, :], K.ps[:, self.back_bank, t * P:(t + 1) * P], K.mv[:, t, 0:1],
                                    K.rstd[:, t:t + 1], ALU.subtract, ALU.mult).then_inc(self.hn_ready, 1)
        for c in range(3):
            yield self.UP_STEP + 2 * c + 1
            n = self.rows[c]
            dve.wait_ge(self.gelu_done, c + 1)
            nc.vector.scalar_tensor_tensor(self.hid[0:n, c, :], K.ps[0:n, self.up_banks[c % len(self.up_banks)][0], :],
                                           K.b2_up[L][0:n, c:c + 1], self.gl[0:n, c % 2, :],
                                           ALU.add, ALU.mult).then_inc(self.hid_ready, 1)
        yield self.DOWN_STEP + NT - 1
        dve.wait_ge(self.down, 1)
        ch.do(nc.vector.tensor_tensor(K.y[:, :, :], K.y[:, :, :],
                                      K.ps[:, self.down_bank, :].rearrange("p (t d) -> p t d", t=NT), ALU.add))
        nc.vector.tensor_tensor(K.y[:, :, :], K.y[:, :, :],
                                K.b2_down[L][:, :].unsqueeze(1).to_broadcast([P, NT, D]), ALU.add)

    def gpsimd(self, pool):
        nc, K = self.nc, self.K
        yield -4
        pool.wait_ge(self.var_ready, 1)
        nc.gpsimd.tensor_tensor(K.rstd[:, 0:NT], K.var[:, 0:NT], K.neghalf[:, 0:NT],
                                ALU.pow).then_inc(self.rstd_ready, 1)

    def scalar(self, act):
        nc, K, L = self.nc, self.K, self.L
        self.shift_act(act)
        yield -2
        act.wait_ge(self.turned, 1)
        nc.scalar.activation(self.hnT[:, :], K.ps[:, self.turn_bank, :], ACT.Identity, scale=K.ln2_g[L][:, 0:1],
                             bias=K.ln2_b[L][:, 0:1]).then_inc(self.hnT_ready, 1)
        for c in range(3):
            yield self.UP_STEP + 2 * c + 1
            n = self.rows[c]
            act.wait_ge(self.up, c + 1)
            if c == 2:
                act.wait_ge(self.hid_ready, 1)
            nc.scalar.activation(self.gl[0:n, c % 2, :], K.ps[0:n, self.up_banks[c % len(self.up_banks)][1], :],
                                 ACT.Gelu, bias=K.b2_up[L][0:n, 3 + c:4 + c]).then_inc(self.gelu_done, 1)


def local_buffers(nc, K, ctx):
    K.v_tm = sbuf(nc, ctx, "v_tm", [P, NT, LH, LD + 1])
    K.qz = sbuf(nc, ctx, "qz", [P, LH, T])
    K.kT = sbuf(nc, ctx, "kT", [P, LH // 2, T])
    K.oT = sbuf(nc, ctx, "oT2", [P, LH // 2, T])


def local_sublayer(nc, K, L):
    with ExitStack() as tmp:
        local_buffers(nc, K, tmp)
        with ExitStack() as scratch:
            tensor, scalar, vector, gpsimd = local_qkv(nc, K, scratch, L)
            with nc.Block() as block:
                @block.tensor
                def _(pe):
                    tensor(pe)

                @block.scalar
                def _(act):
                    scalar(act)

                @block.vector
                def _(dve):
                    vector(dve)

                @block.gpsimd
                def _(pool):
                    gpsimd(pool)
            K.clear()
        local_attention(nc, K, L)




def experts(nc, K, b, next_x):
    (gated, vec, e_in, e_done, h12, silu_done, hid_ready, out_done, used, top_read, projected, gate_projected,
     raw_ready, conv_ready, sig_done, abs_ready, exp_done, ln_done, aet_ready, y_ready, y_done, f_ready,
     stored, loaded) = K.pool[0:24]
    th = slice(64, 96)
    with ExitStack() as tmp:
        sc = sbuf(nc, tmp, "sc", [P, NT, E3])
        top = sbuf(nc, tmp, "top", [P, NT, 8])
        idx = sbuf(nc, tmp, "idx", [P, NT, 8], U32)
        idf = sbuf(nc, tmp, "idf", [P, NT, 8])
        ex = sbuf(nc, tmp, "ex", [P, NT])
        pr = sbuf(nc, tmp, "pr", [P, 2, NT])
        eq = sbuf(nc, tmp, "eq", [P, 2, NT, E3])
        pb = sbuf(nc, tmp, "pb", [P, NT, E3])
        a = sbuf(nc, tmp, "silu_a", [P, 2, T])
        h = sbuf(nc, tmp, "hid", [P, 2, 2, T])
        raw = sbuf(nc, tmp, "raw", [96, T + 3])
        conv = sbuf(nc, tmp, "conv", [96, T])
        aet = sbuf(nc, tmp, "aet", [96, T])
        zt = sbuf(nc, tmp, "zt", [96, T])
        za = sbuf(nc, tmp, "za", [96, T])
        fac = K.att
        with nc.Block() as block:
            @block.tensor
            def _(pe):
                for t in range(NT):
                    mm = nc.tensor.matmul(K.ps[:, 6, t * E3:(t + 1) * E3], K.xnT[:, t * P:(t + 1) * P],
                                          K.w3_gate[:, :], start=True, stop=True)
                mm.then_inc(gated, 1)
                nc.tensor.matmul(K.ps[0:96, 4, :], K.w3_kvq[:, :], K.xnT[:, :], start=True, stop=True)
                nc.tensor.matmul(K.ps[0:96, 5, :], K.w3_aet[:, :], K.xnT[:, :],
                                 start=True, stop=True).then_inc(projected, 1)

                def down(e):
                    pe.wait_ge(hid_ready, 2 * e + 2)
                    if e:
                        pe.wait_ge(used, e)
                    for t in range(NT):
                        for c in range(2):
                            mm = nc.tensor.matmul(K.ps[:, 7, t * P:(t + 1) * P], h[:, e % 2, c, t * P:(t + 1) * P],
                                                  K.w3_down[:, e, c, :], start=(c == 0), stop=(c == 1))
                    mm.then_inc(out_done, 1)

                for e in range(E3):
                    for c in range(2):
                        n = 2 * e + c
                        if n >= 2:
                            pe.wait_ge(hid_ready, n - 1)
                        for m in range(2):
                            mm = nc.tensor.matmul(K.ps[:, 2 * (n % 2) + m, :],
                                                  K.w3_up[:, e, (2 * m + c) * P:(2 * m + c + 1) * P], K.xnT[:, :],
                                                  start=True, stop=True)
                        mm.then_inc(h12, 1)
                    if e:
                        down(e - 1)
                    if e == 1:
                        pe.wait_ge(top_read, 1)
                        for t in range(NT):
                            mm = nc.tensor.matmul(K.ps[:, 6, t * P:(t + 1) * P], K.xnT[:, t * P:(t + 1) * P],
                                                  K.w3_g[:, :], start=True, stop=True)
                        mm.then_inc(gate_projected, 1)
                down(E3 - 1)

            @block.scalar
            def _(act):
                act.wait_ge(e_in, 1)
                nc.scalar.activation(ex[:, :], ex[:, :], ACT.Exp).then_inc(e_done, 1)
                for n in range(2 * E3):
                    if n == 3:
                        act.wait_ge(projected, 1)
                        nc.scalar.activation(raw[:, 3:T + 3], K.ps[0:96, 4, :], ACT.Identity).then_inc(raw_ready, 1)
                    if n == 5:
                        nc.scalar.activation(aet[0:64, :], K.ps[0:64, 5, :], ACT.Sigmoid,
                                             bias=K.b3_aet[0:64, 0:1]).then_inc(sig_done, 1)
                    if n == 9:
                        act.wait_ge(abs_ready, 1)
                        nc.scalar.activation(za[th, :], za[th, :], ACT.Exp, scale=-1.0).then_inc(exp_done, 1)
                    if n == 12:
                        act.wait_ge(exp_done, 1)
                        nc.scalar.activation(za[th, :], za[th, :], ACT.Ln, bias=1.0).then_inc(ln_done, 1)
                    act.wait_ge(h12, n + 1)
                    if n >= 2:
                        act.wait_ge(hid_ready, n - 1)
                    nc.scalar.activation(a[:, n % 2, :], K.ps[:, 2 * (n % 2), :], ACT.Silu).then_inc(silu_done, 1)
                act.wait_ge(y_ready, 1)
                nc.scalar.activation(K.y[:, :, :], K.y[:, :, :], ACT.Silu).then_inc(y_done, 1)

            @block.vector
            def _(dve):
                ch = Chain(dve, vec)
                nc.vector.memset(raw[:, 0:3], 0.0)
                dve.wait_ge(gated, 1)
                nc.vector.tensor_copy(sc[:, :, :], K.ps[:, 6, 0:NT * E3].rearrange("p (t e) -> p t e", t=NT)
                                      ).then_inc(top_read, 1)
                dve.wait_ge(top_read, 1)
                for t in range(NT):
                    ch.tick(nc.vector.max(top[:, t, :], sc[:, t, :]))
                ch.wait()
                for t in range(NT):
                    ch.tick(nc.vector.max_index(idx[:, t, :], top[:, t, :], sc[:, t, :]))
                ch.tick(nc.vector.tensor_tensor(ex[:, :], top[:, :, 1], top[:, :, 0], ALU.subtract))
                ch.wait()
                nc.vector.tensor_copy(idf[:, :, :], idx[:, :, :]).then_inc(e_in, 1)
                dve.wait_ge(e_done, 1)
                ch.do(nc.vector.tensor_scalar(pr[:, 0, :], ex[:, :], 1.0, None, ALU.add))
                ch.do(nc.vector.reciprocal(pr[:, 0, :], pr[:, 0, :]))
                ch.do(nc.vector.tensor_tensor(pr[:, 1, :], ex[:, :], pr[:, 0, :], ALU.mult))
                for r in range(2):
                    for t in range(NT):
                        ch.tick(nc.vector.tensor_scalar(eq[:, r, t, :], K.iota8[:, :], idf[:, t, r:r + 1],
                                                        pr[:, r, t:t + 1], ALU.is_equal, ALU.mult))
                ch.wait()
                ch.do(nc.vector.tensor_tensor(pb[:, :, :], eq[:, 0, :, :], eq[:, 1, :, :], ALU.add))

                def add_out(e):
                    dve.wait_ge(out_done, e + 1)
                    for t in range(NT):
                        o = K.ps[:, 7, t * P:(t + 1) * P]
                        if e == 0:
                            i = nc.vector.tensor_scalar(K.y[:, t, :], o, pb[:, t, e:e + 1], None, ALU.mult)
                        else:
                            i = nc.vector.scalar_tensor_tensor(K.y[:, t, :], o, pb[:, t, e:e + 1], K.y[:, t, :],
                                                               ALU.mult, ALU.add)
                        if t < NT - 1:
                            ch.tick(i)
                    i.then_inc(used, 1)
                    dve.wait_ge(used, e + 1)
                    ch.wait()

                def memory_part(e):
                    if e == 1:
                        dve.wait_ge(projected, 1)
                        ch.do(nc.vector.tensor_scalar(zt[th, :], K.ps[64:96, 5, :], K.b3_aet[th, 0:1], None, ALU.add))
                        nc.vector.scalar_tensor_tensor(za[th, :], zt[th, :], -1.0, zt[th, :], ALU.mult,
                                                       ALU.max).then_inc(abs_ready, 1)
                    if e == 2:
                        dve.wait_ge(raw_ready, 1)
                        ch.do(nc.vector.tensor_scalar(conv[:, :], raw[:, 0:T], K.conv_w[:, 0:1], K.conv_b[:, 0:1],
                                                      ALU.mult, ALU.add))
                    if 2 < e < 6:
                        k = e - 2
                        i = nc.vector.scalar_tensor_tensor(conv[:, :], raw[:, k:k + T], K.conv_w[:, k:k + 1],
                                                           conv[:, :], ALU.mult, ALU.add)
                        if e < 5:
                            ch.do(i)
                        else:
                            i.then_inc(conv_ready, 1)
                    if e == 4:
                        dve.wait_ge(gate_projected, 1)
                        ch.do(nc.vector.tensor_tensor(fac[:, :, :], K.ps[:, 6, :].rearrange("p (t d) -> p t d", t=NT),
                                                      K.g3_b[:, :].unsqueeze(1).to_broadcast([P, NT, D]), ALU.add))
                        ch.do(nc.vector.tensor_tensor(fac[:, :, :], fac[:, :, :],
                                                      K.norm3[:, :].unsqueeze(1).to_broadcast([P, NT, D]), ALU.mult))
                    if e == 6:
                        dve.wait_ge(ln_done, 1)
                        nc.vector.scalar_tensor_tensor(aet[th, :], zt[th, :], 0.0, za[th, :], ALU.max,
                                                       ALU.add).then_inc(aet_ready, 1)

                for e in range(E3):
                    for c in range(2):
                        n = 2 * e + c
                        dve.wait_ge(silu_done, n + 1)
                        if c == 0 and e >= 2:
                            dve.wait_ge(out_done, e - 1)
                        nc.vector.tensor_tensor(h[:, e % 2, c, :], K.ps[:, 2 * (n % 2) + 1, :], a[:, n % 2, :],
                                                ALU.mult).then_inc(hid_ready, 1)
                    if e:
                        add_out(e - 1)
                    memory_part(e)
                add_out(E3 - 1)
                nc.vector.engine_nop().then_inc(y_ready, 1)
                dve.wait_ge(y_done, 1)
                nc.vector.tensor_tensor(fac[:, :, :], fac[:, :, :], K.y[:, :, :], ALU.mult).then_inc(f_ready, 1)

            @block.sync
            def _(sp):
                sp.dma_start(K.x_d[b, :, :].rearrange("(t p) d -> p t d", p=P), K.x[:, :, :]).then_inc(stored, 16)
                sp.wait_ge(stored, 16)
                sp.dma_start(K.x[:, :, :], next_x).then_inc(loaded, 16)
                sp.wait_ge(conv_ready, 1)
                sp.dma_start(K.kvq_d[b, :, :], conv[:, :]).then_inc(stored, 16)
                sp.wait_ge(sig_done, 1)
                sp.wait_ge(aet_ready, 1)
                sp.dma_start(K.aet_d[b, :, :], aet[:, :]).then_inc(stored, 16)
                sp.wait_ge(f_ready, 1)
                sp.dma_start(K.fac_d[b, :, :].rearrange("(t p) d -> p t d", p=P), fac[:, :, :]).then_inc(
                    K.factor_stored, 16)
                sp.wait_ge(stored, 48)
                sp.wait_ge(loaded, 16)
        K.clear()




def memory_coefficients(nc, K, M):
    meant, used, vec, spread_meant, spread_used, kvq_landed = K.pool[0:6]
    landed = K.pool[8:8 + BATCH]
    NTOK = BATCH * T
    with ExitStack() as tmp:
        aet = sbuf(nc, tmp, "aet_in", [96, BATCH, T])
        om = sbuf(nc, tmp, "om", [CH, NTOK])
        et = sbuf(nc, tmp, "et", [CH, NTOK])
        Es = sbuf(nc, tmp, "Es", [CH, NTOK])
        om_s, et_s, Ea, imp = [sbuf(nc, tmp, n, [P, 2 * T]) for n in ("om_s", "et_s", "E_all", "impulse")]
        om0, et0 = [sbuf(nc, tmp, n, [P, 2 * NCH, 1]) for n in ("om0", "et0")]
        by_chunk = lambda a: a[:, :].rearrange("p (n t) -> p n t", t=CH)
        with nc.Block() as block:
            @block.sync
            def _(sp):
                for b in range(BATCH):
                    sp.dma_start(aet[:, b, :], K.aet_d[b, :, :]).then_inc(landed[b], 16)

            @block.scalar
            def _(act):
                for m, dst in enumerate((M.k, M.v, M.q)):
                    src = K.kvq_d[:, 32 * m:32 * m + 32, :].rearrange("(g j) p t -> j p g t", j=4)
                    for j in range(4):
                        act.dma_start(dst[32 * j:32 * j + 32, :, :], src[j]).then_inc(kvq_landed, 16)
                act.wait_ge(kvq_landed, 16 * 12)

            @block.tensor
            def _(pe):
                for b in range(BATCH):
                    g, j = divmod(b, 4)
                    pe.wait_ge(landed[b], 16)
                    if b >= 2:
                        pe.wait_ge(used, 2 * (b - 1))
                    for m in range(2):
                        mm = nc.tensor.matmul(K.ps[0:CH, 2 * (b % 2) + m, :], M.mean_w[:, m, :], aet[:, b, :],
                                              start=True, stop=True)
                    mm.then_inc(meant, 1)
                    if g and j == 0:
                        pe.wait_ge(spread_used, 3)
                    for m in range(3):
                        mm = nc.tensor.matmul(K.ps[32 * j:32 * j + 32, 4 + m, :], M.mean_w[:, m, 0:32], aet[:, b, :],
                                              start=True, stop=True, tile_position=(0, 32 * j))
                    mm.then_inc(spread_meant, 1)

            @block.vector
            def _(dve):
                ch = Chain(dve, vec)
                for b in range(BATCH):
                    g, j = divmod(b, 4)
                    dve.wait_ge(meant, b + 1)
                    s = slice(b * T, (b + 1) * T)
                    nc.vector.tensor_scalar(om[:, s], K.ps[0:CH, 2 * (b % 2), :], -0.1, 1.0, ALU.mult,
                                            ALU.add).then_inc(used, 1)
                    nc.vector.tensor_scalar(et[:, s], K.ps[0:CH, 2 * (b % 2) + 1, :], 0.9, 0.05, ALU.mult,
                                            ALU.add).then_inc(used, 1)
                    if j == 3:
                        dve.wait_ge(spread_meant, b + 1)
                        s = slice(g * T, (g + 1) * T)
                        nc.vector.tensor_scalar(om_s[:, s], K.ps[:, 4, :], -0.1, 1.0, ALU.mult,
                                                ALU.add).then_inc(spread_used, 1)
                        nc.vector.tensor_scalar(et_s[:, s], K.ps[:, 5, :], 0.9, 0.05, ALU.mult,
                                                ALU.add).then_inc(spread_used, 1)
                        nc.vector.tensor_scalar(M.nth[:, g, :], K.ps[:, 6, :], -0.1, None,
                                                ALU.mult).then_inc(spread_used, 1)
                dve.wait_ge(used, 2 * BATCH)
                dve.wait_ge(spread_used, 6)
                ch.tick(nc.vector.tensor_copy(om0[:, :, :], by_chunk(om_s)[:, :, 0:1]))
                ch.tick(nc.vector.tensor_copy(et0[:, :, :], by_chunk(et_s)[:, :, 0:1]))
                ch.tick(nc.vector.memset(by_chunk(om)[:, :, 0:1], 0.0))
                ch.tick(nc.vector.memset(by_chunk(et)[:, :, 0:1], 0.0))
                ch.tick(nc.vector.tensor_copy(by_chunk(M.C), K.ident[0:CH, 0:CH].unsqueeze(1).to_broadcast(
                    [CH, BATCH * NCH, CH])))
                ch.tick(nc.vector.memset(imp[:, :], 0.0))
                ch.wait()
                ch.tick(nc.vector.memset(by_chunk(om_s)[:, :, 0:1], 0.0))
                ch.tick(nc.vector.memset(by_chunk(et_s)[:, :, 0:1], 0.0))
                ch.tick(nc.vector.tensor_copy(by_chunk(imp)[:, :, 0:1], et0[:, :, :]))
                ch.do(nc.vector.tensor_tensor_scan(Es[:, :], et[:, :], M.C[:, :], 0.0, ALU.mult, ALU.add))
                ch.tick(nc.vector.tensor_tensor_scan(M.C[:, :], om[:, :], Es[:, :], 0.0, ALU.mult, ALU.add))
                ch.tick(nc.vector.tensor_copy(M.E_end[:, :, :], by_chunk(Es)[:, :, CH - 1:CH]))
                ch.do(nc.vector.tensor_tensor_scan(Ea[:, :], et_s[:, :], imp[:, :], 0.0, ALU.mult, ALU.add))
                ch.tick(nc.vector.tensor_copy(M.Eall_end[:, :, :], by_chunk(Ea)[:, :, CH - 1:CH]))
                ch.tick(nc.vector.tensor_copy(by_chunk(imp)[:, :, 0:1], om0[:, :, :]))
                ch.do(nc.vector.tensor_tensor_scan(M.B[:, :], om_s[:, :], Ea[:, :], 0.0, ALU.mult, ALU.add))
                ch.do(nc.vector.tensor_tensor_scan(M.A[:, :], om_s[:, :], imp[:, :], 0.0, ALU.mult, ALU.add))
        K.clear()


def memory_chunk(nc, K, M, c):
    (staged, z_done, sg_done, h_done, pred_done, dp_done, dh_done, dz_done, sums_done, sk_done, n2_done, gn_done,
     uw_done, turned, tok_done, vec, g1_done, m1_done, zr_done, hr_done, g2_done, m2_done, r_done, upd_done,
     qab_done, hab_done, ec_done, coef_staged) = K.pool[0:28]
    NB = 2 * CH
    half = lambda t, g: t[:, g * CH:(g + 1) * CH]
    now = lambda t: t[:, :, bass.ds(c * CH, CH)]
    v3 = lambda t: t.rearrange("p (g t) -> p g t", g=2)

    with nc.Block() as block:
        @block.scalar
        def _(act):
            for dst, src in ((M.kc, M.k), (M.qc, M.q), (M.vc, M.v)):
                nc.scalar.activation(v3(dst[:, :]), now(src), ACT.Identity).then_inc(staged, 1)
            act.wait_ge(z_done, 1)
            nc.scalar.activation(M.sg[:, :], K.ps[:, 0, 0:NB], ACT.Sigmoid).then_inc(sg_done, 1)
            act.wait_ge(sums_done, 1)
            nc.scalar.activation(M.sums[:, :], K.ps[:, 3, 2 * NB:4 * NB], ACT.Identity).then_inc(sk_done, 1)
            act.wait_ge(n2_done, 1)
            nc.scalar.activation(M.n2[:, :], M.n2[:, :], ACT.Sqrt).then_inc(gn_done, 1)
            act.wait_ge(zr_done, 1)
            nc.scalar.activation(M.sg[:, :], K.ps[:, 4, 0:NB], ACT.Sigmoid).then_inc(sg_done, 1)

        @block.tensor
        def _(pe):
            pe.wait_ge(staged, 1)
            for g in range(2):
                mm = nc.tensor.matmul(half(K.ps[:, 0, :], g), M.W1T_bd[:, g, :], half(M.kc, g), start=True, stop=True)
            mm.then_inc(z_done, 1)
            pe.wait_ge(qab_done, 1)
            for g in range(2):
                mm = nc.tensor.matmul(K.ps[0:CH, 7, g * 4 * CH:(g + 1) * 4 * CH], half(M.kc, g), M.q_bd[:, g, :],
                                      start=True, stop=True)
            mm.then_inc(g1_done, 1)
            pe.wait_ge(h_done, 1)
            for g in range(2):
                mm = nc.tensor.matmul(half(K.ps[:, 1, :], g), M.W2T_bd[:, g, :], half(M.h, g), start=True, stop=True)
            mm.then_inc(pred_done, 1)
            pe.wait_ge(dp_done, 1)
            for g in range(2):
                mm = nc.tensor.matmul(half(K.ps[:, 2, :], g), M.W2_bd[:, g, :], half(M.dp, g), start=True, stop=True)
            mm.then_inc(dh_done, 1)
            pe.wait_ge(dz_done, 1)
            for m, q in enumerate((M.qdz, M.qdp, M.qk, M.qh)):
                mm = nc.tensor.matmul(K.ps[:, 3, m * NB:(m + 1) * NB], M.ones_bd[:, :], q[:, :], start=True, stop=True)
            mm.then_inc(sums_done, 1)
            pe.wait_ge(uw_done, 1)
            for m, src in enumerate((M.u, M.w, M.h, M.kc)):
                for g in range(2):
                    o = (m % 2) * 256 + g * P
                    mm = nc.tensor.transpose(K.ps[0:CH, m // 2, o:o + P], half(src, g), K.ident[:, :])
            mm.then_inc(turned, 1)
            pe.wait_ge(m1_done, 1)
            pe.wait_ge(tok_done, 1)

            def retrieve(bank, W, S, m, done):
                for g in range(2):
                    o = half(K.ps[:, bank, :], g)
                    nc.tensor.matmul(o, W[:, g, :], half(M.qa, g), start=True, stop=False)
                    nc.tensor.matmul(o, S[:, g, :], half(M.qb, g), start=False, stop=False)
                    for j in range(4):
                        b = 4 * g + j
                        mm = nc.tensor.matmul(K.ps[32 * j:32 * j + 32, bank, g * CH:(g + 1) * CH], M.tok[:, m, b, :],
                                              M.m1[:, b * CH:(b + 1) * CH], start=False, stop=True,
                                              tile_position=(0, 32 * j))
                mm.then_inc(done, 1)

            retrieve(4, M.W1T_bd, M.S1T_bd, 0, zr_done)
            pe.wait_ge(ec_done, 1)
            for m, bank in ((0, 2), (1, 3)):
                for b in range(BATCH):
                    g, j = divmod(b, 4)
                    mm = nc.tensor.matmul(K.ps[32 * j:32 * j + 32, bank, g * 64:(g + 1) * 64], M.tok[:, 3 - m, b, :],
                                          M.ec[:, m, b, :], start=True, stop=True, tile_position=(0, 32 * j))
            mm.then_inc(upd_done, 1)
            pe.wait_ge(hr_done, 1)
            for g in range(2):
                mm = nc.tensor.matmul(K.ps[0:CH, 5, g * 4 * CH:(g + 1) * 4 * CH], half(M.h, g), M.q_bd[:, g, :],
                                      start=True, stop=True)
            mm.then_inc(g2_done, 1)
            pe.wait_ge(m2_done, 1)
            pe.wait_ge(hab_done, 1)
            retrieve(6, M.W2T_bd, M.S2T_bd, 1, r_done)

        @block.gpsimd
        def _(pool):
            nc.gpsimd.tensor_copy(v3(M.ac[:, :]), M.A[:, :].rearrange("p (g t) -> p g t", g=2)[:, :, bass.ds(c * CH, CH)]
                                  ).then_inc(coef_staged, 1)
            nc.gpsimd.tensor_copy(v3(M.bc[:, :]), M.B[:, :].rearrange("p (g t) -> p g t", g=2)[:, :, bass.ds(c * CH, CH)]
                                  ).then_inc(coef_staged, 1)
            nc.gpsimd.tensor_copy(v3(M.tc[:, :]), now(M.nth)).then_inc(coef_staged, 1)

        @block.vector
        def _(dve):
            ch = Chain(dve, vec)
            C_now = M.C[:, :].rearrange("p (b t) -> p b t", b=BATCH)[:, :, bass.ds(c * CH, CH)]
            bd4 = lambda t: t.unsqueeze(2).to_broadcast([P, 2, 4, t.shape[-1]])

            def diagonal(dst, src):
                n = src.shape[-1]
                return nc.vector.tensor_tensor(dst[:, :, :].rearrange("p g (j n) -> p g j n", j=4), bd4(src),
                                               M.blocks[:, :, :, 0:n], ALU.mult)

            ends = lambda t, parts: t[:, :, :].rearrange("p (b n) o -> p b (n o)", n=NCH)[:, :, bass.ds(c, 1)]
            ch.tick(nc.vector.tensor_copy(M.e_end[:, :, :], ends(M.E_end, CH)))
            ch.tick(nc.vector.tensor_copy(M.eall_end[:, :, :], ends(M.Eall_end, P)))
            dve.wait_ge(staged, 2)
            diagonal(M.q_bd, v3(M.qc[:, :])).then_inc(qab_done, 1)
            ch.tick(nc.vector.tensor_tensor(M.qk[:, :], M.kc[:, :], M.kc[:, :], ALU.mult))
            dve.wait_ge(coef_staged, 3)
            ch.tick(nc.vector.tensor_tensor(M.qa[:, :], M.qc[:, :], M.ac[:, :], ALU.mult))
            ch.tick(nc.vector.tensor_tensor(M.qb[:, :], M.qc[:, :], M.bc[:, :], ALU.mult))
            dve.wait_ge(sg_done, 1)
            nc.vector.tensor_tensor(M.h[:, :], K.ps[:, 0, 0:NB], M.sg[:, :], ALU.mult).then_inc(h_done, 1)
            dve.wait_ge(h_done, 1)
            ch.tick(nc.vector.tensor_tensor(M.t1[:, :], M.h[:, :], M.sg[:, :], ALU.mult))
            ch.tick(nc.vector.tensor_tensor(M.ds[:, :], M.h[:, :], M.sg[:, :], ALU.add))
            ch.tick(nc.vector.tensor_tensor(M.qh[:, :], M.h[:, :], M.h[:, :], ALU.mult))
            ch.wait()
            ch.tick(nc.vector.tensor_tensor(M.ds[:, :], M.ds[:, :], M.t1[:, :], ALU.subtract))
            dve.wait_ge(pred_done, 1)
            dve.wait_ge(staged, 3)
            ch.do(nc.vector.tensor_tensor(M.dp[:, :], K.ps[:, 1, 0:NB], M.vc[:, :], ALU.subtract))
            nc.vector.tensor_scalar(M.dp[:, :], M.dp[:, :], 0.2, None, ALU.mult).then_inc(dp_done, 1)
            dve.wait_ge(dp_done, 1)
            ch.tick(nc.vector.tensor_tensor(M.qdp[:, :], M.dp[:, :], M.dp[:, :], ALU.mult))
            dve.wait_ge(dh_done, 1)
            ch.do(nc.vector.tensor_tensor(M.dz[:, :], K.ps[:, 2, 0:NB], M.ds[:, :], ALU.mult))
            nc.vector.tensor_tensor(M.qdz[:, :], M.dz[:, :], M.dz[:, :], ALU.mult).then_inc(dz_done, 1)
            dve.wait_ge(g1_done, 1)
            m1 = M.m1[:, :].rearrange("p (b t) -> p b t", b=BATCH)
            nc.vector.tensor_tensor(m1, K.ps[0:CH, 7, :].rearrange("p (b t) -> p b t", b=BATCH), C_now,
                                    ALU.mult).then_inc(m1_done, 1)
            dve.wait_ge(sk_done, 1)
            ch.do(nc.vector.tensor_tensor(M.sums[:, :], K.ps[:, 3, 0:2 * NB], M.sums[:, :], ALU.mult))
            nc.vector.tensor_tensor(M.n2[:, :], M.sums[:, 0:NB], M.sums[:, NB:2 * NB], ALU.add).then_inc(n2_done, 1)
            dve.wait_ge(gn_done, 1)
            ch.do(nc.vector.tensor_scalar(M.n2[:, :], M.n2[:, :], 1e-6, None, ALU.max))
            ch.do(nc.vector.reciprocal(M.n2[:, :], M.n2[:, :]))
            ch.do(nc.vector.scalar_tensor_tensor(M.n2[:, :], M.n2[:, :], 1.0, M.tc[:, :], ALU.min, ALU.mult))
            ch.do(nc.vector.tensor_tensor(M.u[:, :], M.dz[:, :], M.n2[:, :], ALU.mult))
            nc.vector.tensor_tensor(M.w[:, :], M.dp[:, :], M.n2[:, :], ALU.mult).then_inc(uw_done, 1)
            dve.wait_ge(turned, 1)
            nc.vector.tensor_copy(M.tok[:, :, :, :], K.ps[0:CH, 0:2, :].rearrange(
                "p a (m b d) -> p (a m) b d", m=2, b=BATCH)).then_inc(tok_done, 1)
            dve.wait_ge(tok_done, 1)
            c_end = M.C[:, :].rearrange("p (b t) -> p b t", b=BATCH)[:, :, bass.ds(c * CH + CH - 1, 1)].to_broadcast(
                [CH, BATCH, 32])
            for m in range(2):
                ch.tick(nc.vector.tensor_tensor(M.ec[:, m, :, 0:32], M.tok[:, m, :, :],
                                                M.e_end[:, :, :].to_broadcast([CH, BATCH, 32]), ALU.mult))
                i = nc.vector.tensor_tensor(M.ec[:, m, :, 32:64], M.tok[:, m, :, :], c_end, ALU.mult)
                if m == 0:
                    ch.tick(i)
                else:
                    i.then_inc(ec_done, 1)
            ch.wait()
            dve.wait_ge(ec_done, 1)
            dve.wait_ge(sg_done, 2)
            ch.do(nc.vector.tensor_tensor(M.hr[:, :], K.ps[:, 4, 0:NB], M.sg[:, :], ALU.mult))
            diagonal(M.q_bd, v3(M.hr[:, :])).then_inc(hr_done, 1)
            ch.tick(nc.vector.tensor_tensor(M.qa[:, :], M.hr[:, :], M.ac[:, :], ALU.mult))
            nc.vector.tensor_tensor(M.qb[:, :], M.hr[:, :], M.bc[:, :], ALU.mult).then_inc(hab_done, 1)
            ch.wait()
            dve.wait_ge(g2_done, 1)
            nc.vector.tensor_tensor(m1, K.ps[0:CH, 5, :].rearrange("p (b t) -> p b t", b=BATCH), C_now,
                                    ALU.mult).then_inc(m2_done, 1)
            dve.wait_ge(upd_done, 1)
            a_end = v3(M.ac[:, :])[:, :, CH - 1:CH].to_broadcast([P, 2, 32])
            b_end = v3(M.bc[:, :])[:, :, CH - 1:CH].to_broadcast([P, 2, 32])
            e_end = M.eall_end[:, :, :].to_broadcast([P, 2, 32])
            for W, S, bank in ((M.W1T, M.S1T, 2), (M.W2T, M.S2T, 3)):
                new = K.ps[:, bank, 0:P].rearrange("p (g x) -> p g x", g=2)
                ch.tick(nc.vector.tensor_tensor(W[:, :, :], W[:, :, :], a_end, ALU.mult))
                ch.do(nc.vector.tensor_tensor(M.t2[:, :, :], S[:, :, :], b_end, ALU.mult))
                ch.tick(nc.vector.tensor_tensor(W[:, :, :], W[:, :, :], M.t2[:, :, :], ALU.add))
                ch.do(nc.vector.tensor_tensor(S[:, :, :], S[:, :, :], e_end, ALU.mult))
                ch.tick(nc.vector.tensor_tensor(W[:, :, :], W[:, :, :], new[:, :, 32:64], ALU.add))
                ch.do(nc.vector.tensor_tensor(S[:, :, :], S[:, :, :], new[:, :, 0:32], ALU.add))
            ch.do(nc.vector.transpose(M.W2[:, :, :].rearrange("p b d -> p (b d)"),
                                      M.W2T[:, :, :].rearrange("p b d -> p (b d)")))
            dve.wait_ge(r_done, 1)
            for dst, src in ((M.W1T_bd, M.W1T), (M.W2T_bd, M.W2T), (M.W2_bd, M.W2), (M.S1T_bd, M.S1T),
                             (M.S2T_bd, M.S2T)):
                diagonal(dst, src[:, :, :])
            nc.vector.tensor_copy(now(M.ret), v3(K.ps[:, 6, 0:NB]))
    K.clear()


def memory_output(nc, K, M, g, out):
    staged, projected, vec, ms_ready, rs_ready, done, stored = K.pool[0:7]
    landed = K.pool[8:12]
    of = lambda a, j: a.rearrange("(g j) (t p) d -> j g p t d", j=4, p=P)[j, g]
    with ExitStack() as tmp:
        x, fac = [sbuf(nc, tmp, n, [P, 4, NT, D]) for n in ("x_back", "fac_back")]
        rc = sbuf(nc, tmp, "rc", [P, T])
        var, rstd = [sbuf(nc, tmp, n, [P, 4, NT]) for n in ("out_var", "out_rstd")]
        with nc.Block() as block:
            @block.sync
            def _(sp):
                for j in range(4):
                    sp.dma_start(fac[:, j, :, :], of(K.fac_d, j)).then_inc(landed[j], 16)
                    sp.dma_start(x[:, j, :, :], of(K.x_d, j)).then_inc(landed[j], 16)
                for j in range(4):
                    sp.wait_ge(done, j + 1)
                    sp.dma_start(of(out, j), x[:, j, :, :]).then_inc(stored, 16)
                sp.wait_ge(stored, 64)

            @block.scalar
            def _(act):
                nc.scalar.activation(rc[:, :], M.ret[:, bass.ds(g, 1), :].rearrange("p b t -> p (b t)"),
                                     ACT.Identity).then_inc(staged, 1)

            @block.tensor
            def _(pe):
                pe.wait_ge(staged, 1)
                for j in range(4):
                    q = slice(32 * j, 32 * j + 32)
                    for t in range(NT):
                        mm = nc.tensor.matmul(K.ps[:, j, t * P:(t + 1) * P], rc[q, t * P:(t + 1) * P], M.wo[q, :],
                                              start=True, stop=True, tile_position=(32 * j, 0))
                    mm.then_inc(projected, 1)

            @block.vector
            def _(dve):
                ch = Chain(dve, vec)
                for j in range(4):
                    dve.wait_ge(projected, j + 1)
                    for t in range(NT):
                        ch.tick(nc.vector.bn_stats(K.stats[:, t, :], K.ps[:, j, t * P:(t + 1) * P]))
                    ch.wait()
                    for t in range(NT):
                        ch.tick(nc.vector.bn_aggr(K.mv[:, t, :], K.stats[:, t, :]))
                    ch.wait()
                    ch.do(nc.vector.tensor_tensor(var[:, j, :], K.mv[:, :, 0], K.mv[:, :, 0], ALU.mult))
                    nc.vector.scalar_tensor_tensor(var[:, j, :], K.mv[:, :, 1], 1e-6, var[:, j, :],
                                                   ALU.add, ALU.add).then_inc(ms_ready, 1)
                    dve.wait_ge(ms_ready, j + 1)
                for j in range(4):
                    dve.wait_ge(rs_ready, j + 1)
                    dve.wait_ge(landed[j], 32)
                    for t in range(NT):
                        ch.tick(nc.vector.scalar_tensor_tensor(fac[:, j, t, :], K.ps[:, j, t * P:(t + 1) * P],
                                                               rstd[:, j, t:t + 1], fac[:, j, t, :], ALU.mult,
                                                               ALU.mult))
                    ch.wait()
                    nc.vector.tensor_tensor(x[:, j, :, :], x[:, j, :, :], fac[:, j, :, :], ALU.add).then_inc(done, 1)

            @block.gpsimd
            def _(pool):
                for j in range(4):
                    pool.wait_ge(ms_ready, j + 1)
                    nc.gpsimd.tensor_tensor(rstd[:, j, :], var[:, j, :], K.neghalf[:, 0:NT],
                                            ALU.pow).then_inc(rs_ready, 1)
        K.clear()




def rope_tables():
    theta = (np.float32(10000.0) ** (-2.0 * np.arange(HD // 2, dtype=np.float32) / HD)).astype(np.float32)
    ang = np.outer(np.arange(T, dtype=np.float32), theta).astype(np.float32).astype(np.float64)
    cos = np.repeat(np.cos(ang), 2, axis=1).astype(np.float32)
    sin = np.stack([-np.sin(ang), np.sin(ang)], axis=1).astype(np.float32)
    return (np.ascontiguousarray(cos.reshape(NT, P, HD).transpose(1, 0, 2)),
            np.ascontiguousarray(sin.reshape(NT, P, 2, HD // 2).transpose(1, 0, 2, 3)))


def xpos_tables():
    half = np.arange(0, LD, 2, dtype=np.float32)
    inv = (np.float32(1.0) / np.float32(10000.0) ** (half / np.float32(LD))).astype(np.float32)
    t = np.arange(T, dtype=np.float32)
    fr = (t[:, None] * inv[None, :]).astype(np.float32)
    fr = np.concatenate([fr, fr], axis=1).astype(np.float64)
    base = ((half + np.float32(0.4 * LD)) / np.float32(1.4 * LD)).astype(np.float32)
    power = ((t - T // 2) / np.float32(WIN // 2)).astype(np.float32)
    sc = base[None, :].astype(np.float64) ** power[:, None]
    sc = np.concatenate([sc, sc], axis=1)
    sign = np.where(np.arange(LD) < LD // 2, -1.0, 1.0)
    tabs = np.stack([np.cos(fr) * sc, np.sin(fr) * sc * sign, np.cos(fr) / sc, np.sin(fr) / sc * sign])
    return np.ascontiguousarray(tabs.reshape(4, NT, P, LD).transpose(2, 0, 1, 3).astype(np.float32))


def masks():
    r, c = np.arange(P)[:, None], np.arange(P)[None, :]
    mq = np.where(c > r, NEG, 0.0).astype(np.float32)
    c = np.arange(P + WIN)[None, :]
    band = np.where((c < r) | (c > r + WIN), NEG, 0.0).astype(np.float32)
    band0 = np.where(c < WIN, NEG, band).astype(np.float32)
    return np.concatenate([np.eye(P, dtype=np.float32), mq, mq.T, band, band0], axis=1)


def build_kernel(nc, A, out):
    NAMED.clear()
    with ExitStack() as ctx:
        K = Kit(nc, ctx)
        K.ps = ctx.enter_context(nc.psum_tensor("banks", [P, 8, 512], F32))
        K.x_d = nc.dram_tensor("x_scratch", [BATCH, T, D], F32, kind="Internal").ap()
        K.fac_d = nc.dram_tensor("factor_scratch", [BATCH, T, D], F32, kind="Internal").ap()
        K.parts_d = nc.dram_tensor("parts_scratch", [2, 3, H * HD, T], BF16, kind="Internal").ap()
        K.nmax_d = nc.dram_tensor("maxima_scratch", [2, H, T], BF16, kind="Internal").ap()
        K.ones_d = nc.dram_tensor("ones_scratch", [2, H, T], BF16, kind="Internal").ap()
        K.kvq_d = nc.dram_tensor("kvq_scratch", [BATCH, 96, T], F32, kind="Internal").ap()
        K.aet_d = nc.dram_tensor("aet_scratch", [BATCH, 96, T], F32, kind="Internal").ap()

        def sb(name, shape, dt=F32, c=ctx):
            return sbuf(nc, c, name, shape, dt)

        K.ident = sb("ident", [P, P])
        K.neghalf = sb("neghalf", [P, 2 * NT * LH])
        K.stats = sb("stats", [P, NT, 6])
        K.mv = sb("mv", [P, NT, 2])
        K.var = sb("var", [P, NT])
        K.rstd = sb("rstd", [P, NT])
        with ExitStack() as loop:
            batch_loop(nc, K, loop, A, out)
        with ExitStack() as mem:
            memory(nc, K, mem, A, out)


def batch_loop(nc, K, ctx, A, out):
    def sb(name, shape, dt=F32):
        return sbuf(nc, ctx, name, shape, dt)

    loads = []

    def whole(name, src=None, bc=False):
        src = A[name] if src is None else src
        shape = ([P] + list(src.shape)) if bc else list(src.shape)
        t = sb(name + "_s", shape)
        ap = src.partition_broadcast(P) if bc else src
        full = tuple(slice(None) for _ in shape)
        loads.append((t[full], ap[full] if not bc else ap))
        return t

    K.w0_qkv = whole("w0_qkv")
    K.b0_qkv = whole("b0_qkv", bc=True)
    K.w0_1, K.w0_2, K.w0_h1, K.w0_h2, K.w0_3 = [whole(n) for n in ("w0_1", "w0_2", "w0_h1", "w0_h2", "w0_3")]
    K.s0_1, K.s0_2, K.s0_h1, K.s0_h2 = [whole(n) for n in ("s0_1", "s0_2", "s0_h1", "s0_h2")]
    K.s0_3 = whole("s0_3", bc=True)
    K.w1_q, K.w1_k, K.w1_v, K.w1_o = [whole(n) for n in ("w1_q", "w1_k", "w1_v", "w1_o")]
    K.w_gu = sb("w_gu", [P, 2 * I1])
    K.w_down = sb("w_down", [P, 3, D])
    K.w2_q, K.w2_k, K.w2_v, K.w2_ao = [whole(n) for n in ("w2_q", "w2_k", "w2_v", "w2_ao")]
    K.b2_q, K.b2_k = whole("b2_q"), whole("b2_k")
    K.b2_v, K.b2_ao, K.rmsw = [whole(n, bc=True) for n in ("b2_v", "b2_ao", "rmsw")]
    K.w2_qkv, K.w2_o, K.w2_up, K.w2_down, K.b2_up, K.b2_down, K.ln2_g, K.ln2_b = [], [], [], [], [], [], [], []
    for L in range(2):
        K.w2_qkv.append(whole(f"w2_qkv{L}"))
        K.w2_o.append(whole(f"w2_o{L}"))
        K.w2_up.append(whole(f"w2_up{L}"))
        K.b2_up.append(whole(f"b2_up{L}"))
        K.b2_down.append(whole(f"b2_down{L}", bc=True))
        K.ln2_g.append(whole(f"ln2_g{L}"))
        K.ln2_b.append(whole(f"ln2_b{L}"))
        w = sb(f"w2_down{L}_s", [P, 3, D])
        n = HID2 - 2 * P
        loads.append((w[:, 0:2, :], A[f"w2_down{L}"][0:2 * P, :].rearrange("(c p) d -> p c d", p=P)))
        loads.append((w[0:n, 2, :], A[f"w2_down{L}"][2 * P:HID2, :]))
        K.w2_down.append(w)
    K.w3_up, K.w3_down, K.w3_gate, K.w3_kvq, K.w3_aet, K.w3_g = [
        whole(n) for n in ("w3_up", "w3_down", "w3_gate", "w3_kvq", "w3_aet", "w3_g")]
    K.g3_b, K.norm3 = whole("g3_b", bc=True), whole("norm3", bc=True)
    K.conv_w, K.conv_b, K.b3_aet = whole("conv_w"), whole("conv_b"), whole("b3_aet")

    cos, sin = rope_tables()
    K.rope_cos = whole("rope_cos", nc.inline_tensor(cos, name="rope_cos_c").ap())
    K.rope_sin = whole("rope_sin", nc.inline_tensor(sin, name="rope_sin_c").ap())
    K.iota8 = whole("iota8", nc.inline_tensor(np.arange(E3, dtype=np.float32), name="iota8_c").ap(), bc=True)
    K.cosq, K.sinq, K.cosk, K.sink = [[sb(f"{n}{L}", [P, NT, LD]) for L in range(2)]
                                      for n in ("cosq", "sinq", "cosk", "sink")]
    K.x, K.xn, K.att, K.g = [sb(n, [P, NT, D]) for n in ("x", "xn", "att", "g")]
    K.v32 = sb("v32", [P, NT, H, 32])
    K.xnT = sb("xnT", [P, T])
    K.identb = sb("identb", [P, P], BF16)
    K.mask_q = sb("mask_q", [P, P], BF16)
    K.mask_k = sb("mask_k", [P, P], BF16)
    K.mask_band = sb("mask_band", [P, P + WIN], BF16)
    K.mask_band0 = sb("mask_band0", [P, P + WIN], BF16)
    fills = [(K.neghalf[:, :], -0.5), (K.v32[:, :, :, :], 0.0),
             (K.v32[:, :, :, HD:HD + 1], 1.0)]
    with ExitStack() as tmp:
        consts = masks()
        ct = sbuf(nc, tmp, "consts", [P, consts.shape[1]])
        tabs = sbuf(nc, tmp, "tabs", [P, 4, NT, LD])
        qks = sbuf(nc, tmp, "qks", [P, 2, 4, LD])
        ones = sbuf(nc, tmp, "ones_rows", [2, H, T], BF16)
        K.gate_rows, K.up_rows = [sbuf(nc, tmp, n, [P, 3, D]) for n in ("gate_rows", "up_rows")]
        K.down_rows = sbuf(nc, tmp, "down_rows", [P, I1])
        loads.append((ct[:, :], nc.inline_tensor(consts, name="masks_c").ap()))
        loads.append((K.ident[:, :], nc.inline_tensor(np.eye(P, dtype=np.float32), name="ident_c").ap()))
        loads.append((tabs[:, :, :, :], nc.inline_tensor(xpos_tables(), name="xpos_c").ap()))
        loads.append((qks[:, :, :, :], A["qk_scales"].partition_broadcast(P)))
        for t, n in ((K.gate_rows, "w_gate"), (K.up_rows, "w_up")):
            loads.append((t[:, 0:2, :], A[n][0:2 * P, :].rearrange("(c p) d -> p c d", p=P)))
            loads.append((t[0:I1 - 2 * P, 2, :], A[n][2 * P:I1, :]))
        loads.append((K.down_rows[:, :], A["w_downr"]))
        load_constants(nc, K, loads)
        filled, vec = K.pool[0:2]
        with nc.Block() as block:
            @block.sync
            def _(sp):
                sp.wait_ge(filled, 1)
                sp.dma_start(K.ones_d, ones[:, :, :]).then_inc(K.factor_stored, 16)
                sp.wait_ge(K.factor_stored, 16)

            @block.vector
            def _(dve):
                ch = Chain(dve, vec)
                nc.vector.memset(ones[:, :, :], 1.0).then_inc(filled, 1)
                for dst, value in fills:
                    ch.do(nc.vector.memset(dst, value))
                o = 0
                for t in (K.identb, K.mask_q, K.mask_k, K.mask_band, K.mask_band0):
                    n = t.shape[1]
                    nc.vector.tensor_copy(t[:, :], ct[:, o:o + n])
                    o += n
                for L in range(2):
                    for m, t in enumerate((K.cosq[L], K.sinq[L], K.cosk[L], K.sink[L])):
                        nc.vector.tensor_tensor(t[:, :, :], tabs[:, m, :, :],
                                                qks[:, L, m, :].unsqueeze(1).to_broadcast([P, NT, LD]), ALU.mult)
        K.clear()
        quantize_weights(nc, K, tmp)

    def x_tiles(b):
        return A["x"][b, :, :].rearrange("(t p) d -> p t d", p=P)

    load_constants(nc, K, [(K.x[:, :, :], x_tiles(0))])
    with nc.Fori(0, BATCH) as b:
        def rows():
            c = ExitStack()
            K.qs = sbuf(nc, c, "qs", [P, H, T], BF16)
            K.ks = sbuf(nc, c, "ks", [P, H, T], BF16)
            return c

        with rows():
            with ExitStack() as prep:
                K.parts = sbuf(nc, prep, "parts", [P, 2, 3, T], BF16)
                ffn = TernaryFfn(nc, K, prep).start(nc)
                prepare(nc, K, 0, beside=ffn)
                attention(nc, K, False, beside=ffn, after_store=True)
        with rows():
            with ExitStack() as prep:
                K.parts = sbuf(nc, prep, "parts", [P, 2, 3, T], BF16)
                ffn = Fp4Ffn(nc, K, prep).start(nc)
                prepare(nc, K, 1, beside=ffn)
                attention(nc, K, True, K.w1_o, beside=ffn)
        with ExitStack() as two:
            K.xr, K.y = [sbuf(nc, two, n, [P, NT, D]) for n in ("xr", "y")]
            K.shT = sbuf(nc, two, "shT", [P, T])
            with ExitStack() as prep:
                K.xrT = sbuf(nc, prep, "xrT", [P, T])
                K.parts = sbuf(nc, prep, "parts", [P, 2, 3, T], BF16)
                local_buffers(nc, K, prep)
                with ExitStack() as scratch:
                    prepare(nc, K, 2, then=local_qkv(nc, K, scratch, 0))
                    K.clear()
                local_attention(nc, K, 0)
            with rows() as both:
                attention(nc, K, True, K.w2_ao, K.b2_ao, combine=False, beside=Glu(nc, K, both, 0, False))
            local_sublayer(nc, K, 1)
            with ExitStack() as tmp:
                run_alone(nc, K, Glu(nc, K, tmp, 1, True))
            gated_layer_norm(nc, K)
        with ExitStack() as three:
            K.y = sbuf(nc, three, "y3", [P, NT, D])
            experts(nc, K, b, x_tiles(b + 1))


class Memory:
    pass


def memory(nc, K, ctx, A, out):
    M = Memory()

    def sb(name, shape, dt=F32):
        return sbuf(nc, ctx, name, shape, dt)

    M.wo = sb("wo3", [P, P])
    M.mw = sb("mw", [P, 3, 32])
    M.mean_w = sb("mean_w", [96, 3, CH])
    M.ones_bd = sb("ones_bd", [P, P])
    M.blocks = sb("blocks", [P, 2, 4, CH])
    M.W1T, M.W2T, M.W2, M.S1T, M.S2T = [sb(n, [P, 2, 32]) for n in ("W1T", "W2T", "W2", "S1T", "S2T")]
    M.W1T_bd, M.W2T_bd, M.W2_bd, M.S1T_bd, M.S2T_bd = [
        sb(n + "_bd", [P, 2, P]) for n in ("W1T", "W2T", "W2", "S1T", "S2T")]
    M.k, M.v, M.q, M.ret, M.nth = [sb(n, [P, 2, T]) for n in ("k_all", "v_all", "q_all", "ret", "nth")]
    M.C = sb("C", [CH, BATCH * T])
    M.A, M.B = [sb(n, [P, 2 * T]) for n in ("A_all", "B_all")]
    M.E_end = sb("E_end", [CH, BATCH * NCH, 1])
    M.Eall_end = sb("Eall_end", [P, 2 * NCH, 1])
    mean = np.full((96, 3, CH), 0.0, np.float32)
    for m in range(3):
        mean[32 * m:32 * m + 32, m, :] = 1.0 / 32
    ones = np.kron(np.eye(4, dtype=np.float32), np.ones((32, 32), np.float32))
    blocks = np.kron(np.eye(4, dtype=np.float32), np.ones((32, CH), np.float32)).reshape(P, 1, 4, CH)
    blocks = np.ascontiguousarray(np.concatenate([blocks, blocks], axis=1))
    loads = [(M.mean_w[:, :, :], nc.inline_tensor(mean, name="mean_c").ap()),
             (M.ones_bd[:, :], nc.inline_tensor(ones, name="ones_bd_c").ap()),
             (M.blocks[:, :, :, :], nc.inline_tensor(blocks, name="blocks_c").ap())]
    for j in range(4):
        q = slice(32 * j, 32 * j + 32)
        loads += [(M.wo[q, :], A["w3_o"]), (M.mw[q, :, :], A["mem_w"])]
    load_constants(nc, K, loads)
    copied, = K.pool[0:1]
    with nc.Block() as block:
        @block.sync
        def _(sp):
            sp.wait_ge(K.factor_stored, 16)

        @block.vector
        def _(dve):
            ch = Chain(dve, copied)
            for m, t in enumerate((M.W1T, M.W2T, M.W2)):
                ch.tick(nc.vector.tensor_copy(t[:, :, :], M.mw[:, m, :].unsqueeze(1).to_broadcast([P, 2, 32])))
            for t in (M.S1T, M.S2T):
                nc.vector.memset(t[:, :, :], 0.0)
            for t in (M.S1T_bd, M.S2T_bd):
                nc.vector.memset(t[:, :, :], 0.0)
            ch.wait()
            for dst, src in ((M.W1T_bd, M.W1T), (M.W2T_bd, M.W2T), (M.W2_bd, M.W2)):
                nc.vector.tensor_tensor(dst[:, :, :].rearrange("p g (j n) -> p g j n", j=4),
                                        src[:, :, :].unsqueeze(2).to_broadcast([P, 2, 4, 32]),
                                        M.blocks[:, :, :, 0:32], ALU.mult)
    K.clear()
    memory_coefficients(nc, K, M)
    with ExitStack() as tmp:
        names = ("kc", "vc", "qc", "sg", "h", "dp", "ds", "dz", "t1", "qk", "qh", "qdp", "qdz", "n2", "u", "w", "hr",
                 "qa", "qb", "ac", "bc", "tc")
        (M.kc, M.vc, M.qc, M.sg, M.h, M.dp, M.ds, M.dz, M.t1, M.qk, M.qh, M.qdp, M.qdz, M.n2, M.u, M.w, M.hr,
         M.qa, M.qb, M.ac, M.bc, M.tc) = [sbuf(nc, tmp, n, [P, 2 * CH]) for n in names]
        M.sums = sbuf(nc, tmp, "sums", [P, 4 * CH])
        M.q_bd = sbuf(nc, tmp, "q_bd", [P, 2, 4 * CH])
        M.m1 = sbuf(nc, tmp, "m1", [CH, BATCH * CH])
        M.tok = sbuf(nc, tmp, "tok", [CH, 4, BATCH, 32])
        M.ec = sbuf(nc, tmp, "ec", [CH, 2, BATCH, 64])
        M.t2 = sbuf(nc, tmp, "t2", [P, 2, 32])
        M.e_end = sbuf(nc, tmp, "e_end", [CH, BATCH, 1])
        M.eall_end = sbuf(nc, tmp, "eall_end", [P, 2, 1])
        with nc.Fori(0, NCH) as c:
            memory_chunk(nc, K, M, c)
    with nc.Fori(0, 2) as g:
        memory_output(nc, K, M, g, out)




def lay_out(i):
    c = np.ascontiguousarray
    t = {}
    j = lambda *n: np.concatenate([np.asarray(i[k]) for k in n], axis=0)
    col = lambda v: c(np.asarray(v).reshape(-1, P).T)
    tiles = lambda w: c(np.asarray(w).reshape(-1, P, w.shape[-1]).transpose(1, 0, 2))
    T_ = lambda n: c(np.asarray(i[n]).T)
    x = np.asarray(i["L0_attn_x"])
    t["x"] = np.concatenate([x, x[:1]])
    t["w0_qkv"] = c(j("L0_attn_wq_w", "L0_attn_wk_w", "L0_attn_wv_w").T)
    t["b0_qkv"] = j("L0_attn_wq_b", "L0_attn_wk_b", "L0_attn_wv_b")
    t["w0_1"], t["w0_2"] = T_("L0_ffn_w1_w"), T_("L0_ffn_w2_w")
    t["w0_h1"], t["w0_h2"], t["w0_3"] = tiles(T_("L0_ffn_h1_w")), tiles(T_("L0_ffn_h2_w")), tiles(T_("L0_ffn_w3_w"))
    t["s0_1"], t["s0_2"] = col(i["L0_ffn_w1_s"]), col(i["L0_ffn_w2_s"])
    t["s0_h1"], t["s0_h2"] = col(i["L0_ffn_h1_s"]), col(i["L0_ffn_h2_s"])
    t["s0_3"] = c(i["L0_ffn_w3_s"])
    t["w1_q"], t["w1_k"], t["w1_v"], t["w1_o"] = [T_("L1_attn_W" + n) for n in "qkvo"]
    t["w_gate"], t["w_up"], t["w_downr"] = c(i["L1_ffn_w_gate"]), c(i["L1_ffn_w_up"]), c(i["L1_ffn_w_down"])
    t["w2_q"], t["w2_k"], t["w2_v"], t["w2_ao"] = [T_("L2_attn_W" + n) for n in "qkvo"]
    t["b2_q"], t["b2_k"] = col(i["L2_attn_bq"]), col(i["L2_attn_bk"])
    t["b2_v"], t["b2_ao"], t["rmsw"] = c(i["L2_attn_bv"]), c(i["L2_attn_bo"]), c(i["L2_attn_norm_w"])
    half = LD // 2
    sc = []
    for L in range(2):
        t[f"w2_qkv{L}"] = c(i["L2_ffn_wqkv"][L])
        t[f"w2_o{L}"] = tiles(c(i["L2_ffn_wo"][L]))
        t[f"w2_up{L}"] = c(i["L2_ffn_w1"][L])
        t[f"w2_down{L}"] = c(i["L2_ffn_w2"][L])
        b1 = np.asarray(i["L2_ffn_b1"][L])
        up = np.zeros((6, P), b1.dtype)
        for m in range(2):
            up[3 * m:3 * m + 3].reshape(-1)[:HID2] = b1[m * HID2:(m + 1) * HID2]
        t[f"b2_up{L}"] = c(up.T)
        t[f"b2_down{L}"] = c(i["L2_ffn_b2"][L])
        t[f"ln2_g{L}"], t[f"ln2_b{L}"] = col(i["L2_ffn_ln_g"][L]), col(i["L2_ffn_ln_b"][L])
        q, k = np.asarray(i["L2_ffn_q_scale"][L]), np.asarray(i["L2_ffn_k_scale"][L])
        sc.append(np.stack([q, np.concatenate([q[half:], q[:half]]), k, np.concatenate([k[half:], k[:half]])]))
    t["qk_scales"] = c(np.stack(sc))
    t["w3_up"] = c(np.asarray(i["L3_ffn_w12"]).transpose(2, 0, 1))
    t["w3_down"] = c(np.asarray(i["L3_ffn_w3"]).transpose(2, 0, 1).reshape(2, P, E3, D).transpose(1, 2, 0, 3))
    t["w3_gate"] = T_("L3_ffn_gate_w")
    t["w3_kvq"] = c(j("L3_attn_Wk", "L3_attn_Wv", "L3_attn_Wq").T)
    t["w3_aet"] = c(j("L3_attn_aW", "L3_attn_eW", "L3_attn_tW").T)
    t["w3_g"] = T_("L3_attn_gW")
    t["g3_b"], t["norm3"] = c(i["L3_attn_gb"]), c(i["L3_attn_norm_g"])
    t["conv_w"] = j("L3_attn_ckw", "L3_attn_cvw", "L3_attn_cqw")
    t["conv_b"] = j("L3_attn_ckb", "L3_attn_cvb", "L3_attn_cqb").reshape(96, 1)
    t["b3_aet"] = j("L3_attn_ab", "L3_attn_eb", "L3_attn_tb").reshape(96, 1)
    t["w3_o"] = T_("L3_attn_Wo")
    w1, w2 = np.asarray(i["L3_attn_mW1"]), np.asarray(i["L3_attn_mW2"])
    t["mem_w"] = c(np.stack([w1.T, w2.T, w2], axis=1))
    return t


def kernel(**inputs):
    import concourse.bacc as _bacc
    from concourse.bass_utils import run_bass_kernel_spmd as _run

    nc = _bacc.Bacc("TRN2", target_bir_lowering=False, num_devices=1)
    arrays = {f"in_{n}": np.ascontiguousarray(a) for n, a in lay_out(inputs).items()}
    A = {n[3:]: nc.dram_tensor(n, a.shape, mybir.dt.from_np(a.dtype), kind="ExternalInput").ap()
         for n, a in arrays.items()}
    out = nc.dram_tensor("out_0", (BATCH, T, D), F32, kind="ExternalOutput").ap()
    build_kernel(nc, A, out)
    r = _run(nc, [arrays], core_ids=[0])
    return r.results[0]["out_0"]
```
